# Optimizing a Trainium2 kernel written in Bass

```python
import numpy as np
import jax
import jax.numpy as jnp

def _softmax(x, axis=-1):
    return jax.nn.softmax(x, axis=axis)

def _gelu(x):
    return jax.nn.gelu(x, approximate=True)

def _silu(x):
    return jax.nn.silu(x)

def _sigmoid(x):
    return jax.nn.sigmoid(x)

def _layernorm(x, axis=-1, eps=1e-05):
    m = jnp.mean(x, axis=axis, keepdims=True)
    v = jnp.var(x, axis=axis, keepdims=True)
    return (x - m) / jnp.sqrt(v + eps)

def _scatter_add(tgt, idx, src, axis=0):
    return tgt.at[idx].add(src)

def _segment_sum(src, seg, n):
    return jax.ops.segment_sum(src, seg, n)
kernel_name = 'mk_xattn_seq_d4_seqx_r8_b35a84'

def setup_inputs(seed: int=0):
    np.random.seed(seed)
    _w = jnp.asarray

    def _rec_inputs():
        import jax
        import jax.numpy as jnp
        _rk = jax.random.key(seed)
        x = -0.0002928 + 1 * jax.random.normal(jax.random.fold_in(_rk, 1), (8, 256, 128), jnp.float32)
        _lenS = 256 - jax.random.randint(jax.random.fold_in(_rk, 7), (8,), 0, max(1, 256 // 4) + 1, jnp.int32)
        _lenS2 = 256 - jax.random.randint(jax.random.fold_in(_rk, 8), (8,), 0, max(1, 256 // 4) + 1, jnp.int32)
        _ctx_1024P = jax.random.normal(jax.random.fold_in(_rk, 11), (8, 16, 128), jnp.float32)
        _ctx_1024c = jax.random.dirichlet(jax.random.fold_in(_rk, 511), 0.3 * jnp.ones((16,), jnp.float32), (8, 256))
        _ctx_1024t = jnp.einsum('bsk,bkd->bsd', _ctx_1024c, _ctx_1024P)
        _ctx_1024t = _ctx_1024t * jax.lax.rsqrt(jnp.mean(jnp.square(_ctx_1024t)) + 1e-12) * 0.953939
        ctx_1024 = -1.39393e-06 + 0.999914 * (_ctx_1024t + 0.3 * jax.random.normal(jax.random.fold_in(_rk, 611), (8, 256, 128), jnp.float32))
        pos_BxS2 = jnp.broadcast_to(jnp.arange(256, dtype=jnp.int32), (8, 256))
        return (x, ctx_1024, pos_BxS2)
    x, ctx_1024, pos_BxS2 = _rec_inputs()

    def _L0_xattn_setup():
        import jax, jax.numpy as jnp
        import numpy as np
        EPS = 1e-05

        def _layernorm(x, g, b):
            m = jnp.mean(x, axis=-1, keepdims=True)
            v = jnp.mean((x - m) ** 2, axis=-1, keepdims=True)
            return (x - m) / jnp.sqrt(v + EPS) * g + b

        def _mha(x, kv, Wq, Wk, Wv, mask, causal):
            m = mask[:, None]
            Q = jnp.einsum('bsd,hdk->bhsk', x, Wq) * m
            K = jnp.einsum('bsd,hdk->bhsk', kv, Wk) * m
            V = jnp.einsum('bsd,hdk->bhsk', kv, Wv) * m
            energy = jnp.einsum('bhsk,bhtk->bhst', Q, K)
            S = energy.shape[-1]
            lengths = jnp.sum(energy[:, :, 0, :] != 0, axis=-1)
            cols = jnp.arange(S)
            energy = jnp.where(cols[None, None, None, :] >= lengths[:, :, None, None], -jnp.inf, energy)
            if causal:
                energy = jnp.where(cols[None, :] > cols[:, None], -jnp.inf, energy)
            dk = Wq.shape[-1]
            score = jax.nn.softmax(energy / jnp.sqrt(jnp.asarray(dk, energy.dtype)), axis=-1)
            out = jnp.einsum('bhst,bhtk->bhsk', score, V) * m
            B, H, Sx, dkk = out.shape
            return out.transpose(0, 2, 1, 3).reshape(B, Sx, H * dkk)
        key = jax.random.key(seed)
        ks = jax.random.split(key, 20)
        B, S, D, H = (2, 256, 128, 16)
        dk = D // H
        sd = 0.02
        inp = {'x': jax.random.normal(ks[0], (B, S, D), jnp.float32), 'context': jax.random.normal(ks[1], (B, S, D), jnp.float32), 'Wq1': jax.random.normal(ks[2], (H, D, dk), jnp.float32) * sd, 'Wk1': jax.random.normal(ks[3], (H, D, dk), jnp.float32) * sd, 'Wv1': jax.random.normal(ks[4], (H, D, dk), jnp.float32) * sd, 'Wq2': jax.random.normal(ks[5], (H, D, dk), jnp.float32) * sd, 'Wk2': jax.random.normal(ks[6], (H, D, dk), jnp.float32) * sd, 'Wv2': jax.random.normal(ks[7], (H, D, dk), jnp.float32) * sd, 'ln1_g': jnp.ones((D,), jnp.float32), 'ln1_b': jnp.zeros((D,), jnp.float32), 'ln2_g': jnp.ones((D,), jnp.float32), 'ln2_b': jnp.zeros((D,), jnp.float32), 'ln3_g': jnp.ones((D,), jnp.float32), 'ln3_b': jnp.zeros((D,), jnp.float32), 'fc1_w': jax.random.normal(ks[8], (D, D), jnp.float32) * sd, 'fc1_b': jnp.zeros((D,), jnp.float32), 'fc2_w': jax.random.normal(ks[9], (D, D), jnp.float32) * sd, 'fc2_b': jnp.zeros((D,), jnp.float32)}
        return inp
    _L0_xattn_all = _L0_xattn_setup()
    _L0_xattn_in = {k: v for k, v in _L0_xattn_all.items() if k in ('Wq1', 'Wk1', 'Wv1', 'Wq2', 'Wk2', 'Wv2', 'ln1_g', 'ln1_b', 'ln2_g', 'ln2_b', 'ln3_g', 'ln3_b', 'fc1_w', 'fc1_b', 'fc2_w', 'fc2_b')}
    del _L0_xattn_all

    def _L1_xattn_setup():
        import jax, jax.numpy as jnp
        import numpy as np
        D, H, DH, FF, NQ = (128, 16, 64, 512, 32)

        def layer_norm(x, gamma):
            mu = x.mean(-1, keepdims=True)
            var = x.var(-1, keepdims=True)
            return (x - mu) / jnp.sqrt(var + 1e-05) * gamma

        def rotate_half(x):
            x1, x2 = jnp.split(x, 2, axis=-1)
            return jnp.concatenate((-x2, x1), axis=-1)

        def apply_rope(pos, t):
            return t * jnp.cos(pos) + rotate_half(t) * jnp.sin(pos)
        key = jax.random.key(seed)
        ks = jax.random.split(key, 12)
        B, N = (2, 256)
        s = 0.02
        return {'x': jax.random.normal(ks[0], (B, N, D), jnp.float32), 'context': jax.random.normal(ks[1], (B, NQ, D), jnp.float32), 'gamma_pt': jnp.ones((D,), jnp.float32), 'w_fused': jax.random.normal(ks[2], (D, H * DH + DH + DH + 2 * FF), jnp.float32) * s, 'w_attn_out': jax.random.normal(ks[3], (H * DH, D), jnp.float32) * s, 'w_ff_out': jax.random.normal(ks[4], (FF, D), jnp.float32) * s, 'gamma_ca': jnp.ones((D,), jnp.float32), 'gamma_ctx': jnp.ones((D,), jnp.float32), 'w_q': jax.random.normal(ks[5], (D, H * DH), jnp.float32) * s, 'w_kv': jax.random.normal(ks[6], (D, 2 * DH), jnp.float32) * s, 'w_out': jax.random.normal(ks[7], (H * DH, D), jnp.float32) * s, 'w_ff1': jax.random.normal(ks[8], (D, 2 * FF), jnp.float32) * s, 'w_ff2': jax.random.normal(ks[9], (FF, D), jnp.float32) * s}
    _L1_xattn_all = _L1_xattn_setup()
    _L1_xattn_in = {k: v for k, v in _L1_xattn_all.items() if k in ('gamma_pt', 'w_fused', 'w_attn_out', 'w_ff_out', 'gamma_ca', 'gamma_ctx', 'w_q', 'w_kv', 'w_out', 'w_ff1', 'w_ff2')}
    del _L1_xattn_all

    def _L2_xattn_setup():
        import jax, jax.numpy as jnp
        import numpy as np
        EPS = 1e-06
        NUM_HEADS = 16
        THETA = 10000.0

        def rmsnorm(x, w):
            return x * jax.lax.rsqrt(jnp.mean(x * x, axis=-1, keepdims=True) + EPS) * w

        def rope(x, pos):
            d = x.shape[-1]
            inv_freq = 1.0 / THETA ** (jnp.arange(0, d, 2, dtype=jnp.float32) / d)
            ang = pos.astype(jnp.float32)[:, None, :, None] * inv_freq
            cos = jnp.concatenate([jnp.cos(ang), jnp.cos(ang)], axis=-1)
            sin = jnp.concatenate([jnp.sin(ang), jnp.sin(ang)], axis=-1)
            x1, x2 = (x[..., :d // 2], x[..., d // 2:])
            rot = jnp.concatenate([-x2, x1], axis=-1)
            return x * cos + rot * sin

        def attention(tgt, src, tpos, spos, Wq, Wkv, Wo, qn, kn):
            b, n, dim = tgt.shape
            m = src.shape[1]
            h = NUM_HEADS
            d = dim // h
            q = (tgt @ Wq).reshape(b, n, h, d).transpose(0, 2, 1, 3)
            kv = (src @ Wkv).reshape(b, m, 2, h, d)
            k = kv[:, :, 0].transpose(0, 2, 1, 3)
            v = kv[:, :, 1].transpose(0, 2, 1, 3)
            q = rmsnorm(q, qn)
            k = rmsnorm(k, kn)
            q = rope(q, tpos)
            k = rope(k, spos)
            scores = jnp.einsum('bhnd,bhmd->bhnm', q, k) / jnp.sqrt(jnp.float32(d))
            attn = jax.nn.softmax(scores, axis=-1)
            x = jnp.einsum('bhnm,bhmd->bhnd', attn, v)
            x = x.transpose(0, 2, 1, 3).reshape(b, n, dim)
            return x @ Wo

        def ffn(x, W1, W2, W3):
            return jax.nn.silu(x @ W1) * (x @ W3) @ W2
        key = jax.random.key(seed)
        ks = jax.random.split(key, 20)
        b, n, dim, hid = (2, 256, 128, 512)
        hd = dim // NUM_HEADS
        s = 0.02
        inp = {'tgt': jax.random.normal(ks[0], (b, n, dim), jnp.float32), 'src': jax.random.normal(ks[1], (b, n, dim), jnp.float32), 'tgt_pos': jnp.tile(jnp.arange(n, dtype=jnp.int32)[None, :], (b, 1)), 'src_pos': jnp.tile(jnp.arange(n, dtype=jnp.int32)[None, :], (b, 1)), 'ca_Wq': jax.random.normal(ks[2], (dim, dim), jnp.float32) * s, 'ca_Wkv': jax.random.normal(ks[3], (dim, 2 * dim), jnp.float32) * s, 'ca_Wo': jax.random.normal(ks[4], (dim, dim), jnp.float32) * s, 'ca_qn': jnp.ones((hd,), jnp.float32), 'ca_kn': jnp.ones((hd,), jnp.float32), 'sa_Wq': jax.random.normal(ks[5], (dim, dim), jnp.float32) * s, 'sa_Wkv': jax.random.normal(ks[6], (dim, 2 * dim), jnp.float32) * s, 'sa_Wo': jax.random.normal(ks[7], (dim, dim), jnp.float32) * s, 'sa_qn': jnp.ones((hd,), jnp.float32), 'sa_kn': jnp.ones((hd,), jnp.float32), 'pre_ca_w': jnp.ones((dim,), jnp.float32), 'pre_sa_w': jnp.ones((dim,), jnp.float32), 'pre_ffn_w': jnp.ones((dim,), jnp.float32), 'W1': jax.random.normal(ks[8], (dim, hid), jnp.float32) * s, 'W2': jax.random.normal(ks[9], (hid, dim), jnp.float32) * s, 'W3': jax.random.normal(ks[10], (dim, hid), jnp.float32) * s}
        return inp
    _L2_xattn_all = _L2_xattn_setup()
    _L2_xattn_in = {k: v for k, v in _L2_xattn_all.items() if k in ('ca_Wq', 'ca_Wkv', 'ca_Wo', 'ca_qn', 'ca_kn', 'sa_Wq', 'sa_Wkv', 'sa_Wo', 'sa_qn', 'sa_kn', 'pre_ca_w', 'pre_sa_w', 'pre_ffn_w', 'W1', 'W2', 'W3')}
    del _L2_xattn_all

    def _L3_xattn_setup():
        import jax, jax.numpy as jnp
        import numpy as np
        DIM = 128
        HEADS = 16
        D_HEAD = 64
        INNER = HEADS * D_HEAD
        FF_INNER = 4 * DIM

        def _block(x, context, Wq, Wk, Wv, Wo, bo, W1, b1, W2, b2):
            B, Lq, _ = x.shape
            scale = 1.0 / np.sqrt(D_HEAD).astype(np.float32)
            q = (x @ Wq).reshape(B, Lq, HEADS, D_HEAD)
            k = (context @ Wk).reshape(B, -1, HEADS, D_HEAD)
            v = (context @ Wv).reshape(B, -1, HEADS, D_HEAD)
            sim = jnp.einsum('bqhd,bkhd->bhqk', q, k) * scale
            attn = jax.nn.softmax(sim, axis=-1)
            out = jnp.einsum('bhqk,bkhd->bqhd', attn, v).reshape(B, Lq, INNER)
            x = out @ Wo + bo + x
            h = jax.nn.gelu(x @ W1 + b1, approximate=False)
            return h @ W2 + b2 + x
        key = jax.random.key(seed)
        ks = jax.random.split(key, 12)
        s = lambda fan_in: 1.0 / np.sqrt(fan_in)
        x = jax.random.normal(ks[0], (4, 128, DIM), dtype=jnp.float32)
        context = jax.random.normal(ks[1], (4, 256, DIM), dtype=jnp.float32)
        Wq = jax.random.normal(ks[2], (DIM, INNER), dtype=jnp.float32) * s(DIM)
        Wk = jax.random.normal(ks[3], (DIM, INNER), dtype=jnp.float32) * s(DIM)
        Wv = jax.random.normal(ks[4], (DIM, INNER), dtype=jnp.float32) * s(DIM)
        Wo = jax.random.normal(ks[5], (INNER, DIM), dtype=jnp.float32) * s(INNER)
        bo = jax.random.normal(ks[6], (DIM,), dtype=jnp.float32) * 0.01
        W1 = jax.random.normal(ks[7], (DIM, FF_INNER), dtype=jnp.float32) * s(DIM)
        b1 = jax.random.normal(ks[8], (FF_INNER,), dtype=jnp.float32) * 0.01
        W2 = jax.random.normal(ks[9], (FF_INNER, DIM), dtype=jnp.float32) * s(FF_INNER)
        b2 = jax.random.normal(ks[10], (DIM,), dtype=jnp.float32) * 0.01
        return {'x': x, 'context': context, 'Wq': Wq, 'Wk': Wk, 'Wv': Wv, 'Wo': Wo, 'bo': bo, 'W1': W1, 'b1': b1, 'W2': W2, 'b2': b2}
    _L3_xattn_all = _L3_xattn_setup()
    _L3_xattn_in = {k: v for k, v in _L3_xattn_all.items() if k in ('Wq', 'Wk', 'Wv', 'Wo', 'bo', 'W1', 'b1', 'W2', 'b2')}
    del _L3_xattn_all
    return {'x': x, 'ctx_1024': ctx_1024, 'pos_BxS2': pos_BxS2, 'L0_xattn_Wq1': _L0_xattn_in['Wq1'], 'L0_xattn_Wk1': _L0_xattn_in['Wk1'], 'L0_xattn_Wv1': _L0_xattn_in['Wv1'], 'L0_xattn_Wq2': _L0_xattn_in['Wq2'], 'L0_xattn_Wk2': _L0_xattn_in['Wk2'], 'L0_xattn_Wv2': _L0_xattn_in['Wv2'], 'L0_xattn_ln1_g': _L0_xattn_in['ln1_g'], 'L0_xattn_ln1_b': _L0_xattn_in['ln1_b'], 'L0_xattn_ln2_g': _L0_xattn_in['ln2_g'], 'L0_xattn_ln2_b': _L0_xattn_in['ln2_b'], 'L0_xattn_ln3_g': _L0_xattn_in['ln3_g'], 'L0_xattn_ln3_b': _L0_xattn_in['ln3_b'], 'L0_xattn_fc1_w': _L0_xattn_in['fc1_w'], 'L0_xattn_fc1_b': _L0_xattn_in['fc1_b'], 'L0_xattn_fc2_w': _L0_xattn_in['fc2_w'], 'L0_xattn_fc2_b': _L0_xattn_in['fc2_b'], 'L1_xattn_gamma_pt': _L1_xattn_in['gamma_pt'], 'L1_xattn_w_fused': _L1_xattn_in['w_fused'], 'L1_xattn_w_attn_out': _L1_xattn_in['w_attn_out'], 'L1_xattn_w_ff_out': _L1_xattn_in['w_ff_out'], 'L1_xattn_gamma_ca': _L1_xattn_in['gamma_ca'], 'L1_xattn_gamma_ctx': _L1_xattn_in['gamma_ctx'], 'L1_xattn_w_q': _L1_xattn_in['w_q'], 'L1_xattn_w_kv': _L1_xattn_in['w_kv'], 'L1_xattn_w_out': _L1_xattn_in['w_out'], 'L1_xattn_w_ff1': _L1_xattn_in['w_ff1'], 'L1_xattn_w_ff2': _L1_xattn_in['w_ff2'], 'L2_xattn_ca_Wq': _L2_xattn_in['ca_Wq'], 'L2_xattn_ca_Wkv': _L2_xattn_in['ca_Wkv'], 'L2_xattn_ca_Wo': _L2_xattn_in['ca_Wo'], 'L2_xattn_ca_qn': _L2_xattn_in['ca_qn'], 'L2_xattn_ca_kn': _L2_xattn_in['ca_kn'], 'L2_xattn_sa_Wq': _L2_xattn_in['sa_Wq'], 'L2_xattn_sa_Wkv': _L2_xattn_in['sa_Wkv'], 'L2_xattn_sa_Wo': _L2_xattn_in['sa_Wo'], 'L2_xattn_sa_qn': _L2_xattn_in['sa_qn'], 'L2_xattn_sa_kn': _L2_xattn_in['sa_kn'], 'L2_xattn_pre_ca_w': _L2_xattn_in['pre_ca_w'], 'L2_xattn_pre_sa_w': _L2_xattn_in['pre_sa_w'], 'L2_xattn_pre_ffn_w': _L2_xattn_in['pre_ffn_w'], 'L2_xattn_W1': _L2_xattn_in['W1'], 'L2_xattn_W2': _L2_xattn_in['W2'], 'L2_xattn_W3': _L2_xattn_in['W3'], 'L3_xattn_Wq': _L3_xattn_in['Wq'], 'L3_xattn_Wk': _L3_xattn_in['Wk'], 'L3_xattn_Wv': _L3_xattn_in['Wv'], 'L3_xattn_Wo': _L3_xattn_in['Wo'], 'L3_xattn_bo': _L3_xattn_in['bo'], 'L3_xattn_W1': _L3_xattn_in['W1'], 'L3_xattn_b1': _L3_xattn_in['b1'], 'L3_xattn_W2': _L3_xattn_in['W2'], 'L3_xattn_b2': _L3_xattn_in['b2']}

def reference(x, ctx_1024, pos_BxS2, L0_xattn_Wq1, L0_xattn_Wk1, L0_xattn_Wv1, L0_xattn_Wq2, L0_xattn_Wk2, L0_xattn_Wv2, L0_xattn_ln1_g, L0_xattn_ln1_b, L0_xattn_ln2_g, L0_xattn_ln2_b, L0_xattn_ln3_g, L0_xattn_ln3_b, L0_xattn_fc1_w, L0_xattn_fc1_b, L0_xattn_fc2_w, L0_xattn_fc2_b, L1_xattn_gamma_pt, L1_xattn_w_fused, L1_xattn_w_attn_out, L1_xattn_w_ff_out, L1_xattn_gamma_ca, L1_xattn_gamma_ctx, L1_xattn_w_q, L1_xattn_w_kv, L1_xattn_w_out, L1_xattn_w_ff1, L1_xattn_w_ff2, L2_xattn_ca_Wq, L2_xattn_ca_Wkv, L2_xattn_ca_Wo, L2_xattn_ca_qn, L2_xattn_ca_kn, L2_xattn_sa_Wq, L2_xattn_sa_Wkv, L2_xattn_sa_Wo, L2_xattn_sa_qn, L2_xattn_sa_kn, L2_xattn_pre_ca_w, L2_xattn_pre_sa_w, L2_xattn_pre_ffn_w, L2_xattn_W1, L2_xattn_W2, L2_xattn_W3, L3_xattn_Wq, L3_xattn_Wk, L3_xattn_Wv, L3_xattn_Wo, L3_xattn_bo, L3_xattn_W1, L3_xattn_b1, L3_xattn_W2, L3_xattn_b2):
    import jax
    import jax.numpy as jnp

    def _L0_xattn_ref(x, context, Wq1, Wk1, Wv1, Wq2, Wk2, Wv2, ln1_g, ln1_b, ln2_g, ln2_b, ln3_g, ln3_b, fc1_w, fc1_b, fc2_w, fc2_b):
        import jax, jax.numpy as jnp
        import numpy as np
        EPS = 1e-05

        def _layernorm(x, g, b):
            m = jnp.mean(x, axis=-1, keepdims=True)
            v = jnp.mean((x - m) ** 2, axis=-1, keepdims=True)
            return (x - m) / jnp.sqrt(v + EPS) * g + b

        def _mha(x, kv, Wq, Wk, Wv, mask, causal):
            m = mask[:, None]
            Q = jnp.einsum('bsd,hdk->bhsk', x, Wq) * m
            K = jnp.einsum('bsd,hdk->bhsk', kv, Wk) * m
            V = jnp.einsum('bsd,hdk->bhsk', kv, Wv) * m
            energy = jnp.einsum('bhsk,bhtk->bhst', Q, K)
            S = energy.shape[-1]
            lengths = jnp.sum(energy[:, :, 0, :] != 0, axis=-1)
            cols = jnp.arange(S)
            energy = jnp.where(cols[None, None, None, :] >= lengths[:, :, None, None], -jnp.inf, energy)
            if causal:
                energy = jnp.where(cols[None, :] > cols[:, None], -jnp.inf, energy)
            dk = Wq.shape[-1]
            score = jax.nn.softmax(energy / jnp.sqrt(jnp.asarray(dk, energy.dtype)), axis=-1)
            out = jnp.einsum('bhst,bhtk->bhsk', score, V) * m
            B, H, Sx, dkk = out.shape
            return out.transpose(0, 2, 1, 3).reshape(B, Sx, H * dkk)
        mask0 = 1.0 - jnp.all(x == 0, axis=2, keepdims=True).astype(x.dtype)
        z = _mha(x, x, Wq1, Wk1, Wv1, mask0, causal=True)
        x1 = _layernorm(x + z, ln1_g, ln1_b)
        mask1 = 1.0 - jnp.all(x1 == 0, axis=2, keepdims=True).astype(x1.dtype)
        z = _mha(x1, context, Wq2, Wk2, Wv2, mask1, causal=False)
        x2 = _layernorm(x1 + z, ln2_g, ln2_b)
        z = jnp.maximum(x2 @ fc1_w.T + fc1_b, 0.0) * mask0
        z = (z @ fc2_w.T + fc2_b) * mask0
        return _layernorm(x2 + z, ln3_g, ln3_b)

    def _L1_xattn_ref(x, context, gamma_pt, w_fused, w_attn_out, w_ff_out, gamma_ca, gamma_ctx, w_q, w_kv, w_out, w_ff1, w_ff2):
        import jax, jax.numpy as jnp
        import numpy as np
        D, H, DH, FF, NQ = (128, 16, 64, 512, 32)

        def layer_norm(x, gamma):
            mu = x.mean(-1, keepdims=True)
            var = x.var(-1, keepdims=True)
            return (x - mu) / jnp.sqrt(var + 1e-05) * gamma

        def rotate_half(x):
            x1, x2 = jnp.split(x, 2, axis=-1)
            return jnp.concatenate((-x2, x1), axis=-1)

        def apply_rope(pos, t):
            return t * jnp.cos(pos) + rotate_half(t) * jnp.sin(pos)
        B, N, _ = x.shape
        scale = DH ** (-0.5)
        neg = jnp.finfo(x.dtype).max
        xn = layer_norm(x, gamma_pt)
        proj = xn @ w_fused
        q, k, v, ff = jnp.split(proj, [H * DH, H * DH + DH, H * DH + 2 * DH], axis=-1)
        q = q.reshape(B, N, H, DH).transpose(0, 2, 1, 3)
        inv_freq = 1.0 / 10000.0 ** (jnp.arange(0, DH, 2, dtype=jnp.float32) / DH)
        freqs = jnp.arange(N, dtype=jnp.float32)[:, None] * inv_freq[None, :]
        pos = jnp.concatenate((freqs, freqs), axis=-1)
        q = apply_rope(pos, q)
        k = apply_rope(pos, k)
        q = q * scale
        sim = jnp.einsum('bhid,bjd->bhij', q, k)
        causal = jnp.triu(jnp.ones((N, N), dtype=bool), 1)
        sim = jnp.where(causal, -neg, sim)
        attn = jax.nn.softmax(sim, axis=-1)
        out = jnp.einsum('bhij,bjd->bhid', attn, v)
        out = out.transpose(0, 2, 1, 3).reshape(B, N, H * DH)
        ff_val, ff_gate = jnp.split(ff, 2, axis=-1)
        y = x + out @ w_attn_out + jax.nn.silu(ff_gate) * ff_val @ w_ff_out
        yn = layer_norm(y, gamma_ca)
        ctx = layer_norm(context, gamma_ctx)
        cq = (yn @ w_q).reshape(B, N, H, DH).transpose(0, 2, 1, 3) * scale
        ck, cv = jnp.split(ctx @ w_kv, 2, axis=-1)
        csim = jnp.einsum('bhid,bjd->bhij', cq, ck)
        cattn = jax.nn.softmax(csim, axis=-1)
        cout = jnp.einsum('bhij,bjd->bhid', cattn, cv)
        cout = cout.transpose(0, 2, 1, 3).reshape(B, N, H * DH) @ w_out
        fv, fg = jnp.split(yn @ w_ff1, 2, axis=-1)
        cout = cout + jax.nn.silu(fg) * fv @ w_ff2
        return y + cout

    def _L2_xattn_ref(tgt, src, tgt_pos, src_pos, ca_Wq, ca_Wkv, ca_Wo, ca_qn, ca_kn, sa_Wq, sa_Wkv, sa_Wo, sa_qn, sa_kn, pre_ca_w, pre_sa_w, pre_ffn_w, W1, W2, W3):
        import jax, jax.numpy as jnp
        import numpy as np
        EPS = 1e-06
        NUM_HEADS = 16
        THETA = 10000.0

        def rmsnorm(x, w):
            return x * jax.lax.rsqrt(jnp.mean(x * x, axis=-1, keepdims=True) + EPS) * w

        def rope(x, pos):
            d = x.shape[-1]
            inv_freq = 1.0 / THETA ** (jnp.arange(0, d, 2, dtype=jnp.float32) / d)
            ang = pos.astype(jnp.float32)[:, None, :, None] * inv_freq
            cos = jnp.concatenate([jnp.cos(ang), jnp.cos(ang)], axis=-1)
            sin = jnp.concatenate([jnp.sin(ang), jnp.sin(ang)], axis=-1)
            x1, x2 = (x[..., :d // 2], x[..., d // 2:])
            rot = jnp.concatenate([-x2, x1], axis=-1)
            return x * cos + rot * sin

        def attention(tgt, src, tpos, spos, Wq, Wkv, Wo, qn, kn):
            b, n, dim = tgt.shape
            m = src.shape[1]
            h = NUM_HEADS
            d = dim // h
            q = (tgt @ Wq).reshape(b, n, h, d).transpose(0, 2, 1, 3)
            kv = (src @ Wkv).reshape(b, m, 2, h, d)
            k = kv[:, :, 0].transpose(0, 2, 1, 3)
            v = kv[:, :, 1].transpose(0, 2, 1, 3)
            q = rmsnorm(q, qn)
            k = rmsnorm(k, kn)
            q = rope(q, tpos)
            k = rope(k, spos)
            scores = jnp.einsum('bhnd,bhmd->bhnm', q, k) / jnp.sqrt(jnp.float32(d))
            attn = jax.nn.softmax(scores, axis=-1)
            x = jnp.einsum('bhnm,bhmd->bhnd', attn, v)
            x = x.transpose(0, 2, 1, 3).reshape(b, n, dim)
            return x @ Wo

        def ffn(x, W1, W2, W3):
            return jax.nn.silu(x @ W1) * (x @ W3) @ W2
        y = rmsnorm(tgt, pre_ca_w)
        tgt = tgt + attention(y, src, tgt_pos, src_pos, ca_Wq, ca_Wkv, ca_Wo, ca_qn, ca_kn)
        y = rmsnorm(tgt, pre_sa_w)
        tgt = tgt + attention(y, y, tgt_pos, tgt_pos, sa_Wq, sa_Wkv, sa_Wo, sa_qn, sa_kn)
        y = rmsnorm(tgt, pre_ffn_w)
        return tgt + ffn(y, W1, W2, W3)

    def _L3_xattn_ref(x, context, Wq, Wk, Wv, Wo, bo, W1, b1, W2, b2):
        import jax, jax.numpy as jnp
        import numpy as np
        DIM = 128
        HEADS = 16
        D_HEAD = 64
        INNER = HEADS * D_HEAD
        FF_INNER = 4 * DIM

        def _block(x, context, Wq, Wk, Wv, Wo, bo, W1, b1, W2, b2):
            B, Lq, _ = x.shape
            scale = 1.0 / np.sqrt(D_HEAD).astype(np.float32)
            q = (x @ Wq).reshape(B, Lq, HEADS, D_HEAD)
            k = (context @ Wk).reshape(B, -1, HEADS, D_HEAD)
            v = (context @ Wv).reshape(B, -1, HEADS, D_HEAD)
            sim = jnp.einsum('bqhd,bkhd->bhqk', q, k) * scale
            attn = jax.nn.softmax(sim, axis=-1)
            out = jnp.einsum('bhqk,bkhd->bqhd', attn, v).reshape(B, Lq, INNER)
            x = out @ Wo + bo + x
            h = jax.nn.gelu(x @ W1 + b1, approximate=False)
            return h @ W2 + b2 + x
        return _block(x, context, Wq, Wk, Wv, Wo, bo, W1, b1, W2, b2)
    x = _L0_xattn_ref(x, ctx_1024, L0_xattn_Wq1, L0_xattn_Wk1, L0_xattn_Wv1, L0_xattn_Wq2, L0_xattn_Wk2, L0_xattn_Wv2, L0_xattn_ln1_g, L0_xattn_ln1_b, L0_xattn_ln2_g, L0_xattn_ln2_b, L0_xattn_ln3_g, L0_xattn_ln3_b, L0_xattn_fc1_w, L0_xattn_fc1_b, L0_xattn_fc2_w, L0_xattn_fc2_b)
    x = _L1_xattn_ref(x, ctx_1024, L1_xattn_gamma_pt, L1_xattn_w_fused, L1_xattn_w_attn_out, L1_xattn_w_ff_out, L1_xattn_gamma_ca, L1_xattn_gamma_ctx, L1_xattn_w_q, L1_xattn_w_kv, L1_xattn_w_out, L1_xattn_w_ff1, L1_xattn_w_ff2)
    x = _L2_xattn_ref(x, ctx_1024, pos_BxS2, pos_BxS2, L2_xattn_ca_Wq, L2_xattn_ca_Wkv, L2_xattn_ca_Wo, L2_xattn_ca_qn, L2_xattn_ca_kn, L2_xattn_sa_Wq, L2_xattn_sa_Wkv, L2_xattn_sa_Wo, L2_xattn_sa_qn, L2_xattn_sa_kn, L2_xattn_pre_ca_w, L2_xattn_pre_sa_w, L2_xattn_pre_ffn_w, L2_xattn_W1, L2_xattn_W2, L2_xattn_W3)
    x = _L3_xattn_ref(x, ctx_1024, L3_xattn_Wq, L3_xattn_Wk, L3_xattn_Wv, L3_xattn_Wo, L3_xattn_bo, L3_xattn_W1, L3_xattn_b1, L3_xattn_W2, L3_xattn_b2)
    return x

_drawn_inputs = setup_inputs


def setup_inputs(seed=0):
    import zlib

    import numpy as np

    out = dict(_drawn_inputs(seed))
    spreads = {'L0_xattn_ln1_g': (1.0, 0.2),
     'L0_xattn_ln1_b': (0.0, 0.1),
     'L0_xattn_ln2_g': (1.0, 0.2),
     'L0_xattn_ln2_b': (0.0, 0.1),
     'L0_xattn_ln3_g': (1.0, 0.2),
     'L0_xattn_ln3_b': (0.0, 0.1),
     'L0_xattn_fc1_b': (0.0, 0.731),
     'L0_xattn_fc2_b': (0.0, 0.1),
     'L1_xattn_gamma_pt': (1.0, 0.6),
     'L1_xattn_gamma_ca': (1.0, 0.6),
     'L1_xattn_gamma_ctx': (1.0, 0.6),
     'L2_xattn_ca_qn': (1.0, 0.6),
     'L2_xattn_ca_kn': (1.0, 0.6),
     'L2_xattn_sa_qn': (1.0, 0.6),
     'L2_xattn_sa_kn': (1.0, 0.6),
     'L2_xattn_pre_ca_w': (1.0, 0.6),
     'L2_xattn_pre_sa_w': (1.0, 0.6),
     'L2_xattn_pre_ffn_w': (1.0, 0.6)}
    factors = {'L0_xattn_Wq1': 8.0,
     'L0_xattn_Wk1': 8.0,
     'L0_xattn_Wq2': 8.0,
     'L0_xattn_Wk2': 8.0,
     'L1_xattn_w_ff_out': 4.959,
     'L1_xattn_w_q': 48.401,
     'L1_xattn_w_ff1': 5.039,
     'L1_xattn_w_ff2': 4.955,
     'L2_xattn_ca_Wq': 64.0,
     'L2_xattn_sa_Wq': 8.0,
     'L2_xattn_sa_Wkv': 3.804,
     'L2_xattn_sa_Wo': 4.345,
     'L2_xattn_W1': 5.489,
     'L2_xattn_W2': 5.461,
     'L2_xattn_W3': 5.491,
     'L3_xattn_bo': 40.707,
     'L3_xattn_b1': 64.0,
     'L3_xattn_b2': 46.078,
     'L2_xattn_ca_Wkv': 5.923,
     'L2_xattn_ca_Wo': 5.864}
    for name, (base, spread) in spreads.items():
        noise = np.random.default_rng([zlib.crc32(name.encode()), seed]).standard_normal(out[name].shape)
        drawn = base * np.exp(spread * noise) if base else spread * noise
        out[name] = jnp.asarray(drawn.astype(out[name].dtype))
    for name, factor in factors.items():
        out[name] = (out[name] * factor).astype(out[name].dtype)
    return out
```

```python
from contextlib import ExitStack

import numpy as np

import concourse.bass as bass
from concourse import mybir

F32 = mybir.dt.float32
F32R = mybir.dt.float32r
BF16 = mybir.dt.bfloat16
I32 = mybir.dt.int32
ALU = mybir.AluOpType
ACT = mybir.ActivationFunctionType
AX = mybir.AxisListType.X

P = 128
B, S, D, H = 8, 256, 128, 16
PAIR = 2
ITERATIONS = B // PAIR
ST = S // P
DH = 64
DS = D // H
FF = 512
NF = FF // P
GROUPS, GH = 4, 4
BLK = 32
COL_MAX, COL_LEN = 24, 25
NEG = -1.0e30
MAX_GUARD = 1.0e29
EPS_LN, EPS_RMS = 1e-5, 1e-6
NWORK, NSA, NST, NP, NR = 2, 2, 2, 4, 2
TWO_PI = 2.0 * np.pi
ROUND = 12582912.0

NARROW = [True, True, False, False, True, True, False]
CAUSAL = [True, False, True, False, False, False, False]
SCALE = [DS ** -0.5 if n else DH ** -0.5 for n in NARROW]

W_COLS = {}


def _plan_weights():
    at = 0
    for name, cols in [("L0_1", 384), ("L0_2", 384), ("fc1", 128), ("fc2", 128),
                       ("fused", 2176), ("attn_out", 1024), ("ff_out", 512), ("wq", 1024), ("wkv", 128),
                       ("w_out", 1024), ("w_ff1", 1024), ("w_ff2", 512), ("rot", 1024),
                       ("k2", 128), ("k2rot", 128), ("k2c", 128),
                       ("ca", 384), ("ca_o", 128), ("sa", 384), ("sa_o", 128),
                       ("g_w1", 512), ("g_w3", 512), ("g_w2", 512),
                       ("q3", 1024), ("k3", 1024), ("v3", 1024), ("o3", 1024), ("w1_3", 512), ("w2_3", 512)]:
        W_COLS[name] = (at, cols)
        at += cols
    return at


W_TOTAL = _plan_weights()


def schedule():
    steps = []

    def both(*step):
        for j in range(PAIR):
            steps.append((step[0], *step[1:], j))

    def attention(a):
        groups = [(a, j, g) for j in range(PAIR) for g in range(GROUPS)]
        if not NARROW[a]:
            steps.append(("heads", *groups[0]))
        for i in range(len(groups) + 3):
            if i < len(groups):
                steps.append(("maxima", *groups[i]))
            if 1 <= i <= len(groups):
                steps.append(("probs", *groups[i - 1]))
            if i + 1 < len(groups) and not NARROW[a]:
                steps.append(("heads", *groups[i + 1]))
            if 2 <= i <= len(groups) + 1:
                steps.append(("values", *groups[i - 2]))
            if i >= 3 and not NARROW[a]:
                steps.append(("collect", *groups[i - 3]))
        both("finish8" if NARROW[a] else "finish64", a)

    both("start")
    both("transpose", "x0")
    both("transpose", "craw")
    both("prep8", 0)
    both("length", 0)
    attention(0)
    both("norm_l0a")
    both("transpose", "x1")
    both("transpose", "cm")
    both("prep8", 1)
    both("length", 1)
    attention(1)
    both("norm_l0b")
    both("transpose", "x2")
    both("fc")
    both("norm_l0c")
    both("transpose", "x3")
    both("transpose", "cn")
    both("prep64", 2)
    both("ffn", 0)
    attention(2)
    both("norm_l1")
    both("transpose", "x4")
    both("prep64", 3)
    both("ffn", 1)
    attention(3)
    both("rms_a")
    both("transpose", "x5")
    both("prep8", 4)
    attention(4)
    both("transpose", "z4")
    both("outproj", 4)
    both("rms_b")
    both("transpose", "x6")
    both("prep8", 5)
    attention(5)
    both("transpose", "z5")
    both("outproj", 5)
    both("rms_c")
    both("transpose", "x7")
    both("ffn", 2)
    both("ffn_out", 2)
    both("copy_l3")
    both("transpose", "x8")
    both("prep64", 6)
    attention(6)
    both("bias_l3")
    both("transpose", "x9")
    both("gelu")
    both("ffn_out", 3)
    both("store")
    return steps


TRANSPOSES = {"x0": ("x", "xT"), "craw": ("cx", "crT"), "x1": ("y", "xT"), "cm": ("cm", "cT"), "x2": ("x", "xT"),
              "x3": ("y", "xT"), "cn": ("cm", "cT"), "x4": ("y", "xT"), "x5": ("y", "xT"), "z4": ("z", "zT"),
              "x6": ("y", "xT"), "z5": ("z", "zT"), "x7": ("y", "xT"), "x8": ("x", "xT"), "x9": ("x", "xT")}
SOURCES = {0: ("x0", "x0"), 1: ("x1", "cm"), 2: ("x3", "x3"), 3: ("x4", "cn"), 4: ("x5", "craw"), 5: ("x6", "x6"),
           6: ("x8", "craw")}


def build_program(nc, w, out):
    STEPS = schedule()
    ctx = ExitStack()
    with ctx:
        def sb(name, shape, dt=F32):
            return ctx.enter_context(nc.sbuf_tensor(name, shape, dt))

        sems = {}

        def sem(name):
            if name not in sems:
                sems[name] = ctx.enter_context(nc.semaphore(name))
            return sems[name]

        W = sb("weights", [P, W_TOTAL])
        ident = sb("ident", [P, P])
        identb = sb("identb", [P, P], BF16)
        causal_st = sb("causal_st", [P, P], BF16)
        causal_ts = sb("causal_ts", [P, P], BF16)
        rope_cos = sb("rope_cos", [P, S])
        rope_sin = sb("rope_sin", [P, S])
        iota = sb("iota", [P, S])
        sel = sb("sel", [P, GH, P], F32R)
        consts = sb("consts", [P, 128])
        rows = sb("rows", [P, 11, D])
        qkw = sb("qkw", [P, 4, DS])
        cols = sb("cols", [P, 12])
        cs_all = sb("cs_all", [P, ITERATIONS, PAIR * ST * 16])
        cs = sb("cs", [P, PAIR * ST, 2, DS])
        setup = sb("setup", [P, 6, 64])
        pos = sb("pos", [P, B * ST], I32)

        nat = {k: sb(f"nat_{k}", [P, PAIR, ST, D]) for k in ("x", "y", "z", "cx", "cm")}
        trn = {k: sb(f"trn_{k}", [P, PAIR, S]) for k in ("xT", "cT", "crT", "zT")}
        arena = sb("arena", [P, PAIR, 4128])
        tmp = sb("tmp", [P, PAIR, 1024])
        stacked = sb("stacked", [P, PAIR, 2, 1024], F32R)
        wide_parts = sb("wide_parts", [P, NR, 4, 2, S], F32R)
        shared_k = sb("shared_k", [P, PAIR, 2, 1, S], F32R)
        small = sb("small", [P, PAIR, 192])
        blockq = sb("blockq", [P, GROUPS, P], F32R)
        nmax = sb("nmax", [P, 2, ST, P])
        nmaxT = sb("nmaxT", [P, 2, S], F32R)
        onat = sb("onat", [P, 2, ST, GH * DH])
        probs = sb("probs", [P, NP, 2, ST * S])

        psum = ctx.enter_context(nc.psum_tensor("psum", [P, 4096], F32))

        def score_bank(n):
            return psum[:, 512 * (n % NSA):512 * (n % NSA) + 512].rearrange("p (s t) -> p s t", s=ST)

        def transposed_slot(n):
            o = 512 * NSA + 1024 * (n % NST)
            return psum[:, o:o + 1024].rearrange("p (h c) -> p h c", h=2)

        def span(a, tt):
            first = P if CAUSAL[a] and tt == 1 else 0
            return slice(tt * S, tt * S + S - first), first

        def work_bank(n):
            o = 512 * NSA + 1024 * NST + 512 * (n % NWORK)
            return psum[:, o:o + 512]

        def wt(name, c0=0, n=None):
            at, cols_ = W_COLS[name]
            return W[:, at + c0:at + (cols_ if n is None else c0 + n)]

        def qe(j):
            return arena[:, j, 0:1024].rearrange("p (s g i c) -> p s g i c", s=ST, g=GROUPS, i=GH)

        def ke(j):
            return arena[:, j, 1024:2048].rearrange("p (s g i c) -> p s g i c", s=ST, g=GROUPS, i=GH)

        def head_parts(view, st):
            return view[:, st, :, :, 0:24].rearrange("p g i (r d) -> p (g i) r d", r=3)

        def o8T(j):
            return arena[:, j, 1024:2048].rearrange("p (g s) -> p g s", g=GROUPS)

        def v8(j):
            return arena[:, j, 2048:3072].rearrange("p (t h c) -> p t h c", t=ST, h=H)

        def qk_nat(j, n):
            return arena[:, j, 3072 + 512 * n:3584 + 512 * n].rearrange("p (s e) -> p s e", s=ST)

        def hT(j):
            return arena[:, j, 1024:2048].rearrange("p (f s) -> p f s", f=NF)

        def v64(a, j):
            if a == 6:
                return arena[:, j, 0:ST * H * (DH + 1)].rearrange("p (t h c) -> p t h c", t=ST, h=H)
            return arena[:, j, 0:ST * (DH + 1)].rearrange("p (t h c) -> p t h c", t=ST, h=1)

        def o64T(j):
            return arena[:, j, 2080:4128].rearrange("p (c s) -> p c s", c=8)

        def q8T(j):
            return stacked[:, j, 0, :].rearrange("p (g s) -> p g s", g=GROUPS)

        def k8T(j):
            return stacked[:, j, 1, :].rearrange("p (g s) -> p g s", g=GROUPS)

        def wide(a, j, g, n):
            if n >= 2 and a != 6:
                return shared_k[:, j, n - 2]
            return wide_parts[:, (GROUPS * j + g) % NR, n]

        weights_in = sem("weights_in")
        rows_in = sem("rows_in")
        pos_in = sem("pos_in")
        setup_chain = sem("setup_chain")
        setup_sin = sem("setup_sin")
        loop_first = len(sems)
        tokens_in = sem("tokens_in")
        stored = sem("stored")
        work_full = sem("work_full")
        evacuated = [sem(f"evacuated_{s}") for s in range(NWORK)]
        maxima_full = sem("maxima_full")
        maxima_done = sem("maxima_done")
        scores_full = sem("scores_full")
        probs_full = sem("probs_full")
        scalar_out = sem("scalar_out")
        vector_step = sem("vector_step")
        root_asked = sem("root_asked")
        root_done = sem("root_done")
        narrow_ready = sem("narrow_ready")
        blockq_ready = sem("blockq_ready")
        length_done = sem("length_done")
        ones_ready = sem("ones_ready")
        natural = {t: sem(f"natural_{t}") for t in TRANSPOSES}
        hidden_ready = sem("hidden_ready")
        result_ready = sem("result_ready")

        with nc.Block() as block:
            n_weights = [0]
            n_rows = [0]

            @block.sync
            def _(sp):
                for name, view in w["matrices"]:
                    at = name.split(":")
                    dst = wt(at[0], int(at[1]) if len(at) > 1 else 0, int(at[2]))
                    if len(view.shape) == 3:
                        dst = dst.rearrange("p (t n) -> p t n", t=view.shape[1])
                    sp.dma_start(dst, view).then_inc(weights_in, 16)
                    n_weights[0] += 16

            @block.scalar
            def _(act):
                act.dma_start(pos[:, :], w["pos"]).then_inc(pos_in, 16)
                for dst, src in [(ident[:, :], w["ident"]), (iota[:, :], w["iota"].partition_broadcast(P)),
                                 (rope_cos[:, :], w["rope_cos"]), (rope_sin[:, :], w["rope_sin"]),
                                 (consts[:, :], w["consts"]), (nmax[:, 0, 0, :], w["causal"]),
                                 (nmax[:, 0, 1, :], w["causal_t"]),
                                 (arena[:, 0, 0:512], w["sel"])]:
                    act.dma_start(dst, src).then_inc(rows_in, 16)
                    n_rows[0] += 16
                for n, name in enumerate(["ln1_g", "ln1_b", "ln2_g", "ln2_b", "ln3_g", "ln3_b", "fc2_b", "bo", "b2"]):
                    act.dma_start(rows[:, n, :], w[name].partition_broadcast(P)).then_inc(rows_in, 16)
                    n_rows[0] += 16
                for n, name in enumerate(["ca_qn", "ca_kn", "sa_qn", "sa_kn"]):
                    act.dma_start(qkw[:, n, :], w[name].partition_broadcast(P)).then_inc(rows_in, 16)
                    n_rows[0] += 16
                for n, name in enumerate(["gamma_pt", "gamma_ca", "gamma_ctx", "pre_ca_w", "pre_sa_w", "pre_ffn_w",
                                          "fc1_b"]):
                    act.dma_start(cols[:, n:n + 1], w[name].rearrange("(p o) -> p o", o=1)).then_inc(rows_in, 16)
                    n_rows[0] += 16
                act.dma_start(cols[:, 8:12], w["b1"]).then_inc(rows_in, 16)
                n_rows[0] += 16
                act.wait_ge(setup_sin, 1)
                act.activation(setup[:, 2:4, :], setup[:, 4:6, :], ACT.Sin).then_inc(setup_sin, 1)

            @block.vector
            def _(dve):
                n = [0]

                def link(ins):
                    ins.then_inc(setup_chain, 1)
                    n[0] += 1
                    dve.wait_ge(setup_chain, n[0])

                dve.wait_ge(pos_in, 16)
                dve.wait_ge(rows_in, n_rows[0])
                link(dve.tensor_copy(identb[:, :], ident[:, :]))
                link(dve.tensor_copy(causal_st[:, :], nmax[:, 0, 0, :]))
                link(dve.tensor_copy(causal_ts[:, :], nmax[:, 0, 1, :]))
                link(dve.tensor_copy(sel[:, :, :], arena[:, 0, 0:512].rearrange("p (i m) -> p i m", i=GH)))
                link(dve.memset(nmax[:, :, :, :], 0.0))
                link(dve.tensor_scalar(blockq[:, :, :], arena[:, 0, 0:512].rearrange("p (i m) -> p i m", i=GH), 0.0, None, ALU.mult))
                posf = setup[:, 0, 0:B * ST]
                link(dve.tensor_copy(posf, pos[:, :]))
                ang = setup[:, 1, :].rearrange("p (n f) -> p n f", f=4)
                link(dve.tensor_tensor(ang, posf.unsqueeze(2).broadcast_to([P, B * ST, 4]),
                                       consts[:, 48:52].unsqueeze(1).broadcast_to([P, B * ST, 4]), ALU.mult))
                ang, turns, r = setup[:, 1, :], setup[:, 2, :], setup[:, 4, :]
                link(dve.tensor_scalar(turns, ang, 1.0 / TWO_PI, ROUND, ALU.mult, ALU.add))
                link(dve.tensor_scalar(turns, turns, ROUND, None, ALU.subtract))
                c1 = 6.28125
                c2 = 0.001934051513671875
                c3 = float(TWO_PI - c1 - c2)
                link(dve.scalar_tensor_tensor(r, turns, -c1, ang, ALU.mult, ALU.add))
                link(dve.scalar_tensor_tensor(r, turns, -c2, r, ALU.mult, ALU.add))
                link(dve.scalar_tensor_tensor(r, turns, -c3, r, ALU.mult, ALU.add))
                rc = setup[:, 5, :]
                link(dve.tensor_scalar(rc, r, np.pi / 2, None, ALU.add))
                link(dve.tensor_scalar(turns, rc, np.pi, -TWO_PI, ALU.is_gt, ALU.mult))
                link(dve.tensor_tensor(rc, rc, turns, ALU.add))
                dve.tensor_scalar(setup[:, 4:6, :], setup[:, 4:6, :], 3.1415925, -3.1415925, ALU.min, ALU.max)\
                    .then_inc(setup_sin, 1)
                dve.wait_ge(setup_sin, 2)
                table = cs_all[:, :, :].rearrange("p i (t c r f) -> p (i t) c r f", c=2, r=2, f=4)
                sin4 = setup[:, 2, :].rearrange("p (n f) -> p n f", f=4)
                cos4 = setup[:, 3, :].rearrange("p (n f) -> p n f", f=4)
                link(dve.tensor_copy(table[:, :, 0, 0, :], cos4))
                link(dve.tensor_copy(table[:, :, 0, 1, :], cos4))
                link(dve.tensor_scalar(table[:, :, 1, 0, :], sin4, -1.0, None, ALU.mult))
                link(dve.tensor_copy(table[:, :, 1, 1, :], sin4))
                dve.wait_ge(weights_in, n_weights[0])
                for name, c, c0, m in [("fused", 0, 0, 2176), ("wq", 1, 0, 1024), ("w_ff1", 1, 0, 1024),
                                       ("wkv", 2, 0, 128), ("ca", 3, 0, 128), ("sa", 4, 0, 384),
                                       ("g_w1", 5, 0, 512), ("g_w3", 5, 0, 512)]:
                    link(dve.tensor_scalar(wt(name, c0, m), wt(name, c0, m), cols[:, c:c + 1], None, ALU.mult))
                for dst, src, heads in [("rot", wt("fused", 0, 1024), H), ("k2rot", wt("fused", 1024, 64), 1)]:
                    d4 = wt(dst, 0, heads * DH).rearrange("p (h r c) -> p h r c", r=2, c=DH // 2)
                    s4 = src.rearrange("p (h r c) -> p h r c", r=2, c=DH // 2)
                    link(dve.tensor_scalar(d4[:, :, 0, :], s4[:, :, 1, :], -1.0, None, ALU.mult))
                    link(dve.tensor_copy(d4[:, :, 1, :], s4[:, :, 0, :]))
                for half in range(2):
                    link(dve.tensor_copy(wt("k2", DH * half, DH), wt("fused", 1024, DH)))
                    link(dve.tensor_copy(wt("k2c", DH * half, DH), wt("wkv", 0, DH)))
                link(dve.tensor_copy(wt("k2rot", DH, DH), wt("k2rot", 0, DH)))

        with nc.Fori(0, ITERATIONS, hint_back_edge=True) as it:
            with nc.Block() as block:
                unit = {}
                scalar_count = {}
                score_unit = {}
                trans_unit = {}

                def order(kind):
                    return [s for s in STEPS if s[0] == kind]

                for s in order("maxima"):
                    for i in range(GH):
                        score_unit[(*s[1:], i)] = len(score_unit)
                for s in order("probs"):
                    for hp in range(2):
                        trans_unit[(*s[1:], hp)] = len(trans_unit)

                def wait_evacuated(eng, *key):
                    n = unit[key]
                    eng.wait_ge(evacuated[n % NWORK], n // NWORK + 1)

                def wait_filled(eng, *key):
                    eng.wait_ge(work_full, unit[key] + 1)
                    return work_bank(unit[key])

                def empties(ins, *key):
                    ins.then_inc(evacuated[unit[key] % NWORK], 1)

                @block.tensor
                def _(pe):
                    def work(*key):
                        n = unit[key] = len(unit)
                        if n >= NWORK:
                            pe.wait_ge(evacuated[n % NWORK], n // NWORK)
                        return work_bank(n)

                    def mm(o, l, r, start=True, stop=True):
                        return pe.matmul(o, l, r, start=start, stop=stop)

                    def transpose(tag, j):
                        src, _ = TRANSPOSES[tag]
                        u = work("T", tag, j)
                        pe.wait_ge(natural[tag], j + 1)
                        for st in range(ST):
                            last = pe.transpose(u[:, st * P:(st + 1) * P], nat[src][:, j, st, :], ident[:, :])
                        last.then_inc(work_full, 1)

                    def prep8(a, j):
                        qt, kt = SOURCES[a]
                        wait_evacuated(pe, "T", qt, j)
                        wait_evacuated(pe, "T", kt, j)
                        qs, ks = (trn[TRANSPOSES[t][1]] for t in (qt, kt))
                        m = {0: "L0_1", 1: "L0_2", 4: "ca", 5: "sa"}[a]
                        for st in range(ST):
                            u = work("qkv", a, j, st)
                            mm(u[:, 0:128], qs[:, j, st * P:(st + 1) * P], wt(m, 0, 128))
                            mm(u[:, 128:384], ks[:, j, st * P:(st + 1) * P], wt(m, 128, 256)).then_inc(work_full, 1)
                        if a in (4, 5):
                            pe.wait_ge(narrow_ready, PAIR * (a - 4) + j + 1)
                        for what, view in (("tq", qe(j)), ("tk", ke(j))):
                            for st in range(ST):
                                if a in (0, 1):
                                    wait_evacuated(pe, "qkv", a, j, st)
                                u = work(what, a, j, st)
                                for g in range(GROUPS):
                                    last = pe.transpose(u[:, g * P:(g + 1) * P],
                                                        view[:, st, g, :, :].rearrange("p i c -> p (i c)"), ident[:, :])
                                last.then_inc(work_full, 1)

                    def length(a, j):
                        pe.wait_ge(blockq_ready, PAIR * a + j + 1)
                        for st in range(ST):
                            wait_evacuated(pe, "tk", a, j, st)
                        for gp in range(2):
                            u = work("len", a, j, gp)
                            for e in range(2):
                                last = mm(u[:, e * S:(e + 1) * S], blockq[:, 2 * gp + e, :], k8T(j)[:, 2 * gp + e, :])
                            last.then_inc(work_full, 1)

                    def prep64(a, j):
                        kt = SOURCES[a][1]
                        wait_evacuated(pe, "T", kt, j)
                        ks = trn[TRANSPOSES[kt][1]][:, j, :]
                        kw = {2: ["k2", "k2rot"], 3: ["k2c"], 6: None}[a]
                        if a != 6:
                            project("k", kw, ks, a, j, 0, 1)
                        for tt in range(ST):
                            l = ks[:, tt * P:(tt + 1) * P]
                            if a == 6:
                                for half in range(2):
                                    u = work("v", a, j, tt, half)
                                    mm(u[:, :], l, wt("v3", 512 * half, 512)).then_inc(work_full, 1)
                            else:
                                u = work("v", a, j, tt, 0)
                                mm(u[:, 0:DH], l, wt("fused", 1088, DH) if a == 2 else wt("wkv", DH, DH))\
                                    .then_inc(work_full, 1)

                    def project(what, names, src, a, j, c, tiles):
                        for v, name in enumerate(names):
                            u = work(what, a, j, c, v)
                            for e in range(tiles):
                                last = mm(u[:, e * S:(e + 1) * S], wt(name, (c + e) * P, P), src)
                            last.then_inc(work_full, 1)

                    def heads(a, j, g):
                        qt, kt = SOURCES[a]
                        wait_evacuated(pe, "T", qt, j)
                        qs, ks = (trn[TRANSPOSES[t][1]][:, j, :] for t in (qt, kt))
                        project("q", {2: ["fused", "rot"], 3: ["wq"], 6: ["q3"]}[a], qs, a, j, 2 * g, 2)
                        if a == 6:
                            project("k", ["k3"], ks, a, j, 2 * g, 2)

                    def maxima(a, j, g):
                        if g == 0 and NARROW[a]:
                            for st in range(ST):
                                wait_evacuated(pe, "tq", a, j, st)
                                wait_evacuated(pe, "tk", a, j, st)
                            if a < 2:
                                pe.wait_ge(length_done, PAIR * a + j + 1)
                        if not NARROW[a]:
                            wait_evacuated(pe, "q", a, j, 2 * g, 1 if a == 2 else 0)
                            wait_evacuated(pe, "k", a, j, 2 * g if a == 6 else 0, 1 if a == 2 else 0)
                        for i in range(GH):
                            n = score_unit[(a, j, g, i)]
                            if n >= NSA:
                                pe.wait_ge(maxima_done, n - NSA + 1)
                            bank = score_bank(n)
                            for st in range(ST):
                                t1 = P if CAUSAL[a] and st == 0 else S
                                if NARROW[a]:
                                    r = slice(BLK * i, BLK * i + BLK)
                                    l, m = q8T(j)[r, g, st * P:(st + 1) * P], k8T(j)[r, g, 0:t1]
                                else:
                                    r = slice(DH * (i % 2), DH * (i % 2) + DH)
                                    l = wide(a, j, g, 0)[r, i // 2, st * P:(st + 1) * P]
                                    m = wide(a, j, g, 2)[r, i // 2 if a == 6 else 0, 0:t1]
                                last = mm(bank[:, st, 0:t1], l, m, stop=not CAUSAL[a])
                                if CAUSAL[a]:
                                    last = mm(bank[:, st, t1 - P:t1], identb[:, :], causal_st[:, :], start=False)
                            last.then_inc(maxima_full, 1)

                    def probs_(a, j, g):
                        u = work("max", a, j, g)
                        pe.wait_ge(maxima_done, score_unit[(a, j, g, GH - 1)] + 1)
                        for st in range(ST):
                            src = qe(j)[:, st, g, :, :].rearrange("p i c -> p (i c)") if NARROW[a] else nmax[:, g % 2, st, :]
                            last = pe.transpose(u[:, st * P:(st + 1) * P], src, ident[:, :])
                        last.then_inc(work_full, 1)
                        wait_evacuated(pe, "max", a, j, g)
                        for hp in range(2):
                            n = trans_unit[(a, j, g, hp)]
                            if n >= NST:
                                pe.wait_ge(probs_full, n - NST + 1)
                            slot = transposed_slot(n)
                            for e in range(2):
                                i = 2 * hp + e
                                for tt in range(ST):
                                    at, s0 = span(a, tt)
                                    o = slot[:, e, at]
                                    if NARROW[a]:
                                        r = slice(BLK * i, BLK * i + BLK)
                                        last = mm(o, k8T(j)[r, g, tt * P:(tt + 1) * P], q8T(j)[r, g, s0:S], stop=not CAUSAL[a])
                                    else:
                                        r = slice(DH * e, DH * e + DH)
                                        kc = hp if a == 6 else 0
                                        qh, ql = (wide(a, j, g, m)[r, hp, s0:S] for m in (0, 1))
                                        kh, kl = (wide(a, j, g, m)[r, kc, tt * P:(tt + 1) * P] for m in (2, 3))
                                        mm(o, kh, qh, stop=False)
                                        mm(o, kh, ql, start=False, stop=False)
                                        mm(o, kl, qh, start=False, stop=False)
                                        last = mm(o, sel[0:GH, i, :], nmaxT[0:GH, g % 2, s0:S], start=False,
                                                  stop=not CAUSAL[a])
                                    if CAUSAL[a]:
                                        last = mm(slot[:, e, at.start:at.start + P], identb[:, :], causal_ts[:, :], start=False)
                            last.then_inc(scores_full, 1)

                    def values(a, j, g):
                        n0 = trans_unit[(a, j, g, 0)]
                        pe.wait_ge(probs_full, n0 + 2)
                        if NARROW[a]:
                            u = work("o", a, j, g)
                            for tt in range(ST):
                                at, s0 = span(a, tt)
                                for i in range(GH):
                                    last = mm(u[BLK * i:BLK * i + BLK, s0:S], v8(j)[:, tt, GH * g + i, :],
                                              probs[:, (n0 + i // 2) % NP, i % 2, at], start=tt == 0, stop=tt == 1)
                            last.then_inc(work_full, 1)
                            return
                        if g == 0:
                            pe.wait_ge(ones_ready, PAIR * {2: 0, 3: 1, 6: 2}[a] + j + 1)
                            for tt in range(ST):
                                for half in range(2 if a == 6 else 1):
                                    wait_evacuated(pe, "v", a, j, tt, half)
                        for st in range(ST):
                            u = work("o", a, j, g, st)
                            tiles = [0] if CAUSAL[a] and st == 0 else [0, 1]
                            for i in range(GH):
                                for tt in tiles:
                                    at, s0 = span(a, tt)
                                    c = at.start + st * P - s0
                                    last = mm(u[:, i * 65:i * 65 + 65], probs[:, (n0 + i // 2) % NP, i % 2, c:c + P],
                                              v64(a, j)[:, tt, GH * g + i if a == 6 else 0, :],
                                              start=tt == 0, stop=tt == tiles[-1])
                            last.then_inc(work_full, 1)

                    def collect(a, j, g):
                        for st in range(ST):
                            wait_evacuated(pe, "o", a, j, g, st)
                        u = work("oT", a, j, g)
                        for c in range(2):
                            for st in range(ST):
                                last = pe.transpose(u[:, (2 * c + st) * P:(2 * c + st + 1) * P],
                                                    onat[:, g % 2, st, c * P:(c + 1) * P], ident[:, :])
                        last.then_inc(work_full, 1)

                    def finish8(a, j):
                        for g in range(GROUPS):
                            wait_evacuated(pe, "o", a, j, g)
                        for st in range(ST):
                            u = work("z", a, j, st)
                            for g in range(GROUPS):
                                last = pe.transpose(u[:, g * P:(g + 1) * P], o8T(j)[:, g, st * P:(st + 1) * P], ident[:, :])
                            last.then_inc(work_full, 1)

                    def finish64(a, j):
                        for g in range(GROUPS):
                            wait_evacuated(pe, "oT", a, j, g)
                        u = work("y", a, j)
                        wo = {2: "attn_out", 3: "w_out", 6: "o3"}[a]
                        terms = [(o64T(j)[:, c, :], wt(wo, c * P, P)) for c in range(8)]
                        if a != 6:
                            pe.wait_ge(hidden_ready, PAIR * NF * (a - 2) + NF * (j + 1))
                            terms += [(hT(j)[:, f, :], wt("ff_out" if a == 2 else "w_ff2", f * P, P)) for f in range(NF)]
                        for st in range(ST):
                            for n, (l, r) in enumerate(terms):
                                last = mm(u[:, st * P:(st + 1) * P], l[:, st * P:(st + 1) * P], r,
                                          start=n == 0, stop=n == len(terms) - 1)
                        last.then_inc(work_full, 1)

                    def ffn(k, j):
                        tag = {0: "x3", 1: "x4", 2: "x7"}[k]
                        wait_evacuated(pe, "T", tag, j)
                        for f in range(NF):
                            u = work("ff", k, j, f)
                            if k == 2:
                                val, gate = wt("g_w3", f * P, P), wt("g_w1", f * P, P)
                            else:
                                name, c0 = ("fused", 1152) if k == 0 else ("w_ff1", 0)
                                val, gate = wt(name, c0 + f * P, P), wt(name, c0 + FF + f * P, P)
                            mm(u[:, 0:S], val, trn["xT"][:, j, :])
                            mm(u[:, S:2 * S], gate, trn["xT"][:, j, :]).then_inc(work_full, 1)

                    def ffn_out(k, j):
                        if k == 2:
                            pe.wait_ge(hidden_ready, PAIR * NF * 2 + NF * (j + 1))
                        else:
                            for f in range(NF):
                                wait_evacuated(pe, "h", j, f)
                        u = work("fo", k, j)
                        name = "g_w2" if k == 2 else "w2_3"
                        for st in range(ST):
                            for f in range(NF):
                                last = mm(u[:, st * P:(st + 1) * P], hT(j)[:, f, st * P:(st + 1) * P], wt(name, f * P, P),
                                          start=f == 0, stop=f == NF - 1)
                        last.then_inc(work_full, 1)

                    def gelu(j):
                        wait_evacuated(pe, "T", "x9", j)
                        for f in range(NF):
                            u = work("h", j, f)
                            mm(u[:, 0:S], wt("w1_3", f * P, P), trn["xT"][:, j, :]).then_inc(work_full, 1)

                    def fc(j):
                        wait_evacuated(pe, "T", "x2", j)
                        u = work("fc1", j)
                        mm(u[:, 0:S], wt("fc1"), trn["xT"][:, j, :]).then_inc(work_full, 1)
                        wait_evacuated(pe, "fc1", j)
                        u = work("fc2", j)
                        for st in range(ST):
                            last = mm(u[:, st * P:(st + 1) * P], hT(j)[:, 0, st * P:(st + 1) * P], wt("fc2"))
                        last.then_inc(work_full, 1)

                    def outproj(a, j):
                        wait_evacuated(pe, "T", f"z{a}", j)
                        u = work("y", a, j)
                        for st in range(ST):
                            last = mm(u[:, st * P:(st + 1) * P], trn["zT"][:, j, st * P:(st + 1) * P],
                                      wt("ca_o" if a == 4 else "sa_o"))
                        last.then_inc(work_full, 1)

                    stages = dict(transpose=transpose, prep8=prep8, length=length, prep64=prep64, heads=heads,
                                  maxima=maxima, probs=probs_, values=values, collect=collect, finish8=finish8, finish64=finish64,
                                  ffn=ffn, ffn_out=ffn_out, gelu=gelu, fc=fc, outproj=outproj)
                    for kind, *args in STEPS:
                        if kind in stages:
                            stages[kind](*args)

                @block.scalar
                def _(act):
                    done = [0]
                    group_done = {n: unit[("o", *k[:3])] if NARROW[k[0]] else unit[("o", *k[:3], ST - 1)]
                                  for k, n in trans_unit.items()}

                    def to_vector(ins, *key):
                        ins.then_inc(scalar_out, 1)
                        done[0] += 1
                        scalar_count[key] = done[0]

                    def transpose(tag, j):
                        u = wait_filled(act, "T", tag, j)
                        empties(act.activation(trn[TRANSPOSES[tag][1]][:, j, :], u[:, 0:S], ACT.Copy), "T", tag, j)

                    def prep8(a, j):
                        for st in range(ST):
                            key = ("qkv", a, j, st)
                            u = wait_filled(act, *key)
                            heads = u[:, 0:384].rearrange("p (x h d) -> p x h d", x=3, d=DS)
                            act.activation(v8(j)[:, st, :, 0:DS], heads[:, 2], ACT.Copy)
                            if a < 2:
                                for view, x, slots in ((qe(j), 0, (0, 1)), (ke(j), 1, (0, 2))):
                                    hp = head_parts(view, st)
                                    o = hp[:, :, slots[0]:slots[1] + 1:slots[1] - slots[0], :]
                                    last = act.activation(o.bitcast(F32R), heads[:, x].unsqueeze(2).broadcast_to([P, H, 2, DS]), ACT.Copy)
                                to_vector(last, *key)
                            else:
                                empties(act.activation(qk_nat(j, 0)[:, st, :], u[:, 0:256], ACT.Copy), *key)
                        for what, dst in (("tq", q8T(j)), ("tk", k8T(j))):
                            for st in range(ST):
                                u = wait_filled(act, what, a, j, st)
                                empties(act.activation(dst[:, :, st * P:(st + 1) * P],
                                                       u.rearrange("p (g s) -> p g s", g=GROUPS), ACT.Copy), what, a, j, st)

                    def prep64(a, j):
                        if a == 3:
                            hi_part("k", a, j, 0, 1)
                        for tt in range(ST):
                            for half in range(2 if a == 6 else 1):
                                u = wait_filled(act, "v", a, j, tt, half)
                                k = 8 if a == 6 else 1
                                empties(act.activation(v64(a, j)[:, tt, 8 * half:8 * half + k, 0:DH],
                                                       u[:, 0:k * DH].rearrange("p (h d) -> p h d", d=DH), ACT.Copy),
                                        "v", a, j, tt, half)

                    def hi_part(what, a, j, g, k):
                        u = wait_filled(act, what, a, j, 2 * g, 0)
                        to_vector(act.activation(wide(a, j, g, 0 if what == "q" else 2),
                                                 u[:, 0:k * S].rearrange("p (c s) -> p c s", c=k), ACT.Copy),
                                  what, a, j, 2 * g)

                    def heads(a, j, g):
                        if a != 2:
                            hi_part("q", a, j, g, 2)
                        if a == 6:
                            hi_part("k", a, j, g, 2)

                    def probs_(a, j, g):
                        for hp in range(2):
                            n = trans_unit[(a, j, g, hp)]
                            act.wait_ge(scores_full, n + 1)
                            if n >= NP:
                                act.wait_ge(work_full, group_done[n - NP] + 1)
                            c = span(a, 1)[0].stop
                            act.activation(probs[:, n % NP, :, 0:c], transposed_slot(n)[:, :, 0:c], ACT.Exp,
                                           scale=float(SCALE[a])).then_inc(probs_full, 1)

                    def values(a, j, g):
                        if NARROW[a]:
                            u = wait_filled(act, "o", a, j, g)
                            empties(act.activation(o8T(j)[:, g, :], u[:, 0:S], ACT.Copy), "o", a, j, g)

                    def collect(a, j, g):
                        u = wait_filled(act, "oT", a, j, g)
                        empties(act.activation(o64T(j)[:, 2 * g:2 * g + 2, :],
                                               u.rearrange("p (c s) -> p c s", c=2), ACT.Copy), "oT", a, j, g)

                    def ffn(k, j):
                        for f in range(NF):
                            u = wait_filled(act, "ff", k, j, f)
                            to_vector(act.activation(hT(j)[:, f, :], u[:, S:2 * S], ACT.Exp, scale=-1.0), "ff", k, j, f)

                    def gelu(j):
                        for f in range(NF):
                            u = wait_filled(act, "h", j, f)
                            empties(act.activation(hT(j)[:, f, :], u[:, 0:S], ACT.Gelu, bias=cols[:, 8 + f:9 + f]), "h", j, f)

                    def fc(j):
                        u = wait_filled(act, "fc1", j)
                        empties(act.activation(hT(j)[:, 0, :], u[:, 0:S], ACT.Relu, bias=cols[:, 6:7]), "fc1", j)

                    stages = dict(transpose=transpose, prep8=prep8, prep64=prep64, heads=heads, probs=probs_, values=values,
                                  collect=collect, ffn=ffn, gelu=gelu, fc=fc)
                    for kind, *args in STEPS:
                        if kind in stages:
                            stages[kind](*args)

                @block.vector
                def _(dve):
                    chain = [0]

                    def link(ins):
                        ins.then_inc(vector_step, 1)
                        chain[0] += 1
                        dve.wait_ge(vector_step, chain[0])

                    def signal(ins, s, value):
                        ins.then_inc(s, 1)
                        dve.wait_ge(s, value)

                    asked = [0]

                    def inverse_root(ins):
                        ins.then_inc(root_asked, 1)
                        asked[0] += 1
                        dve.wait_ge(root_done, asked[0])

                    def row(n):
                        return rows[:, n, :].unsqueeze(1).broadcast_to([P, ST, D])

                    def statistics(j, src, eps, mean):
                        sm = small[:, j, :]
                        if mean:
                            for st in range(ST):
                                link(dve.bn_stats(sm[:, 8 + 6 * st:14 + 6 * st], src[:, j, st, :]))
                            for st in range(ST):
                                link(dve.bn_aggr(sm[:, 4 + 2 * st:6 + 2 * st], sm[:, 8 + 6 * st:14 + 6 * st]))
                            mv = sm[:, 4:8].rearrange("p (s c) -> p s c", c=2)
                            link(dve.tensor_copy(sm[:, 0:2], mv[:, :, 0]))
                            inverse_root(dve.tensor_scalar(sm[:, 2:4], mv[:, :, 1], eps, None, ALU.add))
                        else:
                            sq = tmp[:, j, 0:S].rearrange("p (s d) -> p s d", s=ST)
                            link(dve.tensor_tensor(sq, src[:, j], src[:, j], ALU.mult))
                            link(dve.tensor_reduce(sm[:, 4:6], sq, axis=AX, op=ALU.add))
                            inverse_root(dve.tensor_scalar(sm[:, 2:4], sm[:, 4:6], 1.0 / D, eps, ALU.mult, ALU.add))

                    def normed(j, src, dst, mean=True, eps=EPS_LN):
                        statistics(j, src, eps, mean)
                        sm = small[:, j, :]
                        for st in range(ST):
                            if mean:
                                last = dve.tensor_scalar(dst[:, j, st, :], src[:, j, st, :], sm[:, st:st + 1],
                                                         sm[:, 2 + st:3 + st], ALU.subtract, ALU.mult)
                            else:
                                last = dve.tensor_scalar(dst[:, j, st, :], src[:, j, st, :], sm[:, 2 + st:3 + st], None, ALU.mult)
                            if st == 0:
                                link(last)
                        return last

                    def start(j):
                        if j == 0:
                            dve.wait_ge(tokens_in, 32)
                            link(dve.tensor_copy(cs[:, :, :, :].rearrange("p t c d -> p (t c d)").unsqueeze(1),
                                                 cs_all[:, bass.ds(it, 1), :]))
                        token_mask(j, nat["x"], 24)
                        signal(dve.tensor_copy(small[:, j, 30:31], small[:, j, 24:25]), natural["x0"], j + 1)
                        dve.tensor_copy(small[:, j, 31:32], small[:, j, 24:25]).then_inc(natural["craw"], 1)

                    def token_mask(j, src, at):
                        sm = small[:, j, :]
                        link(dve.tensor_reduce(sm[:, at + 2:at + 4], src[:, j], axis=AX, op=ALU.max, apply_absolute_value=True))
                        link(dve.tensor_scalar(sm[:, at:at + 2], sm[:, at + 2:at + 4], 0.0, None, ALU.not_equal))

                    def pads(j):
                        q_, k_ = (view.rearrange("p s g i c -> p (s g i) c")[:, :, 24:32] for view in (qe(j), ke(j)))
                        dve.tensor_copy(q_, consts[:, 8:16].unsqueeze(1).broadcast_to([P, 32, 8]))
                        dve.tensor_copy(k_, consts[:, 16:24].unsqueeze(1).broadcast_to([P, 32, 8]))
                        link(dve.tensor_copy(v8(j).rearrange("p t h c -> p (t h) c")[:, :, 8:32],
                                        consts[:, 24:48].unsqueeze(1).broadcast_to([P, 32, 24])))

                    def prep8(a, j):
                        pads(j)
                        if a < 2:
                            for st in range(ST):
                                key = ("qkv", a, j, st)
                                wait_filled(dve, *key)
                                u = work_bank(unit[key])
                                dve.wait_ge(scalar_out, scalar_count[key])
                                heads = u[:, 0:256].rearrange("p (x h d) -> p x h d", x=2, d=DS)
                                for view, x, lo in ((qe(j), 0, 2), (ke(j), 1, 1)):
                                    hp = head_parts(view, st)
                                    last = dve.tensor_tensor(hp[:, :, lo, :].bitcast(F32R), heads[:, x], hp[:, :, 0, :], ALU.subtract)
                                empties(last, *key)
                            return
                        for st in range(ST):
                            wait_evacuated(dve, "qkv", a, j, st)
                        X, Y = qk_nat(j, 0), qk_nat(j, 1)
                        Z = tmp[:, j, 0:512].rearrange("p (s e) -> p s e", s=ST)
                        X3, Y3 = (v.rearrange("p s (n d) -> p (s n) d", d=DS) for v in (X, Y))
                        ms = small[:, j, 64:128]
                        link(dve.tensor_tensor(Y, X, X, ALU.mult))
                        link(dve.tensor_reduce(ms, Y3, axis=AX, op=ALU.add))
                        inverse_root(dve.tensor_scalar(ms, ms, 1.0 / DS, EPS_RMS, ALU.mult, ALU.add))
                        link(dve.tensor_tensor(X3, X3, ms.unsqueeze(2).broadcast_to([P, 64, DS]), ALU.mult))
                        for x in range(2):
                            v = X[:, :, 128 * x:128 * x + 128].rearrange("p s (n d) -> p s n d", d=DS)
                            g_ = qkw[:, 2 * (a - 4) + x, :].unsqueeze(1).unsqueeze(1).broadcast_to([P, ST, H, DS])
                            link(dve.tensor_tensor(v, v, g_, ALU.mult))
                        for st in range(ST):
                            x3, y3, z3 = (v[:, st, :].rearrange("p (n d) -> p n d", d=DS) for v in (X, Y, Z))
                            c_, s_ = (cs[:, ST * j + st, m, :].unsqueeze(1).broadcast_to([P, 32, DS]) for m in (0, 1))
                            dve.tensor_tensor(y3, x3, c_, ALU.mult)
                            dve.tensor_tensor(z3[:, :, 0:4], x3[:, :, 4:8], s_[:, :, 0:4], ALU.mult)
                            link(dve.tensor_tensor(z3[:, :, 4:8], x3[:, :, 0:4], s_[:, :, 4:8], ALU.mult))
                        link(dve.tensor_tensor(X, Y, Z, ALU.add))
                        for st in range(ST):
                            for view, x, slots, lo in ((qe(j), 0, (0, 1), 2), (ke(j), 1, (0, 2), 1)):
                                hp = head_parts(view, st)
                                src = X[:, st, 128 * x:128 * x + 128].rearrange("p (h d) -> p h d", d=DS)
                                o = hp[:, :, slots[0]:slots[1] + 1:slots[1] - slots[0], :]
                                link(dve.tensor_copy(o.bitcast(F32R), src.unsqueeze(2).broadcast_to([P, H, 2, DS])))
                                last = dve.tensor_tensor(hp[:, :, lo, :].bitcast(F32R), src, hp[:, :, 0, :], ALU.subtract)
                        signal(last, narrow_ready, PAIR * (a - 4) + j + 1)

                    def length(a, j):
                        wait_evacuated(dve, "tq", a, j, 0)
                        if (a, j) != (0, 0):
                            pa, pj = (a, j - 1) if j else (a - 1, 1)
                            wait_filled(dve, "len", pa, pj, 1)
                        cols25 = blockq[:, :, :].rearrange("p g (i c) -> p g i c", i=GH)[:, :, :, COL_LEN]
                        first = q8T(j)[:, :, 0:1].bitcast(F32).broadcast_to([P, GROUPS, GH])
                        signal(dve.tensor_tensor(cols25, first, consts[:, 0:4].unsqueeze(1).broadcast_to([P, GROUPS, GH]), ALU.mult),
                               blockq_ready, PAIR * a + j + 1)
                        ln = small[:, j, 32:36]
                        for gp in range(2):
                            u = wait_filled(dve, "len", a, j, gp)
                            t = tmp[:, j, 0:512]
                            signal(dve.tensor_scalar(t, u, 0.0, None, ALU.not_equal),
                                   evacuated[unit[("len", a, j, gp)] % NWORK], unit[("len", a, j, gp)] // NWORK + 1)
                            link(dve.tensor_reduce(ln[:, 2 * gp:2 * gp + 2], t.rearrange("p (e t) -> p e t", e=2), axis=AX, op=ALU.add))
                        lm = tmp[:, j, :].rearrange("p (g t) -> p g t", g=GROUPS)
                        for g in range(GROUPS):
                            link(dve.tensor_scalar(lm[:, g, :], iota[:, :], ln[:, g:g + 1], consts[:, 4:5], ALU.is_ge, ALU.mult))
                        signal(dve.tensor_tensor(k8T(j), k8T(j).bitcast(F32), lm, ALU.add), length_done, PAIR * a + j + 1)

                    def prep64(a, j):
                        ones = v64(a, j)[:, :, :, DH:DH + 1].rearrange("p t h c -> p (t h) c")
                        n = ones.shape[1]
                        signal(dve.tensor_copy(ones, consts[:, 24:25].unsqueeze(1).broadcast_to([P, n, 1])),
                               ones_ready, PAIR * {2: 0, 3: 1, 6: 2}[a] + j + 1)
                        if a != 6:
                            split("k", a, j, 0, 1)

                    def heads(a, j, g):
                        split("q", a, j, g, 2)
                        if a == 6:
                            split("k", a, j, g, 2)

                    def split(what, a, j, g, k):
                        m, c = (0 if what == "q" else 2), 2 * g
                        hi, lo = wide(a, j, g, m), wide(a, j, g, m + 1)
                        if a != 2:
                            key = (what, a, j, c, 0)
                            u = wait_filled(dve, *key)[:, 0:k * S].rearrange("p (c s) -> p c s", c=k)
                            dve.wait_ge(scalar_out, scalar_count[(what, a, j, c)])
                            empties(dve.tensor_tensor(lo, u, hi.bitcast(F32), ALU.subtract), *key)
                            return
                        t = [tmp[:, j, 512 * v:512 * v + k * S].rearrange("p (c s) -> p c s", c=k) for v in range(2)]
                        for v, table in enumerate((rope_cos, rope_sin)):
                            u = wait_filled(dve, what, a, j, c, v)[:, 0:k * S].rearrange("p (c s) -> p c s", c=k)
                            n = unit[(what, a, j, c, v)]
                            ins = dve.tensor_tensor(t[v], u, table[:, :].unsqueeze(1).broadcast_to([P, k, S]), ALU.mult)
                            if v == 0:
                                signal(ins, evacuated[n % NWORK], n // NWORK + 1)
                            else:
                                link(ins)
                        link(dve.tensor_tensor(t[0], t[0], t[1], ALU.add))
                        link(dve.tensor_copy(hi, t[0]))
                        signal(dve.tensor_tensor(lo, t[0], hi.bitcast(F32), ALU.subtract), evacuated[n % NWORK], n // NWORK + 1)

                    def maxima(a, j, g):
                        for i in range(GH):
                            n = score_unit[(a, j, g, i)]
                            dve.wait_ge(maxima_full, n + 1)
                            o = qe(j)[:, :, g, i, COL_MAX] if NARROW[a] else nmax[:, g % 2, :, i]
                            bank = score_bank(n)
                            if CAUSAL[a]:
                                dve.tensor_reduce(o[:, 0:1], bank[:, 0, 0:P], axis=AX, op=ALU.max, negate=True)
                                dve.tensor_reduce(o[:, 1:2], bank[:, 1, :], axis=AX, op=ALU.max, negate=True)\
                                    .then_inc(maxima_done, 1)
                            else:
                                dve.tensor_reduce(o, bank, axis=AX, op=ALU.max, negate=True).then_inc(maxima_done, 1)

                    def probs_(a, j, g):
                        u = wait_filled(dve, "max", a, j, g)
                        if NARROW[a]:
                            empties(dve.tensor_scalar(q8T(j)[:, g, :], u[:, 0:S], MAX_GUARD, None, ALU.min), "max", a, j, g)
                        else:
                            empties(dve.tensor_scalar(nmaxT[0:GH, g % 2, :], u[0:GH, 0:S], MAX_GUARD, None, ALU.min), "max", a, j, g)

                    def values(a, j, g):
                        if NARROW[a]:
                            return
                        for st in range(ST):
                            u = wait_filled(dve, "o", a, j, g, st)[:, 0:GH * 65].rearrange("p (h c) -> p h c", h=GH)
                            rec = small[:, j, 40 + 4 * st:44 + 4 * st]
                            link(dve.reciprocal(rec, u[:, :, DH]))
                            empties(dve.tensor_tensor(onat[:, g % 2, st, :].rearrange("p (h d) -> p h d", h=GH), u[:, :, 0:DH],
                                                      rec.unsqueeze(2).broadcast_to([P, GH, DH]), ALU.mult), "o", a, j, g, st)

                    def finish8(a, j):
                        for st in range(ST):
                            u = wait_filled(dve, "z", a, j, st).rearrange("p (h c) -> p h c", h=H)
                            rec = small[:, j, 128 + 16 * st:144 + 16 * st]
                            link(dve.reciprocal(rec, u[:, :, DS]))
                            if a < 2:
                                m = (24 if a == 0 else 56) + st
                                link(dve.tensor_scalar(rec, rec, small[:, j, m:m + 1], None, ALU.mult))
                            n = unit[("z", a, j, st)]
                            signal(dve.tensor_tensor(nat["z"][:, j, st, :].rearrange("p (h d) -> p h d", h=H), u[:, :, 0:DS],
                                                     rec.unsqueeze(2).broadcast_to([P, H, DS]), ALU.mult),
                                   evacuated[n % NWORK], n // NWORK + 1)
                        if a in (4, 5):
                            dve.tensor_copy(small[:, j, 30:31], small[:, j, 24:25]).then_inc(natural[f"z{a}"], 1)

                    def add_unit(j, *key):
                        u = wait_filled(dve, *key)[:, 0:S].rearrange("p (s d) -> p s d", s=ST)
                        n = unit[key]
                        signal(dve.tensor_tensor(nat["x"][:, j], nat["x"][:, j], u, ALU.add), evacuated[n % NWORK], n // NWORK + 1)

                    def norm_l0a(j):
                        link(dve.tensor_tensor(nat["z"][:, j], nat["z"][:, j], nat["x"][:, j], ALU.add))
                        link(normed(j, nat["z"], nat["y"]))
                        link(dve.tensor_tensor(nat["y"][:, j], nat["y"][:, j], row(0), ALU.mult))
                        signal(dve.tensor_tensor(nat["y"][:, j], nat["y"][:, j], row(1), ALU.add), natural["x1"], j + 1)
                        token_mask(j, nat["y"], 56)
                        for st in range(ST):
                            last = dve.tensor_scalar(nat["cm"][:, j, st, :], nat["cx"][:, j, st, :], small[:, j, 56 + st:57 + st], None, ALU.mult)
                        last.then_inc(natural["cm"], 1)

                    def norm_l0b(j):
                        link(dve.tensor_tensor(nat["z"][:, j], nat["z"][:, j], nat["y"][:, j], ALU.add))
                        link(normed(j, nat["z"], nat["x"]))
                        link(dve.tensor_tensor(nat["x"][:, j], nat["x"][:, j], row(2), ALU.mult))
                        signal(dve.tensor_tensor(nat["x"][:, j], nat["x"][:, j], row(3), ALU.add), natural["x2"], j + 1)

                    def norm_l0c(j):
                        u = wait_filled(dve, "fc2", j)[:, 0:S].rearrange("p (s d) -> p s d", s=ST)
                        n = unit[("fc2", j)]
                        signal(dve.tensor_tensor(nat["z"][:, j], u, row(6), ALU.add), evacuated[n % NWORK], n // NWORK + 1)
                        for st in range(ST):
                            link(dve.scalar_tensor_tensor(nat["z"][:, j, st, :], nat["z"][:, j, st, :], small[:, j, 24 + st:25 + st],
                                                          nat["x"][:, j, st, :], ALU.mult, ALU.add))
                        link(normed(j, nat["z"], nat["x"]))
                        link(dve.tensor_tensor(nat["x"][:, j], nat["x"][:, j], row(4), ALU.mult))
                        link(dve.tensor_tensor(nat["x"][:, j], nat["x"][:, j], row(5), ALU.add))
                        signal(normed(j, nat["x"], nat["y"]), natural["x3"], j + 1)
                        signal(normed(j, nat["cx"], nat["cm"]), natural["cn"], j + 1)

                    def norm_l1(j):
                        signal(normed(j, nat["x"], nat["y"]), natural["x4"], j + 1)

                    def rms_(tag, j):
                        signal(normed(j, nat["x"], nat["y"], mean=False, eps=EPS_RMS), natural[tag], j + 1)

                    def ffn(k, j):
                        for f in range(NF):
                            u = wait_filled(dve, "ff", k, j, f)
                            dve.wait_ge(scalar_out, scalar_count[("ff", k, j, f)])
                            h = hT(j)[:, f, :]
                            link(dve.tensor_scalar(h, h, 1.0, None, ALU.add))
                            link(dve.reciprocal(h, h))
                            link(dve.tensor_tensor(h, h, u[:, S:2 * S], ALU.mult))
                            n = unit[("ff", k, j, f)]
                            signal(dve.tensor_tensor(h, h, u[:, 0:S], ALU.mult), evacuated[n % NWORK], n // NWORK + 1)
                            dve.tensor_copy(small[:, j, 30:31], small[:, j, 24:25]).then_inc(hidden_ready, 1)

                    def copy_l3(j):
                        add_unit(j, "fo", 2, j)
                        dve.tensor_copy(small[:, j, 30:31], small[:, j, 24:25]).then_inc(natural["x8"], 1)

                    def bias_l3(j):
                        signal(dve.tensor_tensor(nat["x"][:, j], nat["x"][:, j], row(7), ALU.add), natural["x9"], j + 1)

                    def store(j):
                        add_unit(j, "fo", 3, j)
                        dve.tensor_tensor(nat["y"][:, j], nat["x"][:, j], row(8), ALU.add).then_inc(result_ready, 1)

                    stages = dict(start=start, prep8=prep8, length=length, prep64=prep64, heads=heads, maxima=maxima, probs=probs_,
                                  values=values, finish8=finish8, ffn=ffn,
                                  finish64=lambda a, j: add_unit(j, "y", a, j),
                                  outproj=lambda a, j: add_unit(j, "y", a, j),
                                  norm_l0a=norm_l0a, norm_l0b=norm_l0b, norm_l0c=norm_l0c, norm_l1=norm_l1,
                                  rms_a=lambda j: rms_("x5", j), rms_b=lambda j: rms_("x6", j), rms_c=lambda j: rms_("x7", j),
                                  copy_l3=copy_l3, bias_l3=bias_l3, store=store)
                    for kind, *args in STEPS:
                        if kind in stages:
                            stages[kind](*args)

                @block.gpsimd
                def _(pool):
                    asked = [0]

                    def inverse_root(view):
                        asked[0] += 1
                        pool.wait_ge(root_asked, asked[0])
                        pool.tensor_tensor(view, view, consts[:, 52:53].broadcast_to(list(view.shape)), ALU.pow)\
                            .then_inc(root_done, 1)

                    norms = dict(norm_l0a=1, norm_l0b=1, norm_l0c=3, norm_l1=1, rms_a=1, rms_b=1, rms_c=1)
                    for kind, *args in STEPS:
                        if kind in norms:
                            for _ in range(norms[kind]):
                                inverse_root(small[:, args[-1], 2:4])
                        if kind == "prep8" and args[0] in (4, 5):
                            inverse_root(small[:, args[1], 64:128])

                @block.sync
                def _(sp):
                    def rows_of(t):
                        return t.rearrange("(i j) (s p) d -> i p (j s) d", j=PAIR, p=P)[bass.ds(it, 1)].rearrange("o p a d -> (o p) a d")
                    for k, src in (("x", w["x"]), ("cx", w["ctx"])):
                        sp.dma_start(nat[k][:, :, :, :].rearrange("p j s d -> p (j s) d"), rows_of(src)).then_inc(tokens_in, 16)
                    sp.wait_ge(result_ready, PAIR)
                    sp.dma_start(rows_of(out), nat["y"][:, :, :, :].rearrange("p j s d -> p (j s) d")).then_inc(stored, 16)
                    sp.wait_ge(stored, 16)

            names = [s for s in list(sems.values())[loop_first:]]
            nums = sorted(s.num for s in names)
            assert nums == list(range(nums[0], nums[-1] + 1))
            nc.gpsimd.sem_clear(range(nums[0], nums[-1] + 1))
            nc.all_engine_barrier()


def _tables():
    p, f = np.arange(P), np.float32
    ident = np.eye(P, dtype=f)
    causal = np.where(p[None, :] > p[:, None], f(NEG), f(0)).astype(f)
    inv = (1.0 / f(10000.0) ** (np.arange(0, DH, 2, dtype=f) / f(DH))).astype(f)
    ang = np.arange(S, dtype=f)[:, None] * inv[None, :]
    ang = np.concatenate([ang] * 4, axis=1).T
    consts = np.zeros((P, 128), f)
    for i in range(GH):
        consts[BLK * i:BLK * i + 3 * DS, i] = 1.0
        consts[BLK * i + COL_LEN, 4] = NEG
    consts[:, 8 + COL_LEN - 24] = 1.0
    consts[:, 16 + COL_MAX - 24] = 1.0
    consts[:, 24] = 1.0
    consts[:, 48:52] = 1.0 / f(10000.0) ** (np.arange(0, DS, 2, dtype=f) / f(DS))
    consts[:, 52] = -0.5
    sel = np.zeros((P, GH, P), f)
    for i in range(GH):
        sel[i, i, :] = 1.0
    return {"ident": ident, "causal": causal, "causal_t": np.ascontiguousarray(causal.T), "iota": np.arange(S, dtype=f),
            "rope_cos": np.cos(ang.astype(np.float64)).astype(f), "rope_sin": np.sin(ang.astype(np.float64)).astype(f),
            "consts": consts, "sel": sel.reshape(P, GH * P)}


def kernel(**inputs):
    import concourse.bacc as bacc
    from concourse.bass_utils import run_bass_kernel_spmd

    nc = bacc.Bacc("TRN2", target_bir_lowering=False, num_devices=1)
    arrays = {}

    def dram(name, a):
        a = np.ascontiguousarray(a)
        arrays[name] = a
        return nc.dram_tensor(name, a.shape, mybir.dt.from_np(a.dtype), kind="ExternalInput").ap()

    i = {k: np.asarray(v) for k, v in inputs.items()}
    w = {"x": dram("x_in", i["x"]), "ctx": dram("ctx_in", i["ctx_1024"]), "pos": dram("pos_in", i["pos_BxS2"].reshape(B * ST, P).T)}
    for k, v in _tables().items():
        w[k] = dram(f"table_{k}", v)

    def heads_in(name):
        return dram(name, i[name].transpose(1, 0, 2).reshape(D, D))

    def plain(name):
        return dram(name, i[name])

    def tiled(name):
        return plain(name).rearrange("(t p) n -> p t n", p=P)

    w["matrices"] = (
        [(f"L0_{c}:{128 * n}:128", heads_in(f"L0_xattn_W{x}{c}")) for c in (1, 2) for n, x in enumerate("qkv")]
        + [("fc1:0:128", dram("fc1_wT", i["L0_xattn_fc1_w"].T)), ("fc2:0:128", dram("fc2_wT", i["L0_xattn_fc2_w"].T)),
           ("fused:0:2176", plain("L1_xattn_w_fused")), ("attn_out:0:1024", tiled("L1_xattn_w_attn_out")),
           ("ff_out:0:512", tiled("L1_xattn_w_ff_out")), ("wq:0:1024", plain("L1_xattn_w_q")),
           ("wkv:0:128", plain("L1_xattn_w_kv")), ("w_out:0:1024", tiled("L1_xattn_w_out")),
           ("w_ff1:0:1024", plain("L1_xattn_w_ff1")), ("w_ff2:0:512", tiled("L1_xattn_w_ff2")),
           ("ca:0:128", plain("L2_xattn_ca_Wq")), ("ca:128:256", plain("L2_xattn_ca_Wkv")), ("ca_o:0:128", plain("L2_xattn_ca_Wo")),
           ("sa:0:128", plain("L2_xattn_sa_Wq")), ("sa:128:256", plain("L2_xattn_sa_Wkv")), ("sa_o:0:128", plain("L2_xattn_sa_Wo")),
           ("g_w1:0:512", plain("L2_xattn_W1")), ("g_w3:0:512", plain("L2_xattn_W3")), ("g_w2:0:512", tiled("L2_xattn_W2")),
           ("q3:0:1024", plain("L3_xattn_Wq")), ("k3:0:1024", plain("L3_xattn_Wk")), ("v3:0:1024", plain("L3_xattn_Wv")),
           ("o3:0:1024", tiled("L3_xattn_Wo")), ("w1_3:0:512", plain("L3_xattn_W1")), ("w2_3:0:512", tiled("L3_xattn_W2"))])
    for k in ("ln1_g", "ln1_b", "ln2_g", "ln2_b", "ln3_g", "ln3_b", "fc1_b", "fc2_b"):
        w[k] = plain(f"L0_xattn_{k}")
    for k in ("gamma_pt", "gamma_ca", "gamma_ctx"):
        w[k] = plain(f"L1_xattn_{k}")
    for k in ("ca_qn", "ca_kn", "sa_qn", "sa_kn", "pre_ca_w", "pre_sa_w", "pre_ffn_w"):
        w[k] = plain(f"L2_xattn_{k}")
    for k in ("bo", "b2"):
        w[k] = plain(f"L3_xattn_{k}")
    w["b1"] = dram("b1_columns", i["L3_xattn_b1"].reshape(NF, P).T)

    out = nc.dram_tensor("out", (B, S, D), F32, kind="ExternalOutput").ap()
    build_program(nc, w, out)
    r = run_bass_kernel_spmd(nc, [arrays], core_ids=[0])
    return r.results[0]["out"]
```

```python
from contextlib import ExitStack

import numpy as np

import concourse.bass as bass
from concourse import mybir

F32 = mybir.dt.float32
F32R = mybir.dt.float32r
BF16 = mybir.dt.bfloat16
I32 = mybir.dt.int32
ALU = mybir.AluOpType
ACT = mybir.ActivationFunctionType
AX = mybir.AxisListType.X

P = 128
B, S, D, H = 8, 256, 128, 16
PAIR = 2
ITERATIONS = B // PAIR
ST = S // P
DH = 64
DS = D // H
FF = 512
NF = FF // P
GROUPS, GH = 4, 4
BLK = 32
COL_MAX, COL_LEN = 24, 25
NEG = -1.0e30
MAX_GUARD = 1.0e29
EPS_LN, EPS_RMS = 1e-5, 1e-6
NWORK, NSA, NST, NP, NR = 2, 2, 2, 4, 2
TWO_PI = 2.0 * np.pi
ROUND = 12582912.0

NARROW = [True, True, False, False, True, True, False]
CAUSAL = [True, False, True, False, False, False, False]
SCALE = [DS ** -0.5 if n else DH ** -0.5 for n in NARROW]

W_COLS = {}


def _plan_weights():
    at = 0
    for name, cols in [("L0_1", 384), ("L0_2", 384), ("fc1", 128), ("fc2", 128),
                       ("fused", 2176), ("attn_out", 1024), ("ff_out", 512), ("wq", 1024), ("wkv", 128),
                       ("w_out", 1024), ("w_ff1", 1024), ("w_ff2", 512), ("rot", 1024),
                       ("k2", 128), ("k2rot", 128), ("k2c", 128),
                       ("ca", 384), ("ca_o", 128), ("sa", 384), ("sa_o", 128),
                       ("g_w1", 512), ("g_w3", 512), ("g_w2", 512),
                       ("q3", 1024), ("k3", 1024), ("v3", 1024), ("o3", 1024), ("w1_3", 512), ("w2_3", 512)]:
        W_COLS[name] = (at, cols)
        at += cols
    return at


W_TOTAL = _plan_weights()


def schedule():
    steps = []

    def both(*step):
        for j in range(PAIR):
            steps.append((step[0], *step[1:], j))

    def attention(a):
        groups = [(a, j, g) for j in range(PAIR) for g in range(GROUPS)]
        steps.append(("heads", *groups[0]))
        for i in range(len(groups) + 2):
            if 1 <= i <= len(groups):
                steps.append(("turn_maxima", *groups[i - 1]))
            for hp in range(2):
                if i < len(groups):
                    steps.append(("maxima", *groups[i], hp))
                if 1 <= i <= len(groups):
                    steps.append(("probs", *groups[i - 1], hp))
            if i + 1 < len(groups):
                steps.append(("heads", *groups[i + 1]))
            if 1 <= i <= len(groups):
                steps.append(("values", *groups[i - 1]))
            if i >= 2 and not NARROW[a]:
                steps.append(("collect", *groups[i - 2]))
        both("finish8" if NARROW[a] else "finish64", a)

    both("start")
    both("transpose", "x0")
    both("transpose", "craw")
    both("prep8", 0)
    both("length", 0)
    attention(0)
    both("norm_l0a")
    both("transpose", "x1")
    both("transpose", "cm")
    both("prep8", 1)
    both("length", 1)
    attention(1)
    both("norm_l0b")
    both("transpose", "x2")
    both("fc")
    both("norm_l0c")
    both("transpose", "x3")
    both("transpose", "cn")
    both("prep64", 2)
    both("ffn", 0)
    attention(2)
    both("norm_l1")
    both("transpose", "x4")
    both("prep64", 3)
    both("ffn", 1)
    attention(3)
    both("rms_a")
    both("transpose", "x5")
    both("prep8", 4)
    attention(4)
    both("transpose", "z4")
    both("outproj", 4)
    both("rms_b")
    both("transpose", "x6")
    both("prep8", 5)
    attention(5)
    both("transpose", "z5")
    both("outproj", 5)
    both("rms_c")
    both("transpose", "x7")
    both("ffn", 2)
    both("ffn_out", 2)
    both("copy_l3")
    both("transpose", "x8")
    both("prep64", 6)
    attention(6)
    both("bias_l3")
    both("transpose", "x9")
    both("gelu")
    both("ffn_out", 3)
    both("store")
    return steps


TRANSPOSES = {"x0": ("x", "xT"), "craw": ("cx", "crT"), "x1": ("y", "xT"), "cm": ("z", "cT"), "x2": ("x", "xT"),
              "x3": ("y", "xT"), "cn": ("z", "cT"), "x4": ("y", "xT"), "x5": ("y", "xT"), "z4": ("z", "cT"),
              "x6": ("y", "xT"), "z5": ("z", "cT"), "x7": ("y", "xT"), "x8": ("x", "xT"), "x9": ("x", "xT")}
SOURCES = {0: ("x0", "x0"), 1: ("x1", "cm"), 2: ("x3", "x3"), 3: ("x4", "cn"), 4: ("x5", "craw"), 5: ("x6", "x6"),
           6: ("x8", "craw")}


def build_program(nc, w, out):
    STEPS = schedule()
    ctx = ExitStack()
    with ctx:
        def sb(name, shape, dt=F32):
            return ctx.enter_context(nc.sbuf_tensor(name, shape, dt))

        sems = {}

        def sem(name):
            if name not in sems:
                sems[name] = ctx.enter_context(nc.semaphore(name))
            return sems[name]

        W = sb("weights", [P, W_TOTAL])
        ident = sb("ident", [P, P])
        identb = sb("identb", [P, P], BF16)
        causal_st = sb("causal_st", [P, P], BF16)
        causal_ts = sb("causal_ts", [P, P], BF16)
        rope_cos = sb("rope_cos", [P, S])
        rope_sin = sb("rope_sin", [P, S])
        iota = sb("iota", [P, S])
        sel = sb("sel", [P, GH, P], F32R)
        consts = sb("consts", [P, 128])
        rows = sb("rows", [P, 11, D])
        qkw = sb("qkw", [P, 4, DS])
        cols = sb("cols", [P, 12])
        cs_all = sb("cs_all", [P, ITERATIONS, PAIR * ST * 16])
        cs = sb("cs", [P, PAIR * ST, 2, DS])
        setup = sb("setup", [P, 6, 64])
        pos = sb("pos", [P, B * ST], I32)

        nat = {k: sb(f"nat_{k}", [P, PAIR, ST, D]) for k in ("x", "y", "z", "cx")}
        trn = {k: sb(f"trn_{k}", [P, PAIR, S]) for k in ("xT", "cT", "crT")}
        arena = sb("arena", [P, PAIR, 4128])
        tmp = sb("tmp", [P, 1024])
        stacked = sb("stacked", [P, 2, 2, 1024], F32R)
        own_keys = sb("own_keys", [P, NR, GH, S], F32R)
        lo_keys = sb("lo_keys", [P, NR, GH, S], F32R)
        shared_k = sb("shared_k", [P, PAIR, 3, S], F32R)
        small = sb("small", [P, PAIR, 192])
        blockq = sb("blockq", [P, GROUPS, P], F32R)
        nmax = sb("nmax", [P, 2, ST, P])
        nmaxT = sb("nmaxT", [P, 2, S], F32R)
        onat = sb("onat", [P, 2, ST, GH * DH])
        probs = sb("probs", [P, NP, 2, ST * S])

        psum = ctx.enter_context(nc.psum_tensor("psum", [P, 4096], F32))

        def score_bank(n):
            return psum[:, 512 * (n % NSA):512 * (n % NSA) + 512].rearrange("p (s t) -> p s t", s=ST)

        def transposed_slot(n):
            o = 512 * NSA + 1024 * (n % NST)
            return psum[:, o:o + 1024].rearrange("p (h c) -> p h c", h=2)

        def span(a, tt):
            first = P if CAUSAL[a] and tt == 1 else 0
            return slice(tt * S, tt * S + S - first), first

        def work_bank(n):
            o = 512 * NSA + 1024 * NST + 512 * (n % NWORK)
            return psum[:, o:o + 512]

        def wt(name, c0=0, n=None):
            at, cols_ = W_COLS[name]
            return W[:, at + c0:at + (cols_ if n is None else c0 + n)]

        def qe(j):
            return arena[:, j, 0:1024].rearrange("p (s g i c) -> p s g i c", s=ST, g=GROUPS, i=GH)

        def ke(j):
            return arena[:, j, 1024:2048].rearrange("p (s g i c) -> p s g i c", s=ST, g=GROUPS, i=GH)

        def head_parts(view, st):
            return view[:, st, :, :, 0:24].rearrange("p g i (r d) -> p (g i) r d", r=3)

        def o8T(j):
            return arena[:, j, 1024:2048].rearrange("p (g s) -> p g s", g=GROUPS)

        def v8(j):
            return arena[:, j, 2048:3072].rearrange("p (t h c) -> p t h c", t=ST, h=H)

        def qk_nat(j, n):
            return arena[:, j, 3072 + 512 * n:3584 + 512 * n].rearrange("p (s e) -> p s e", s=ST)

        def hT(j):
            return arena[:, j, 1024:2048].rearrange("p (f s) -> p f s", f=NF)

        def v64(a, j):
            if a == 6:
                return arena[:, j, 0:ST * H * (DH + 1)].rearrange("p (t h c) -> p t h c", t=ST, h=H)
            return arena[:, j, 0:ST * (DH + 1)].rearrange("p (t h c) -> p t h c", t=ST, h=1)

        def o64T(j):
            return arena[:, j, 2080:4128].rearrange("p (c s) -> p c s", c=8)

        def q8T(j):
            return stacked[:, j, 0, :].rearrange("p (g s) -> p g s", g=GROUPS)

        def k8T(j):
            return stacked[:, j, 1, :].rearrange("p (g s) -> p g s", g=GROUPS)

        def wide_q(g):
            return stacked[:, 0, g % NR, :].rearrange("p (i s) -> p i s", i=GH)

        def wide_k(g):
            return stacked[:, 1, g % NR, :].rearrange("p (i s) -> p i s", i=GH)

        def key_parts(a, j, g, i):
            if a == 6:
                return wide_k(g)[:, i, :], lo_keys[:, g % NR, i, :]
            return shared_k[:, j, 0, :], shared_k[:, j, 1 + i % 2, :]

        def half(i):
            return slice(DH * (i % 2), DH * (i % 2) + DH)

        def other(i):
            return half(i + 1)

        weights_in = sem("weights_in")
        rows_in = sem("rows_in")
        pos_in = sem("pos_in")
        setup_chain = sem("setup_chain")
        setup_sin = sem("setup_sin")
        loop_first = len(sems)
        tokens_in = sem("tokens_in")
        stored = sem("stored")
        work_full = sem("work_full")
        evacuated = [sem(f"evacuated_{s}") for s in range(NWORK)]
        maxima_full = sem("maxima_full")
        maxima_done = sem("maxima_done")
        scores_full = sem("scores_full")
        probs_full = sem("probs_full")
        scalar_out = sem("scalar_out")
        vector_step = sem("vector_step")
        root_asked = sem("root_asked")
        root_done = sem("root_done")
        narrow_ready = sem("narrow_ready")
        keys_ready = sem("keys_ready")
        blockq_ready = sem("blockq_ready")
        length_done = sem("length_done")
        ones_ready = sem("ones_ready")
        natural = {t: sem(f"natural_{t}") for t in TRANSPOSES}
        hidden_ready = sem("hidden_ready")
        result_ready = sem("result_ready")

        with nc.Block() as block:
            n_weights = [0]
            n_rows = [0]

            @block.sync
            def _(sp):
                for name, view in w["matrices"]:
                    at = name.split(":")
                    dst = wt(at[0], int(at[1]) if len(at) > 1 else 0, int(at[2]))
                    if len(view.shape) == 3:
                        dst = dst.rearrange("p (t n) -> p t n", t=view.shape[1])
                    sp.dma_start(dst, view).then_inc(weights_in, 16)
                    n_weights[0] += 16

            @block.scalar
            def _(act):
                act.dma_start(pos[:, :], w["pos"]).then_inc(pos_in, 16)
                for dst, src in [(ident[:, :], w["ident"]), (iota[:, :], w["iota"].partition_broadcast(P)),
                                 (rope_cos[:, :], w["rope_cos"]), (rope_sin[:, :], w["rope_sin"]),
                                 (consts[:, :], w["consts"]), (nmax[:, 0, 0, :], w["causal"]),
                                 (nmax[:, 0, 1, :], w["causal_t"]),
                                 (arena[:, 0, 0:512], w["sel"])]:
                    act.dma_start(dst, src).then_inc(rows_in, 16)
                    n_rows[0] += 16
                for n, name in enumerate(["ln1_g", "ln1_b", "ln2_g", "ln2_b", "ln3_g", "ln3_b", "fc2_b", "bo", "b2"]):
                    act.dma_start(rows[:, n, :], w[name].partition_broadcast(P)).then_inc(rows_in, 16)
                    n_rows[0] += 16
                for n, name in enumerate(["ca_qn", "ca_kn", "sa_qn", "sa_kn"]):
                    act.dma_start(qkw[:, n, :], w[name].partition_broadcast(P)).then_inc(rows_in, 16)
                    n_rows[0] += 16
                for n, name in enumerate(["gamma_pt", "gamma_ca", "gamma_ctx", "pre_ca_w", "pre_sa_w", "pre_ffn_w",
                                          "fc1_b"]):
                    act.dma_start(cols[:, n:n + 1], w[name].rearrange("(p o) -> p o", o=1)).then_inc(rows_in, 16)
                    n_rows[0] += 16
                act.dma_start(cols[:, 8:12], w["b1"]).then_inc(rows_in, 16)
                n_rows[0] += 16
                act.wait_ge(setup_sin, 1)
                act.activation(setup[:, 2:4, :], setup[:, 4:6, :], ACT.Sin).then_inc(setup_sin, 1)

            @block.vector
            def _(dve):
                n = [0]

                def link(ins):
                    ins.then_inc(setup_chain, 1)
                    n[0] += 1
                    dve.wait_ge(setup_chain, n[0])

                dve.wait_ge(pos_in, 16)
                dve.wait_ge(rows_in, n_rows[0])
                link(dve.tensor_copy(identb[:, :], ident[:, :]))
                link(dve.tensor_copy(causal_st[:, :], nmax[:, 0, 0, :]))
                link(dve.tensor_copy(causal_ts[:, :], nmax[:, 0, 1, :]))
                link(dve.tensor_copy(sel[:, :, :], arena[:, 0, 0:512].rearrange("p (i m) -> p i m", i=GH)))
                link(dve.memset(nmax[:, :, :, :], 0.0))
                for zeroed in (own_keys, lo_keys):
                    link(dve.memset(zeroed[:, :, :, :].rearrange("p n i s -> p (n i s)").bitcast(F32), 0.0))
                link(dve.memset(shared_k[:, :, :, :].rearrange("p j n s -> p (j n s)").bitcast(F32), 0.0))
                link(dve.memset(nmaxT[:, :, :].rearrange("p n s -> p (n s)").bitcast(F32), 0.0))
                link(dve.tensor_scalar(blockq[:, :, :], arena[:, 0, 0:512].rearrange("p (i m) -> p i m", i=GH), 0.0, None, ALU.mult))
                posf = setup[:, 0, 0:B * ST]
                link(dve.tensor_copy(posf, pos[:, :]))
                ang = setup[:, 1, :].rearrange("p (n f) -> p n f", f=4)
                link(dve.tensor_tensor(ang, posf.unsqueeze(2).broadcast_to([P, B * ST, 4]),
                                       consts[:, 48:52].unsqueeze(1).broadcast_to([P, B * ST, 4]), ALU.mult))
                ang, turns, r = setup[:, 1, :], setup[:, 2, :], setup[:, 4, :]
                link(dve.tensor_scalar(turns, ang, 1.0 / TWO_PI, ROUND, ALU.mult, ALU.add))
                link(dve.tensor_scalar(turns, turns, ROUND, None, ALU.subtract))
                c1 = 6.28125
                c2 = 0.001934051513671875
                c3 = float(TWO_PI - c1 - c2)
                link(dve.scalar_tensor_tensor(r, turns, -c1, ang, ALU.mult, ALU.add))
                link(dve.scalar_tensor_tensor(r, turns, -c2, r, ALU.mult, ALU.add))
                link(dve.scalar_tensor_tensor(r, turns, -c3, r, ALU.mult, ALU.add))
                rc = setup[:, 5, :]
                link(dve.tensor_scalar(rc, r, np.pi / 2, None, ALU.add))
                link(dve.tensor_scalar(turns, rc, np.pi, -TWO_PI, ALU.is_gt, ALU.mult))
                link(dve.tensor_tensor(rc, rc, turns, ALU.add))
                dve.tensor_scalar(setup[:, 4:6, :], setup[:, 4:6, :], 3.1415925, -3.1415925, ALU.min, ALU.max)\
                    .then_inc(setup_sin, 1)
                dve.wait_ge(setup_sin, 2)
                table = cs_all[:, :, :].rearrange("p i (t c r f) -> p (i t) c r f", c=2, r=2, f=4)
                sin4 = setup[:, 2, :].rearrange("p (n f) -> p n f", f=4)
                cos4 = setup[:, 3, :].rearrange("p (n f) -> p n f", f=4)
                link(dve.tensor_copy(table[:, :, 0, 0, :], cos4))
                link(dve.tensor_copy(table[:, :, 0, 1, :], cos4))
                link(dve.tensor_scalar(table[:, :, 1, 0, :], sin4, -1.0, None, ALU.mult))
                link(dve.tensor_copy(table[:, :, 1, 1, :], sin4))
                dve.wait_ge(weights_in, n_weights[0])
                for name, c, c0, m in [("fused", 0, 0, 2176), ("wq", 1, 0, 1024), ("w_ff1", 1, 0, 1024),
                                       ("wkv", 2, 0, 128), ("ca", 3, 0, 128), ("sa", 4, 0, 384),
                                       ("g_w1", 5, 0, 512), ("g_w3", 5, 0, 512)]:
                    link(dve.tensor_scalar(wt(name, c0, m), wt(name, c0, m), cols[:, c:c + 1], None, ALU.mult))
                for dst, src, heads in [("rot", wt("fused", 0, 1024), H), ("k2rot", wt("fused", 1024, 64), 1)]:
                    d4 = wt(dst, 0, heads * DH).rearrange("p (h r c) -> p h r c", r=2, c=DH // 2)
                    s4 = src.rearrange("p (h r c) -> p h r c", r=2, c=DH // 2)
                    link(dve.tensor_scalar(d4[:, :, 0, :], s4[:, :, 1, :], -1.0, None, ALU.mult))
                    link(dve.tensor_copy(d4[:, :, 1, :], s4[:, :, 0, :]))
                for half in range(2):
                    link(dve.tensor_copy(wt("k2", DH * half, DH), wt("fused", 1024, DH)))
                    link(dve.tensor_copy(wt("k2c", DH * half, DH), wt("wkv", 0, DH)))
                link(dve.tensor_copy(wt("k2rot", DH, DH), wt("k2rot", 0, DH)))

        with nc.Fori(0, ITERATIONS, hint_back_edge=True) as it:
            with nc.Block() as block:
                unit = {}
                scalar_count = {}
                score_unit = {}
                trans_unit = {}

                def order(kind):
                    return [s for s in STEPS if s[0] == kind]

                key_unit = {s[1:]: n for n, s in enumerate(s for s in order("heads") if NARROW[s[1]])}

                for _, a, j, g, hp in order("maxima"):
                    for i in (2 * hp, 2 * hp + 1):
                        score_unit[(a, j, g, i)] = len(score_unit)
                for _, a, j, g, hp in order("probs"):
                    trans_unit[(a, j, g, hp)] = len(trans_unit)

                def wait_evacuated(eng, *key):
                    n = unit[key]
                    eng.wait_ge(evacuated[n % NWORK], n // NWORK + 1)

                def wait_filled(eng, *key):
                    eng.wait_ge(work_full, unit[key] + 1)
                    return work_bank(unit[key])

                def empties(ins, *key):
                    ins.then_inc(evacuated[unit[key] % NWORK], 1)

                @block.tensor
                def _(pe):
                    def work(*key):
                        n = unit[key] = len(unit)
                        if n >= NWORK:
                            pe.wait_ge(evacuated[n % NWORK], n // NWORK)
                        return work_bank(n)

                    def mm(o, l, r, start=True, stop=True):
                        return pe.matmul(o, l, r, start=start, stop=stop)

                    def transpose(tag, j):
                        src, _ = TRANSPOSES[tag]
                        u = work("T", tag, j)
                        pe.wait_ge(natural[tag], j + 1)
                        for st in range(ST):
                            last = pe.transpose(u[:, st * P:(st + 1) * P], nat[src][:, j, st, :], ident[:, :])
                        last.then_inc(work_full, 1)

                    def prep8(a, j):
                        qt, kt = SOURCES[a]
                        wait_evacuated(pe, "T", qt, j)
                        wait_evacuated(pe, "T", kt, j)
                        qs, ks = (trn[TRANSPOSES[t][1]] for t in (qt, kt))
                        m = {0: "L0_1", 1: "L0_2", 4: "ca", 5: "sa"}[a]
                        for st in range(ST):
                            u = work("qkv", a, j, st)
                            mm(u[:, 0:128], qs[:, j, st * P:(st + 1) * P], wt(m, 0, 128))
                            mm(u[:, 128:384], ks[:, j, st * P:(st + 1) * P], wt(m, 128, 256)).then_inc(work_full, 1)
                        if a in (4, 5):
                            pe.wait_ge(narrow_ready, PAIR * (a - 4) + j + 1)
                        for what, view in (("tq", qe(j)), ("tk", ke(j))):
                            for st in range(ST):
                                if a in (0, 1):
                                    wait_evacuated(pe, "qkv", a, j, st)
                                u = work(what, a, j, st)
                                for g in range(GROUPS):
                                    last = pe.transpose(u[:, g * P:(g + 1) * P],
                                                        view[:, st, g, :, :].rearrange("p i c -> p (i c)"), ident[:, :])
                                last.then_inc(work_full, 1)

                    def length(a, j):
                        pe.wait_ge(blockq_ready, PAIR * a + j + 1)
                        for st in range(ST):
                            wait_evacuated(pe, "tk", a, j, st)
                        for gp in range(2):
                            u = work("len", a, j, gp)
                            for e in range(2):
                                last = mm(u[:, e * S:(e + 1) * S], blockq[:, 2 * gp + e, :], k8T(j)[:, 2 * gp + e, :])
                            last.then_inc(work_full, 1)

                    def prep64(a, j):
                        kt = SOURCES[a][1]
                        wait_evacuated(pe, "T", kt, j)
                        ks = trn[TRANSPOSES[kt][1]][:, j, :]
                        kw = {2: ["k2", "k2rot"], 3: ["k2c"], 6: None}[a]
                        if a != 6:
                            project("k", kw, ks, a, j, 0, 1)
                        for tt in range(ST):
                            l = ks[:, tt * P:(tt + 1) * P]
                            if a == 6:
                                for half in range(2):
                                    u = work("v", a, j, tt, half)
                                    mm(u[:, :], l, wt("v3", 512 * half, 512)).then_inc(work_full, 1)
                            else:
                                u = work("v", a, j, tt, 0)
                                mm(u[:, 0:DH], l, wt("fused", 1088, DH) if a == 2 else wt("wkv", DH, DH))\
                                    .then_inc(work_full, 1)

                    def project(what, names, src, a, j, c, tiles):
                        for v, name in enumerate(names):
                            u = work(what, a, j, c, v)
                            for e in range(tiles):
                                last = mm(u[:, e * S:(e + 1) * S], wt(name, (c + e) * P, P), src)
                            last.then_inc(work_full, 1)

                    def heads(a, j, g):
                        if NARROW[a]:
                            return
                        qt, kt = SOURCES[a]
                        wait_evacuated(pe, "T", qt, j)
                        qs, ks = (trn[TRANSPOSES[t][1]][:, j, :] for t in (qt, kt))
                        project("q", {2: ["fused", "rot"], 3: ["wq"], 6: ["q3"]}[a], qs, a, j, 2 * g, 2)
                        if a == 6:
                            project("k", ["k3"], ks, a, j, 2 * g, 2)

                    def maxima(a, j, g, hp):
                        if g == 0 and hp == 0 and NARROW[a]:
                            for st in range(ST):
                                wait_evacuated(pe, "tq", a, j, st)
                                wait_evacuated(pe, "tk", a, j, st)
                        if NARROW[a]:
                            pe.wait_ge(keys_ready, key_unit[(a, j, g)] + 1)
                        else:
                            wait_evacuated(pe, "q", a, j, 2 * g, 1 if a == 2 else 0)
                            wait_evacuated(pe, "k", a, j, 2 * g if a == 6 else 0, 1 if a == 2 else 0)
                        for i in (2 * hp, 2 * hp + 1):
                            n = score_unit[(a, j, g, i)]
                            if n >= NSA:
                                pe.wait_ge(maxima_done, n - NSA + 1)
                            bank = score_bank(n)
                            for st in range(ST):
                                t1 = P if CAUSAL[a] and st == 0 else S
                                if NARROW[a]:
                                    l, m = q8T(j)[:, g, st * P:(st + 1) * P], own_keys[:, key_unit[(a, j, g)] % NR, i, 0:t1]
                                else:
                                    l, m = wide_q(g)[:, i, st * P:(st + 1) * P], key_parts(a, j, g, i)[0][:, 0:t1]
                                last = mm(bank[:, st, 0:t1], l, m, stop=not CAUSAL[a])
                                if CAUSAL[a]:
                                    last = mm(bank[:, st, t1 - P:t1], identb[:, :], causal_st[:, :], start=False)
                            last.then_inc(maxima_full, 1)

                    def turn_maxima(a, j, g):
                        u = work("max", a, j, g)
                        pe.wait_ge(maxima_done, score_unit[(a, j, g, GH - 1)] + 1)
                        for st in range(ST):
                            src = qe(j)[:, st, g, :, :].rearrange("p i c -> p (i c)") if NARROW[a] else nmax[:, g % 2, st, :]
                            last = pe.transpose(u[:, st * P:(st + 1) * P], src, ident[:, :])
                        last.then_inc(work_full, 1)

                    def probs_(a, j, g, hp):
                        n = trans_unit[(a, j, g, hp)]
                        if n >= NST:
                            pe.wait_ge(probs_full, n - NST + 1)
                        slot = transposed_slot(n)
                        wait_evacuated(pe, "max", a, j, g)
                        for i, tt in [(2 * hp + e, tt) for e in range(2) for tt in range(ST)]:
                            at, s0 = span(a, tt)
                            o = slot[:, i % 2, at]
                            if NARROW[a]:
                                last = mm(o, own_keys[:, key_unit[(a, j, g)] % NR, i, tt * P:(tt + 1) * P],
                                          q8T(j)[:, g, s0:S], stop=not CAUSAL[a])
                            else:
                                hi, lo = (k[:, tt * P:(tt + 1) * P] for k in key_parts(a, j, g, i))
                                mm(o, hi, wide_q(g)[:, i, s0:S], stop=False)
                                mm(o, lo, wide_q(g)[:, i, s0:S], start=False, stop=False)
                                last = mm(o, sel[:, i, :], nmaxT[:, g % 2, s0:S], start=False, stop=not CAUSAL[a])
                            if CAUSAL[a]:
                                last = mm(slot[:, i % 2, at.start:at.start + P], identb[:, :], causal_ts[:, :], start=False)
                        last.then_inc(scores_full, 1)

                    def values(a, j, g):
                        n0 = trans_unit[(a, j, g, 0)]
                        pe.wait_ge(probs_full, n0 + 2)
                        if NARROW[a]:
                            u = work("o", a, j, g)
                            for tt in range(ST):
                                at, s0 = span(a, tt)
                                for i in range(GH):
                                    last = mm(u[BLK * i:BLK * i + BLK, s0:S], v8(j)[:, tt, GH * g + i, :],
                                              probs[:, (n0 + i // 2) % NP, i % 2, at], start=tt == 0, stop=tt == 1)
                            last.then_inc(work_full, 1)
                            return
                        if g == 0:
                            pe.wait_ge(ones_ready, PAIR * {2: 0, 3: 1, 6: 2}[a] + j + 1)
                            for tt in range(ST):
                                for half in range(2 if a == 6 else 1):
                                    wait_evacuated(pe, "v", a, j, tt, half)
                        for st in range(ST):
                            u = work("o", a, j, g, st)
                            tiles = [0] if CAUSAL[a] and st == 0 else [0, 1]
                            for i in range(GH):
                                for tt in tiles:
                                    at, s0 = span(a, tt)
                                    c = at.start + st * P - s0
                                    last = mm(u[:, i * 65:i * 65 + 65], probs[:, (n0 + i // 2) % NP, i % 2, c:c + P],
                                              v64(a, j)[:, tt, GH * g + i if a == 6 else 0, :],
                                              start=tt == 0, stop=tt == tiles[-1])
                            last.then_inc(work_full, 1)

                    def collect(a, j, g):
                        for st in range(ST):
                            wait_evacuated(pe, "o", a, j, g, st)
                        u = work("oT", a, j, g)
                        for c in range(2):
                            for st in range(ST):
                                last = pe.transpose(u[:, (2 * c + st) * P:(2 * c + st + 1) * P],
                                                    onat[:, g % 2, st, c * P:(c + 1) * P], ident[:, :])
                        last.then_inc(work_full, 1)

                    def finish8(a, j):
                        for g in range(GROUPS):
                            wait_evacuated(pe, "o", a, j, g)
                        for st in range(ST):
                            u = work("z", a, j, st)
                            for g in range(GROUPS):
                                last = pe.transpose(u[:, g * P:(g + 1) * P], o8T(j)[:, g, st * P:(st + 1) * P], ident[:, :])
                            last.then_inc(work_full, 1)

                    def finish64(a, j):
                        for g in range(GROUPS):
                            wait_evacuated(pe, "oT", a, j, g)
                        u = work("y", a, j)
                        wo = {2: "attn_out", 3: "w_out", 6: "o3"}[a]
                        terms = [(o64T(j)[:, c, :], wt(wo, c * P, P)) for c in range(8)]
                        if a != 6:
                            pe.wait_ge(hidden_ready, PAIR * NF * (a - 2) + NF * (j + 1))
                            terms += [(hT(j)[:, f, :], wt("ff_out" if a == 2 else "w_ff2", f * P, P)) for f in range(NF)]
                        for st in range(ST):
                            for n, (l, r) in enumerate(terms):
                                last = mm(u[:, st * P:(st + 1) * P], l[:, st * P:(st + 1) * P], r,
                                          start=n == 0, stop=n == len(terms) - 1)
                        last.then_inc(work_full, 1)

                    def ffn(k, j):
                        tag = {0: "x3", 1: "x4", 2: "x7"}[k]
                        wait_evacuated(pe, "T", tag, j)
                        for f in range(NF):
                            u = work("ff", k, j, f)
                            if k == 2:
                                val, gate = wt("g_w3", f * P, P), wt("g_w1", f * P, P)
                            else:
                                name, c0 = ("fused", 1152) if k == 0 else ("w_ff1", 0)
                                val, gate = wt(name, c0 + f * P, P), wt(name, c0 + FF + f * P, P)
                            mm(u[:, 0:S], val, trn["xT"][:, j, :])
                            mm(u[:, S:2 * S], gate, trn["xT"][:, j, :]).then_inc(work_full, 1)

                    def ffn_out(k, j):
                        if k == 2:
                            pe.wait_ge(hidden_ready, PAIR * NF * 2 + NF * (j + 1))
                        else:
                            for f in range(NF):
                                wait_evacuated(pe, "h", j, f)
                        u = work("fo", k, j)
                        name = "g_w2" if k == 2 else "w2_3"
                        for st in range(ST):
                            for f in range(NF):
                                last = mm(u[:, st * P:(st + 1) * P], hT(j)[:, f, st * P:(st + 1) * P], wt(name, f * P, P),
                                          start=f == 0, stop=f == NF - 1)
                        last.then_inc(work_full, 1)

                    def gelu(j):
                        wait_evacuated(pe, "T", "x9", j)
                        for f in range(NF):
                            u = work("h", j, f)
                            mm(u[:, 0:S], wt("w1_3", f * P, P), trn["xT"][:, j, :]).then_inc(work_full, 1)

                    def fc(j):
                        wait_evacuated(pe, "T", "x2", j)
                        u = work("fc1", j)
                        mm(u[:, 0:S], wt("fc1"), trn["xT"][:, j, :]).then_inc(work_full, 1)
                        wait_evacuated(pe, "fc1", j)
                        u = work("fc2", j)
                        for st in range(ST):
                            last = mm(u[:, st * P:(st + 1) * P], hT(j)[:, 0, st * P:(st + 1) * P], wt("fc2"))
                        last.then_inc(work_full, 1)

                    def outproj(a, j):
                        wait_evacuated(pe, "T", f"z{a}", j)
                        u = work("y", a, j)
                        for st in range(ST):
                            last = mm(u[:, st * P:(st + 1) * P], trn["cT"][:, j, st * P:(st + 1) * P],
                                      wt("ca_o" if a == 4 else "sa_o"))
                        last.then_inc(work_full, 1)

                    stages = dict(transpose=transpose, prep8=prep8, length=length, prep64=prep64, heads=heads,
                                  turn_maxima=turn_maxima, maxima=maxima, probs=probs_, values=values, collect=collect,
                                  finish8=finish8, finish64=finish64,
                                  ffn=ffn, ffn_out=ffn_out, gelu=gelu, fc=fc, outproj=outproj)
                    for kind, *args in STEPS:
                        if kind in stages:
                            stages[kind](*args)

                @block.scalar
                def _(act):
                    done = [0]
                    group_done = {n: unit[("o", *k[:3])] if NARROW[k[0]] else unit[("o", *k[:3], ST - 1)]
                                  for k, n in trans_unit.items()}

                    def to_vector(ins, *key):
                        ins.then_inc(scalar_out, 1)
                        done[0] += 1
                        scalar_count[key] = done[0]

                    def transpose(tag, j):
                        u = wait_filled(act, "T", tag, j)
                        empties(act.activation(trn[TRANSPOSES[tag][1]][:, j, :], u[:, 0:S], ACT.Copy), "T", tag, j)

                    def prep8(a, j):
                        for st in range(ST):
                            key = ("qkv", a, j, st)
                            u = wait_filled(act, *key)
                            heads = u[:, 0:384].rearrange("p (x h d) -> p x h d", x=3, d=DS)
                            act.activation(v8(j)[:, st, :, 0:DS], heads[:, 2], ACT.Copy)
                            if a < 2:
                                for view, x, slots in ((qe(j), 0, (0, 1)), (ke(j), 1, (0, 2))):
                                    hp = head_parts(view, st)
                                    o = hp[:, :, slots[0]:slots[1] + 1:slots[1] - slots[0], :]
                                    last = act.activation(o.bitcast(F32R), heads[:, x].unsqueeze(2).broadcast_to([P, H, 2, DS]), ACT.Copy)
                                to_vector(last, *key)
                            else:
                                empties(act.activation(qk_nat(j, 0)[:, st, :], u[:, 0:256], ACT.Copy), *key)
                        for what, dst in (("tq", q8T(j)), ("tk", k8T(j))):
                            for st in range(ST):
                                u = wait_filled(act, what, a, j, st)
                                empties(act.activation(dst[:, :, st * P:(st + 1) * P],
                                                       u.rearrange("p (g s) -> p g s", g=GROUPS), ACT.Copy), what, a, j, st)

                    def prep64(a, j):
                        if a == 3:
                            u = wait_filled(act, "k", a, j, 0, 0)
                            to_vector(act.activation(shared_k[:, j, 0, :], u[:, 0:S], ACT.Copy), "k", a, j, 0)
                        for tt in range(ST):
                            for half in range(2 if a == 6 else 1):
                                u = wait_filled(act, "v", a, j, tt, half)
                                k = 8 if a == 6 else 1
                                empties(act.activation(v64(a, j)[:, tt, 8 * half:8 * half + k, 0:DH],
                                                       u[:, 0:k * DH].rearrange("p (h d) -> p h d", d=DH), ACT.Copy),
                                        "v", a, j, tt, half)

                    def heads(a, j, g):
                        if NARROW[a]:
                            if a < 2:
                                act.wait_ge(length_done, PAIR * a + j + 1)
                            else:
                                for st in range(ST):
                                    wait_evacuated(act, "tk", a, j, st)
                            for i in range(GH):
                                r = slice(BLK * i, BLK * i + BLK)
                                last = act.activation(own_keys[r, key_unit[(a, j, g)] % NR, i, :],
                                                      k8T(j)[r, g, :].bitcast(F32), ACT.Copy)
                            last.then_inc(keys_ready, 1)
                            return
                        if a == 2:
                            return
                        for what in ("q", "k") if a == 6 else ("q",):
                            u = wait_filled(act, what, a, j, 2 * g, 0).rearrange("p (c s) -> p c s", c=2)
                            dst = wide_q(g) if what == "q" else wide_k(g)
                            for i in range(2):
                                last = act.activation(dst[half(i), i::2, :], u[half(i)], ACT.Copy)
                                if what == "k":
                                    last = act.activation(dst[other(i), i::2, :], u[half(i)], ACT.Copy)
                            to_vector(last, what, a, j, g)

                    def probs_(a, j, g, hp):
                        n = trans_unit[(a, j, g, hp)]
                        act.wait_ge(scores_full, n + 1)
                        if n >= NP:
                            act.wait_ge(work_full, group_done[n - NP] + 1)
                        c = span(a, 1)[0].stop
                        act.activation(probs[:, n % NP, :, 0:c], transposed_slot(n)[:, :, 0:c], ACT.Exp,
                                       scale=float(SCALE[a])).then_inc(probs_full, 1)

                    def values(a, j, g):
                        if NARROW[a]:
                            u = wait_filled(act, "o", a, j, g)
                            empties(act.activation(o8T(j)[:, g, :], u[:, 0:S], ACT.Copy), "o", a, j, g)

                    def collect(a, j, g):
                        u = wait_filled(act, "oT", a, j, g)
                        empties(act.activation(o64T(j)[:, 2 * g:2 * g + 2, :],
                                               u.rearrange("p (c s) -> p c s", c=2), ACT.Copy), "oT", a, j, g)

                    def ffn(k, j):
                        for f in range(NF):
                            u = wait_filled(act, "ff", k, j, f)
                            to_vector(act.activation(hT(j)[:, f, :], u[:, S:2 * S], ACT.Silu), "ff", k, j, f)

                    def gelu(j):
                        for f in range(NF):
                            u = wait_filled(act, "h", j, f)
                            empties(act.activation(hT(j)[:, f, :], u[:, 0:S], ACT.Gelu, bias=cols[:, 8 + f:9 + f]), "h", j, f)

                    def fc(j):
                        u = wait_filled(act, "fc1", j)
                        empties(act.activation(hT(j)[:, 0, :], u[:, 0:S], ACT.Relu, bias=cols[:, 6:7]), "fc1", j)

                    stages = dict(transpose=transpose, prep8=prep8, prep64=prep64, heads=heads, probs=probs_, values=values,
                                  collect=collect, ffn=ffn, gelu=gelu, fc=fc)
                    for kind, *args in STEPS:
                        if kind in stages:
                            stages[kind](*args)

                @block.vector
                def _(dve):
                    chain = [0]

                    def link(ins):
                        ins.then_inc(vector_step, 1)
                        chain[0] += 1
                        dve.wait_ge(vector_step, chain[0])

                    def signal(ins, s, value):
                        ins.then_inc(s, 1)
                        dve.wait_ge(s, value)

                    asked = [0]

                    def inverse_root(ins):
                        ins.then_inc(root_asked, 1)
                        asked[0] += 1
                        dve.wait_ge(root_done, asked[0])

                    def row(n):
                        return rows[:, n, :].unsqueeze(1).broadcast_to([P, ST, D])

                    def statistics(j, src, eps, mean):
                        sm = small[:, j, :]
                        if mean:
                            for st in range(ST):
                                link(dve.bn_stats(sm[:, 8 + 6 * st:14 + 6 * st], src[:, j, st, :]))
                            for st in range(ST):
                                link(dve.bn_aggr(sm[:, 4 + 2 * st:6 + 2 * st], sm[:, 8 + 6 * st:14 + 6 * st]))
                            mv = sm[:, 4:8].rearrange("p (s c) -> p s c", c=2)
                            link(dve.tensor_copy(sm[:, 0:2], mv[:, :, 0]))
                            inverse_root(dve.tensor_scalar(sm[:, 2:4], mv[:, :, 1], eps, None, ALU.add))
                        else:
                            sq = tmp[:, 0:S].rearrange("p (s d) -> p s d", s=ST)
                            link(dve.tensor_tensor(sq, src[:, j], src[:, j], ALU.mult))
                            link(dve.tensor_reduce(sm[:, 4:6], sq, axis=AX, op=ALU.add))
                            inverse_root(dve.tensor_scalar(sm[:, 2:4], sm[:, 4:6], 1.0 / D, eps, ALU.mult, ALU.add))

                    def normed(j, src, dst, mean=True, eps=EPS_LN):
                        statistics(j, src, eps, mean)
                        sm = small[:, j, :]
                        for st in range(ST):
                            if mean:
                                last = dve.tensor_scalar(dst[:, j, st, :], src[:, j, st, :], sm[:, st:st + 1],
                                                         sm[:, 2 + st:3 + st], ALU.subtract, ALU.mult)
                            else:
                                last = dve.tensor_scalar(dst[:, j, st, :], src[:, j, st, :], sm[:, 2 + st:3 + st], None, ALU.mult)
                            if st == 0:
                                link(last)
                        return last

                    def start(j):
                        if j == 0:
                            dve.wait_ge(tokens_in, 32)
                            link(dve.tensor_copy(cs[:, :, :, :].rearrange("p t c d -> p (t c d)").unsqueeze(1),
                                                 cs_all[:, bass.ds(it, 1), :]))
                        token_mask(j, nat["x"], 24)
                        signal(dve.tensor_copy(small[:, j, 30:31], small[:, j, 24:25]), natural["x0"], j + 1)
                        dve.tensor_copy(small[:, j, 31:32], small[:, j, 24:25]).then_inc(natural["craw"], 1)

                    def token_mask(j, src, at):
                        sm = small[:, j, :]
                        link(dve.tensor_reduce(sm[:, at + 2:at + 4], src[:, j], axis=AX, op=ALU.max, apply_absolute_value=True))
                        link(dve.tensor_scalar(sm[:, at:at + 2], sm[:, at + 2:at + 4], 0.0, None, ALU.not_equal))

                    def pads(j):
                        q_, k_ = (view.rearrange("p s g i c -> p (s g i) c")[:, :, 24:32] for view in (qe(j), ke(j)))
                        dve.tensor_copy(q_, consts[:, 8:16].unsqueeze(1).broadcast_to([P, 32, 8]))
                        dve.tensor_copy(k_, consts[:, 16:24].unsqueeze(1).broadcast_to([P, 32, 8]))
                        link(dve.tensor_copy(v8(j).rearrange("p t h c -> p (t h) c")[:, :, 8:32],
                                        consts[:, 24:48].unsqueeze(1).broadcast_to([P, 32, 24])))

                    def prep8(a, j):
                        pads(j)
                        if a < 2:
                            for st in range(ST):
                                key = ("qkv", a, j, st)
                                wait_filled(dve, *key)
                                u = work_bank(unit[key])
                                dve.wait_ge(scalar_out, scalar_count[key])
                                heads = u[:, 0:256].rearrange("p (x h d) -> p x h d", x=2, d=DS)
                                for view, x, lo in ((qe(j), 0, 2), (ke(j), 1, 1)):
                                    hp = head_parts(view, st)
                                    last = dve.tensor_tensor(hp[:, :, lo, :].bitcast(F32R), heads[:, x], hp[:, :, 0, :], ALU.subtract)
                                empties(last, *key)
                            return
                        for st in range(ST):
                            wait_evacuated(dve, "qkv", a, j, st)
                        X, Y = qk_nat(j, 0), qk_nat(j, 1)
                        Z = tmp[:, 0:512].rearrange("p (s e) -> p s e", s=ST)
                        X3, Y3 = (v.rearrange("p s (n d) -> p (s n) d", d=DS) for v in (X, Y))
                        ms = small[:, j, 64:128]
                        link(dve.tensor_tensor(Y, X, X, ALU.mult))
                        link(dve.tensor_reduce(ms, Y3, axis=AX, op=ALU.add))
                        inverse_root(dve.tensor_scalar(ms, ms, 1.0 / DS, EPS_RMS, ALU.mult, ALU.add))
                        link(dve.tensor_tensor(X3, X3, ms.unsqueeze(2).broadcast_to([P, 64, DS]), ALU.mult))
                        for x in range(2):
                            v = X[:, :, 128 * x:128 * x + 128].rearrange("p s (n d) -> p s n d", d=DS)
                            g_ = qkw[:, 2 * (a - 4) + x, :].unsqueeze(1).unsqueeze(1).broadcast_to([P, ST, H, DS])
                            link(dve.tensor_tensor(v, v, g_, ALU.mult))
                        for st in range(ST):
                            x3, y3, z3 = (v[:, st, :].rearrange("p (n d) -> p n d", d=DS) for v in (X, Y, Z))
                            c_, s_ = (cs[:, ST * j + st, m, :].unsqueeze(1).broadcast_to([P, 32, DS]) for m in (0, 1))
                            dve.tensor_tensor(y3, x3, c_, ALU.mult)
                            dve.tensor_tensor(z3[:, :, 0:4], x3[:, :, 4:8], s_[:, :, 0:4], ALU.mult)
                            link(dve.tensor_tensor(z3[:, :, 4:8], x3[:, :, 0:4], s_[:, :, 4:8], ALU.mult))
                        link(dve.tensor_tensor(X, Y, Z, ALU.add))
                        for st in range(ST):
                            for view, x, slots, lo in ((qe(j), 0, (0, 1), 2), (ke(j), 1, (0, 2), 1)):
                                hp = head_parts(view, st)
                                src = X[:, st, 128 * x:128 * x + 128].rearrange("p (h d) -> p h d", d=DS)
                                o = hp[:, :, slots[0]:slots[1] + 1:slots[1] - slots[0], :]
                                link(dve.tensor_copy(o.bitcast(F32R), src.unsqueeze(2).broadcast_to([P, H, 2, DS])))
                                last = dve.tensor_tensor(hp[:, :, lo, :].bitcast(F32R), src, hp[:, :, 0, :], ALU.subtract)
                        signal(last, narrow_ready, PAIR * (a - 4) + j + 1)

                    def length(a, j):
                        wait_evacuated(dve, "tq", a, j, 0)
                        if (a, j) != (0, 0):
                            pa, pj = (a, j - 1) if j else (a - 1, 1)
                            wait_filled(dve, "len", pa, pj, 1)
                        cols25 = blockq[:, :, :].rearrange("p g (i c) -> p g i c", i=GH)[:, :, :, COL_LEN]
                        first = q8T(j)[:, :, 0:1].bitcast(F32).broadcast_to([P, GROUPS, GH])
                        signal(dve.tensor_tensor(cols25, first, consts[:, 0:4].unsqueeze(1).broadcast_to([P, GROUPS, GH]), ALU.mult),
                               blockq_ready, PAIR * a + j + 1)
                        ln = small[:, j, 32:36]
                        for gp in range(2):
                            u = wait_filled(dve, "len", a, j, gp)
                            t = tmp[:, 0:512]
                            signal(dve.tensor_scalar(t, u, 0.0, None, ALU.not_equal),
                                   evacuated[unit[("len", a, j, gp)] % NWORK], unit[("len", a, j, gp)] // NWORK + 1)
                            link(dve.tensor_reduce(ln[:, 2 * gp:2 * gp + 2], t.rearrange("p (e t) -> p e t", e=2), axis=AX, op=ALU.add))
                        lm = tmp[:, :].rearrange("p (g t) -> p g t", g=GROUPS)
                        for g in range(GROUPS):
                            link(dve.tensor_scalar(lm[:, g, :], iota[:, :], ln[:, g:g + 1], consts[:, 4:5], ALU.is_ge, ALU.mult))
                        signal(dve.tensor_tensor(k8T(j), k8T(j).bitcast(F32), lm, ALU.add), length_done, PAIR * a + j + 1)

                    def prep64(a, j):
                        ones = v64(a, j)[:, :, :, DH:DH + 1].rearrange("p t h c -> p (t h) c")
                        n = ones.shape[1]
                        signal(dve.tensor_copy(ones, consts[:, 24:25].unsqueeze(1).broadcast_to([P, n, 1])),
                               ones_ready, PAIR * {2: 0, 3: 1, 6: 2}[a] + j + 1)
                        hi, *lo = (shared_k[:, j, m, :] for m in range(3))
                        if a == 2:
                            t = turned("k", a, j, 0, 1)[:, 0, :]
                            link(dve.tensor_copy(hi, t))
                        elif a == 3:
                            t = wait_filled(dve, "k", a, j, 0, 0)[:, 0:S]
                            dve.wait_ge(scalar_out, scalar_count[("k", a, j, 0)])
                        if a != 6:
                            n = unit[("k", a, j, 0, 1 if a == 2 else 0)]
                            for i in range(2):
                                last = dve.tensor_tensor(lo[i][half(i)], t[half(i)], hi[half(i)].bitcast(F32), ALU.subtract)
                            signal(last, evacuated[n % NWORK], n // NWORK + 1)

                    def heads(a, j, g):
                        if NARROW[a]:
                            return
                        q = wide_q(g)
                        if a == 2:
                            t = turned("q", a, j, 2 * g, 2)
                            for i in range(2):
                                last = dve.tensor_copy(q[half(i), i::2, :], t[half(i)])
                            link(last)
                            n = unit[("q", a, j, 2 * g, 1)]
                        else:
                            t = wait_filled(dve, "q", a, j, 2 * g, 0).rearrange("p (c s) -> p c s", c=2)
                            dve.wait_ge(scalar_out, scalar_count[("q", a, j, g)])
                            n = unit[("q", a, j, 2 * g, 0)]
                        for i in range(2):
                            last = dve.tensor_tensor(q[other(i), i::2, :], t[half(i)], q[half(i), i::2, :].bitcast(F32), ALU.subtract)
                        signal(last, evacuated[n % NWORK], n // NWORK + 1)
                        if a == 6:
                            key = ("k", a, j, 2 * g, 0)
                            t = wait_filled(dve, *key).rearrange("p (c s) -> p c s", c=2)
                            dve.wait_ge(scalar_out, scalar_count[("k", a, j, g)])
                            for i in range(2):
                                last = dve.tensor_tensor(lo_keys[half(i), g % NR, i::2, :], t[half(i)],
                                                         wide_k(g)[half(i), i::2, :].bitcast(F32), ALU.subtract)
                            empties(last, *key)

                    def turned(what, a, j, c, k):
                        t = [tmp[:, 512 * v:512 * v + k * S].rearrange("p (c s) -> p c s", c=k) for v in range(2)]
                        for v, table in enumerate((rope_cos, rope_sin)):
                            u = wait_filled(dve, what, a, j, c, v)[:, 0:k * S].rearrange("p (c s) -> p c s", c=k)
                            n = unit[(what, a, j, c, v)]
                            ins = dve.tensor_tensor(t[v], u, table[:, :].unsqueeze(1).broadcast_to([P, k, S]), ALU.mult)
                            if v == 0:
                                signal(ins, evacuated[n % NWORK], n // NWORK + 1)
                            else:
                                link(ins)
                        link(dve.tensor_tensor(t[0], t[0], t[1], ALU.add))
                        return t[0]

                    def maxima(a, j, g, hp):
                        for i in (2 * hp, 2 * hp + 1):
                            n = score_unit[(a, j, g, i)]
                            dve.wait_ge(maxima_full, n + 1)
                            o = qe(j)[:, :, g, i, COL_MAX] if NARROW[a] else nmax[:, g % 2, :, i]
                            bank = score_bank(n)
                            if CAUSAL[a]:
                                dve.tensor_reduce(o[:, 0:1], bank[:, 0, 0:P], axis=AX, op=ALU.max, negate=True)
                                dve.tensor_reduce(o[:, 1:2], bank[:, 1, :], axis=AX, op=ALU.max, negate=True)\
                                    .then_inc(maxima_done, 1)
                            else:
                                dve.tensor_reduce(o, bank, axis=AX, op=ALU.max, negate=True).then_inc(maxima_done, 1)

                    def turn_maxima(a, j, g):
                        u = wait_filled(dve, "max", a, j, g)
                        if NARROW[a]:
                            empties(dve.tensor_scalar(q8T(j)[:, g, :], u[:, 0:S], MAX_GUARD, None, ALU.min), "max", a, j, g)
                        else:
                            empties(dve.tensor_scalar(nmaxT[0:GH, g % 2, :], u[0:GH, 0:S], MAX_GUARD, None, ALU.min), "max", a, j, g)

                    def values(a, j, g):
                        if NARROW[a]:
                            return
                        for st in range(ST):
                            u = wait_filled(dve, "o", a, j, g, st)[:, 0:GH * 65].rearrange("p (h c) -> p h c", h=GH)
                            rec = small[:, j, 40 + 4 * st:44 + 4 * st]
                            link(dve.reciprocal(rec, u[:, :, DH]))
                            empties(dve.tensor_tensor(onat[:, g % 2, st, :].rearrange("p (h d) -> p h d", h=GH), u[:, :, 0:DH],
                                                      rec.unsqueeze(2).broadcast_to([P, GH, DH]), ALU.mult), "o", a, j, g, st)

                    def finish8(a, j):
                        for st in range(ST):
                            u = wait_filled(dve, "z", a, j, st).rearrange("p (h c) -> p h c", h=H)
                            rec = small[:, j, 128 + 16 * st:144 + 16 * st]
                            link(dve.reciprocal(rec, u[:, :, DS]))
                            if a < 2:
                                m = (24 if a == 0 else 56) + st
                                link(dve.tensor_scalar(rec, rec, small[:, j, m:m + 1], None, ALU.mult))
                            n = unit[("z", a, j, st)]
                            signal(dve.tensor_tensor(nat["z"][:, j, st, :].rearrange("p (h d) -> p h d", h=H), u[:, :, 0:DS],
                                                     rec.unsqueeze(2).broadcast_to([P, H, DS]), ALU.mult),
                                   evacuated[n % NWORK], n // NWORK + 1)
                        if a in (4, 5):
                            dve.tensor_copy(small[:, j, 30:31], small[:, j, 24:25]).then_inc(natural[f"z{a}"], 1)

                    def add_unit(j, *key):
                        u = wait_filled(dve, *key)[:, 0:S].rearrange("p (s d) -> p s d", s=ST)
                        n = unit[key]
                        signal(dve.tensor_tensor(nat["x"][:, j], nat["x"][:, j], u, ALU.add), evacuated[n % NWORK], n // NWORK + 1)

                    def norm_l0a(j):
                        link(dve.tensor_tensor(nat["z"][:, j], nat["z"][:, j], nat["x"][:, j], ALU.add))
                        link(normed(j, nat["z"], nat["y"]))
                        link(dve.tensor_tensor(nat["y"][:, j], nat["y"][:, j], row(0), ALU.mult))
                        signal(dve.tensor_tensor(nat["y"][:, j], nat["y"][:, j], row(1), ALU.add), natural["x1"], j + 1)
                        token_mask(j, nat["y"], 56)
                        for st in range(ST):
                            last = dve.tensor_scalar(nat["z"][:, j, st, :], nat["cx"][:, j, st, :], small[:, j, 56 + st:57 + st], None, ALU.mult)
                        last.then_inc(natural["cm"], 1)

                    def norm_l0b(j):
                        link(dve.tensor_tensor(nat["z"][:, j], nat["z"][:, j], nat["y"][:, j], ALU.add))
                        link(normed(j, nat["z"], nat["x"]))
                        link(dve.tensor_tensor(nat["x"][:, j], nat["x"][:, j], row(2), ALU.mult))
                        signal(dve.tensor_tensor(nat["x"][:, j], nat["x"][:, j], row(3), ALU.add), natural["x2"], j + 1)

                    def norm_l0c(j):
                        u = wait_filled(dve, "fc2", j)[:, 0:S].rearrange("p (s d) -> p s d", s=ST)
                        n = unit[("fc2", j)]
                        signal(dve.tensor_tensor(nat["z"][:, j], u, row(6), ALU.add), evacuated[n % NWORK], n // NWORK + 1)
                        for st in range(ST):
                            link(dve.scalar_tensor_tensor(nat["z"][:, j, st, :], nat["z"][:, j, st, :], small[:, j, 24 + st:25 + st],
                                                          nat["x"][:, j, st, :], ALU.mult, ALU.add))
                        link(normed(j, nat["z"], nat["x"]))
                        link(dve.tensor_tensor(nat["x"][:, j], nat["x"][:, j], row(4), ALU.mult))
                        link(dve.tensor_tensor(nat["x"][:, j], nat["x"][:, j], row(5), ALU.add))
                        signal(normed(j, nat["x"], nat["y"]), natural["x3"], j + 1)
                        signal(normed(j, nat["cx"], nat["z"]), natural["cn"], j + 1)

                    def norm_l1(j):
                        signal(normed(j, nat["x"], nat["y"]), natural["x4"], j + 1)

                    def rms_(tag, j):
                        signal(normed(j, nat["x"], nat["y"], mean=False, eps=EPS_RMS), natural[tag], j + 1)

                    def ffn(k, j):
                        for f in range(NF):
                            u = wait_filled(dve, "ff", k, j, f)
                            dve.wait_ge(scalar_out, scalar_count[("ff", k, j, f)])
                            h = hT(j)[:, f, :]
                            n = unit[("ff", k, j, f)]
                            signal(dve.tensor_tensor(h, h, u[:, 0:S], ALU.mult), evacuated[n % NWORK], n // NWORK + 1)
                            dve.tensor_copy(small[:, j, 30:31], small[:, j, 24:25]).then_inc(hidden_ready, 1)

                    def copy_l3(j):
                        add_unit(j, "fo", 2, j)
                        dve.tensor_copy(small[:, j, 30:31], small[:, j, 24:25]).then_inc(natural["x8"], 1)

                    def bias_l3(j):
                        signal(dve.tensor_tensor(nat["x"][:, j], nat["x"][:, j], row(7), ALU.add), natural["x9"], j + 1)

                    def store(j):
                        add_unit(j, "fo", 3, j)
                        dve.tensor_tensor(nat["y"][:, j], nat["x"][:, j], row(8), ALU.add).then_inc(result_ready, 1)

                    stages = dict(start=start, prep8=prep8, length=length, prep64=prep64, heads=heads, turn_maxima=turn_maxima, maxima=maxima,
                                  values=values, finish8=finish8, ffn=ffn,
                                  finish64=lambda a, j: add_unit(j, "y", a, j),
                                  outproj=lambda a, j: add_unit(j, "y", a, j),
                                  norm_l0a=norm_l0a, norm_l0b=norm_l0b, norm_l0c=norm_l0c, norm_l1=norm_l1,
                                  rms_a=lambda j: rms_("x5", j), rms_b=lambda j: rms_("x6", j), rms_c=lambda j: rms_("x7", j),
                                  copy_l3=copy_l3, bias_l3=bias_l3, store=store)
                    for kind, *args in STEPS:
                        if kind in stages:
                            stages[kind](*args)

                @block.gpsimd
                def _(pool):
                    asked = [0]

                    def inverse_root(view):
                        asked[0] += 1
                        pool.wait_ge(root_asked, asked[0])
                        pool.tensor_tensor(view, view, consts[:, 52:53].broadcast_to(list(view.shape)), ALU.pow)\
                            .then_inc(root_done, 1)

                    norms = dict(norm_l0a=1, norm_l0b=1, norm_l0c=3, norm_l1=1, rms_a=1, rms_b=1, rms_c=1)
                    for kind, *args in STEPS:
                        if kind in norms:
                            for _ in range(norms[kind]):
                                inverse_root(small[:, args[-1], 2:4])
                        if kind == "prep8" and args[0] in (4, 5):
                            inverse_root(small[:, args[1], 64:128])

                @block.sync
                def _(sp):
                    def rows_of(t):
                        return t.rearrange("(i j) (s p) d -> i p (j s) d", j=PAIR, p=P)[bass.ds(it, 1)].rearrange("o p a d -> (o p) a d")
                    for k, src in (("x", w["x"]), ("cx", w["ctx"])):
                        sp.dma_start(nat[k][:, :, :, :].rearrange("p j s d -> p (j s) d"), rows_of(src)).then_inc(tokens_in, 16)
                    sp.wait_ge(result_ready, PAIR)
                    sp.dma_start(rows_of(out), nat["y"][:, :, :, :].rearrange("p j s d -> p (j s) d")).then_inc(stored, 16)
                    sp.wait_ge(stored, 16)

            names = [s for s in list(sems.values())[loop_first:]]
            nums = sorted(s.num for s in names)
            assert nums == list(range(nums[0], nums[-1] + 1))
            nc.gpsimd.sem_clear(range(nums[0], nums[-1] + 1))
            nc.all_engine_barrier()


def _tables():
    p, f = np.arange(P), np.float32
    ident = np.eye(P, dtype=f)
    causal = np.where(p[None, :] > p[:, None], f(NEG), f(0)).astype(f)
    inv = (1.0 / f(10000.0) ** (np.arange(0, DH, 2, dtype=f) / f(DH))).astype(f)
    ang = np.arange(S, dtype=f)[:, None] * inv[None, :]
    ang = np.concatenate([ang] * 4, axis=1).T
    consts = np.zeros((P, 128), f)
    for i in range(GH):
        consts[BLK * i:BLK * i + 3 * DS, i] = 1.0
        consts[BLK * i + COL_LEN, 4] = NEG
    consts[:, 8 + COL_LEN - 24] = 1.0
    consts[:, 16 + COL_MAX - 24] = 1.0
    consts[:, 24] = 1.0
    consts[:, 48:52] = 1.0 / f(10000.0) ** (np.arange(0, DS, 2, dtype=f) / f(DS))
    consts[:, 52] = -0.5
    sel = np.zeros((P, GH, P), f)
    for i in range(GH):
        sel[i, i, :] = 1.0
    return {"ident": ident, "causal": causal, "causal_t": np.ascontiguousarray(causal.T), "iota": np.arange(S, dtype=f),
            "rope_cos": np.cos(ang.astype(np.float64)).astype(f), "rope_sin": np.sin(ang.astype(np.float64)).astype(f),
            "consts": consts, "sel": sel.reshape(P, GH * P)}


def kernel(**inputs):
    import concourse.bacc as bacc
    from concourse.bass_utils import run_bass_kernel_spmd

    nc = bacc.Bacc("TRN2", target_bir_lowering=False, num_devices=1)
    arrays = {}

    def dram(name, a):
        a = np.ascontiguousarray(a)
        arrays[name] = a
        return nc.dram_tensor(name, a.shape, mybir.dt.from_np(a.dtype), kind="ExternalInput").ap()

    i = {k: np.asarray(v) for k, v in inputs.items()}
    w = {"x": dram("x_in", i["x"]), "ctx": dram("ctx_in", i["ctx_1024"]), "pos": dram("pos_in", i["pos_BxS2"].reshape(B * ST, P).T)}
    for k, v in _tables().items():
        w[k] = dram(f"table_{k}", v)

    def heads_in(name):
        return dram(name, i[name].transpose(1, 0, 2).reshape(D, D))

    def plain(name):
        return dram(name, i[name])

    def tiled(name):
        return plain(name).rearrange("(t p) n -> p t n", p=P)

    w["matrices"] = (
        [(f"L0_{c}:{128 * n}:128", heads_in(f"L0_xattn_W{x}{c}")) for c in (1, 2) for n, x in enumerate("qkv")]
        + [("fc1:0:128", dram("fc1_wT", i["L0_xattn_fc1_w"].T)), ("fc2:0:128", dram("fc2_wT", i["L0_xattn_fc2_w"].T)),
           ("fused:0:2176", plain("L1_xattn_w_fused")), ("attn_out:0:1024", tiled("L1_xattn_w_attn_out")),
           ("ff_out:0:512", tiled("L1_xattn_w_ff_out")), ("wq:0:1024", plain("L1_xattn_w_q")),
           ("wkv:0:128", plain("L1_xattn_w_kv")), ("w_out:0:1024", tiled("L1_xattn_w_out")),
           ("w_ff1:0:1024", plain("L1_xattn_w_ff1")), ("w_ff2:0:512", tiled("L1_xattn_w_ff2")),
           ("ca:0:128", plain("L2_xattn_ca_Wq")), ("ca:128:256", plain("L2_xattn_ca_Wkv")), ("ca_o:0:128", plain("L2_xattn_ca_Wo")),
           ("sa:0:128", plain("L2_xattn_sa_Wq")), ("sa:128:256", plain("L2_xattn_sa_Wkv")), ("sa_o:0:128", plain("L2_xattn_sa_Wo")),
           ("g_w1:0:512", plain("L2_xattn_W1")), ("g_w3:0:512", plain("L2_xattn_W3")), ("g_w2:0:512", tiled("L2_xattn_W2")),
           ("q3:0:1024", plain("L3_xattn_Wq")), ("k3:0:1024", plain("L3_xattn_Wk")), ("v3:0:1024", plain("L3_xattn_Wv")),
           ("o3:0:1024", tiled("L3_xattn_Wo")), ("w1_3:0:512", plain("L3_xattn_W1")), ("w2_3:0:512", tiled("L3_xattn_W2"))])
    for k in ("ln1_g", "ln1_b", "ln2_g", "ln2_b", "ln3_g", "ln3_b", "fc1_b", "fc2_b"):
        w[k] = plain(f"L0_xattn_{k}")
    for k in ("gamma_pt", "gamma_ca", "gamma_ctx"):
        w[k] = plain(f"L1_xattn_{k}")
    for k in ("ca_qn", "ca_kn", "sa_qn", "sa_kn", "pre_ca_w", "pre_sa_w", "pre_ffn_w"):
        w[k] = plain(f"L2_xattn_{k}")
    for k in ("bo", "b2"):
        w[k] = plain(f"L3_xattn_{k}")
    w["b1"] = dram("b1_columns", i["L3_xattn_b1"].reshape(NF, P).T)

    out = nc.dram_tensor("out", (B, S, D), F32, kind="ExternalOutput").ap()
    build_program(nc, w, out)
    r = run_bass_kernel_spmd(nc, [arrays], core_ids=[0])
    return r.results[0]["out"]
```

```python
from contextlib import ExitStack

import numpy as np

import concourse.bass as bass
from concourse import mybir

F32 = mybir.dt.float32
F32R = mybir.dt.float32r
BF16 = mybir.dt.bfloat16
I32 = mybir.dt.int32
ALU = mybir.AluOpType
ACT = mybir.ActivationFunctionType
AX = mybir.AxisListType.X

P = 128
B, S, D, H = 8, 256, 128, 16
PAIR = 2
ITERATIONS = B // PAIR
ST = S // P
DH = 64
DS = D // H
FF = 512
NF = FF // P
GROUPS, GH = 4, 4
BLK = 32
COL_MAX, COL_LEN = 24, 25
NEG = -1.0e30
MAX_GUARD = 1.0e29
EPS_LN, EPS_RMS = 1e-5, 1e-6
NWORK, NSA, NST, NP, NR = 4, 2, 2, 8, 2
TWO_PI = 2.0 * np.pi
ROUND = 12582912.0

NARROW = [True, True, False, False, True, True, False]
CAUSAL = [True, False, True, False, False, False, False]
SCALE = [DS ** -0.5 if n else DH ** -0.5 for n in NARROW]

W_COLS = {}


def _plan_weights():
    at = 0
    for name, cols in [("L0_1", 384), ("L0_2", 384), ("fc1", 128), ("fc2", 128),
                       ("fused", 2176), ("attn_out", 1024), ("ff_out", 512), ("wq", 1024), ("wkv", 128),
                       ("w_out", 1024), ("w_ff1", 1024), ("w_ff2", 512), ("rot", 1024),
                       ("k2", 128), ("k2rot", 128), ("k2c", 128),
                       ("ca", 384), ("ca_o", 128), ("sa", 384), ("sa_o", 128),
                       ("g_w1", 512), ("g_w3", 512), ("g_w2", 512),
                       ("q3", 1024), ("k3", 1024), ("v3", 1024), ("o3", 1024), ("w1_3", 512), ("w2_3", 512)]:
        W_COLS[name] = (at, cols)
        at += cols
    return at


W_TOTAL = _plan_weights()


def chains():
    return [
        [[("start",)], [("transpose", "x0"), ("transpose", "craw")], [("project8", 0)], [("turn8", 0)], [("length", 0)], [("mask", 0)]],
        [[("finish8", 0)], [("norm_l0a",)], [("transpose", "x1"), ("transpose", "cm")], [("project8", 1)], [("turn8", 1)], [("length", 1)], [("mask", 1)]],
        [[("finish8", 1)], [("norm_l0b",)], [("transpose", "x2")], [("fc",), ("norm_l0c",)],
         [("norm_x3",)], [("transpose", "x3")], [("prep64", 2)]],
        [[("finish64", 2)], [("norm_l1",)], [("norm_cn",)], [("transpose", "x4"), ("transpose", "cn")], [("prep64", 3)]],
        [[("finish64", 3)], [("rms_a",)], [("transpose", "x5")], [("project8", 4)], [("norm8", 4)],
         [("rope8", 4)], [("split8", 4)], [("turn8", 4)]],
        [[("finish8", 4)], [("transpose", "z4")], [("outproj", 4)], [("rms_b",)], [("transpose", "x6")], [("project8", 5)], [("norm8", 5)],
         [("rope8", 5)], [("split8", 5)], [("turn8", 5)]],
        [[("finish8", 5)], [("transpose", "z5")], [("outproj", 5)], [("rms_c",)], [("transpose", "x7")], [("ffn", 2)],
         [("ffn_out", 2), ("copy_l3",)], [("transpose", "x8")], [("prep64", 6)]],
        [[("finish64", 6)], [("bias_l3",)], [("transpose", "x9")], [("gelu",)], [("ffn_out", 3), ("store",)]],
    ]


PLACES = {
    (0, 1): [0, 0, 5, 7, 8, 12],
    (1, 0): [3, 4, 6, 8, 10, 10, 12],
    (1, 1): [3, 4, 6, 7, 8, 10, 12],
    (2, 0): [3, 4, 6, 6, 8, 11, 13],
    (2, 1): [3, 4, 8, 9, 10, 11, 13],
    (3, 0): [5, 6, 7, 9, 11],
    (3, 1): [4, 6, 9, 11, 12],
    (4, 0): [5, 6, 8, 9, 10, 12, 12, 14],
    (4, 1): [5, 6, 6, 8, 8, 9, 11, 12],
    (5, 0): [3, 4, 5, 6, 7, 9, 10, 10, 12, 14],
    (5, 1): [3, 4, 6, 7, 7, 7, 9, 11, 12, 14],
    (6, 0): [3, 4, 5, 5, 7, 8, 10, 11, 12],
    (6, 1): [3, 4, 6, 6, 9, 9, 11, 13, 14],
    (7, 0): [4, 6, 11, 15, 17],
}


def schedule():
    groups = [(a, j, g) for a in range(len(NARROW)) for j in range(PAIR) for g in range(GROUPS)]
    slots, gaps = len(groups) + 2, 4
    between = {(t, k): [] for t in range(slots) for k in range(gaps)}
    before, behind = [], []
    for a, chain in enumerate(chains()):
        for j in range(PAIR):
            pieces = [[(*s, j) for s in piece] for piece in chain]
            if (a, j) == (0, 0):
                before = sum(pieces, [])
            elif (a, j) == (len(NARROW), PAIR - 1):
                behind = sum(pieces, [])
            else:
                last = groups.index((a - 1, j, GROUPS - 1)) if a else -1
                for piece, place in zip(pieces, PLACES[a, j], strict=True):
                    between[last + 1 + place // gaps, place % gaps] += piece
    for k in range(2):
        for j in range(PAIR):
            between[groups.index((2 + k, j, 1)), 2].append(("ffn", k, j))

    steps = [*before, ("heads", *groups[0])]
    for t in range(slots):
        now = groups[t] if t < len(groups) else None
        then = groups[t - 1] if 1 <= t <= len(groups) else None
        if then:
            steps.append(("turn_maxima", *then))
        if now:
            steps.append(("maxima", *now, 0))
        if t >= 2 and not NARROW[groups[t - 2][0]]:
            steps.append(("collect", *groups[t - 2]))
        if then:
            steps.append(("probs", *then, 0))
        steps += between[t, 0]
        if now:
            steps.append(("maxima", *now, 1))
        steps += between[t, 1]
        if then:
            steps.append(("probs", *then, 1))
        steps += between[t, 2]
        if t + 1 < len(groups):
            steps.append(("heads", *groups[t + 1]))
        if then:
            steps.append(("values", *then))
        steps += between[t, 3]
    return steps + behind


TRANSPOSES = {"x0": ("x", "xT"), "craw": ("cx", "crT"), "x1": ("y", "xT"), "cm": ("z", "cT"), "x2": ("x", "xT"),
              "x3": ("y", "xT"), "cn": ("z", "cT"), "x4": ("y", "xT"), "x5": ("y", "xT"), "z4": ("z", "cT"),
              "x6": ("y", "xT"), "z5": ("z", "cT"), "x7": ("y", "xT"), "x8": ("x", "xT"), "x9": ("x", "xT")}
SOURCES = {0: ("x0", "x0"), 1: ("x1", "cm"), 2: ("x3", "x3"), 3: ("x4", "cn"), 4: ("x5", "craw"), 5: ("x6", "x6"),
           6: ("x8", "craw")}


def build_program(nc, w, out):
    STEPS = schedule()
    ctx = ExitStack()
    with ctx:
        def sb(name, shape, dt=F32):
            return ctx.enter_context(nc.sbuf_tensor(name, shape, dt))

        sems = {}

        def sem(name):
            if name not in sems:
                sems[name] = ctx.enter_context(nc.semaphore(name))
            return sems[name]

        W = sb("weights", [P, W_TOTAL])
        ident = sb("ident", [P, P])
        identb = sb("identb", [P, P], BF16)
        causal_st = sb("causal_st", [P, P], BF16)
        causal_ts = sb("causal_ts", [P, P], BF16)
        rope_cos = sb("rope_cos", [P, S])
        rope_sin = sb("rope_sin", [P, S])
        iota = sb("iota", [P, S])
        sel = sb("sel", [P, GH, P], F32R)
        consts = sb("consts", [P, 128])
        rows = sb("rows", [P, 11, D])
        qkw = sb("qkw", [P, 4, DS])
        cols = sb("cols", [P, 12])
        cs_all = sb("cs_all", [P, ITERATIONS, PAIR * ST * 16])
        cs = sb("cs", [P, PAIR * ST, 2, DS])
        setup = sb("setup", [P, 6, 64])
        pos = sb("pos", [P, B * ST], I32)

        nat = {k: sb(f"nat_{k}", [P, PAIR, ST, D]) for k in ("x", "y", "z", "cx")}
        trn = {k: sb(f"trn_{k}", [P, PAIR, S]) for k in ("xT", "cT", "crT")}
        arena = sb("arena", [P, PAIR, 4128])
        tmp = sb("tmp", [P, 1024])
        stacked = sb("stacked", [P, 2, 2, 1024], F32R)
        own_keys = sb("own_keys", [P, NR, GH, S], F32R)
        lo_keys = sb("lo_keys", [P, NR, GH, S], F32R)
        shared_k = sb("shared_k", [P, PAIR, 3, S], F32R)
        small = sb("small", [P, PAIR, 192])
        blockq = sb("blockq", [P, GROUPS, P], F32R)
        nmax = sb("nmax", [P, 2, ST, P])
        nmaxT = sb("nmaxT", [P, 2, S], F32R)
        onat = sb("onat", [P, 2, ST, GH * DH])
        probs = sb("probs", [P, NP, ST * S])

        psum = ctx.enter_context(nc.psum_tensor("psum", [P, 4096], F32))

        def score_bank(n):
            return psum[:, 512 * (n % NSA):512 * (n % NSA) + 512].rearrange("p (s t) -> p s t", s=ST)

        def transposed_slot(n):
            o = 512 * NSA + 512 * (n % NST)
            return psum[:, o:o + 512]

        def span(a, tt):
            first = P if CAUSAL[a] and tt == 1 else 0
            return slice(tt * S, tt * S + S - first), first

        def work_bank(n):
            o = 512 * NSA + 512 * NST + 512 * (n % NWORK)
            return psum[:, o:o + 512]

        def wt(name, c0=0, n=None):
            at, cols_ = W_COLS[name]
            return W[:, at + c0:at + (cols_ if n is None else c0 + n)]

        def qe(j):
            return arena[:, j, 0:1024].rearrange("p (s g i c) -> p s g i c", s=ST, g=GROUPS, i=GH)

        def ke(j):
            return arena[:, j, 1024:2048].rearrange("p (s g i c) -> p s g i c", s=ST, g=GROUPS, i=GH)

        def head_parts(view, st):
            return view[:, st, :, :, 0:24].rearrange("p g i (r d) -> p (g i) r d", r=3)

        def o8T(j):
            return arena[:, j, 1024:2048].rearrange("p (g s) -> p g s", g=GROUPS)

        def v8(j):
            return arena[:, j, 2048:3072].rearrange("p (t h c) -> p t h c", t=ST, h=H)

        def qk_nat(j, n):
            return arena[:, j, 3072 + 512 * n:3584 + 512 * n].rearrange("p (s e) -> p s e", s=ST)

        def hT(j):
            return arena[:, j, 1024:2048].rearrange("p (f s) -> p f s", f=NF)

        def v64(a, j):
            if a == 6:
                return arena[:, j, 0:ST * H * (DH + 1)].rearrange("p (t h c) -> p t h c", t=ST, h=H)
            return arena[:, j, 0:ST * (DH + 1)].rearrange("p (t h c) -> p t h c", t=ST, h=1)

        def o64T(j):
            return arena[:, j, 2080:4128].rearrange("p (c s) -> p c s", c=8)

        def q8T(j):
            return stacked[:, j, 0, :].rearrange("p (g s) -> p g s", g=GROUPS)

        def k8T(j):
            return stacked[:, j, 1, :].rearrange("p (g s) -> p g s", g=GROUPS)

        def wide_q(a, j, g):
            return stacked[:, 0 if a == 6 else j, g % NR, :].rearrange("p (i s) -> p i s", i=GH)

        def wide_k(g):
            return stacked[:, 1, 1 - g % NR, :].rearrange("p (i s) -> p i s", i=GH)

        def key_parts(a, j, g, i):
            if a == 6:
                return wide_k(g)[:, i, :], lo_keys[:, g % NR, i, :]
            return shared_k[:, j, 0, :], shared_k[:, j, 1 + i % 2, :]

        def half(i):
            return slice(DH * (i % 2), DH * (i % 2) + DH)

        def other(i):
            return half(i + 1)

        weights_in = sem("weights_in")
        rows_in = sem("rows_in")
        pos_in = sem("pos_in")
        setup_chain = sem("setup_chain")
        setup_sin = sem("setup_sin")
        loop_first = len(sems)
        tokens_in = sem("tokens_in")
        stored = sem("stored")
        work_full = sem("work_full")
        evacuated = [sem(f"evacuated_{s}") for s in range(NWORK)]
        maxima_full = sem("maxima_full")
        maxima_done = sem("maxima_done")
        scores_full = sem("scores_full")
        probs_full = sem("probs_full")
        scalar_out = sem("scalar_out")
        vector_step = sem("vector_step")
        root_asked = sem("root_asked")
        root_done = sem("root_done")
        inverse_ready = sem("inverse_ready")
        head_roots = sem("head_roots")
        narrow_ready = sem("narrow_ready")
        keys_ready = sem("keys_ready")
        blockq_ready = sem("blockq_ready")
        length_done = sem("length_done")
        ones_ready = sem("ones_ready")
        natural = {t: sem(f"natural_{t}") for t in TRANSPOSES}
        hidden_ready = sem("hidden_ready")
        result_ready = sem("result_ready")

        with nc.Block() as block:
            n_weights = [0]
            n_rows = [0]

            @block.sync
            def _(sp):
                for name, view in w["matrices"]:
                    at = name.split(":")
                    dst = wt(at[0], int(at[1]) if len(at) > 1 else 0, int(at[2]))
                    if len(view.shape) == 3:
                        dst = dst.rearrange("p (t n) -> p t n", t=view.shape[1])
                    sp.dma_start(dst, view).then_inc(weights_in, 16)
                    n_weights[0] += 16

            @block.scalar
            def _(act):
                act.dma_start(pos[:, :], w["pos"]).then_inc(pos_in, 16)
                for dst, src in [(ident[:, :], w["ident"]), (iota[:, :], w["iota"].partition_broadcast(P)),
                                 (rope_cos[:, :], w["rope_cos"]), (rope_sin[:, :], w["rope_sin"]),
                                 (consts[:, :], w["consts"]), (nmax[:, 0, 0, :], w["causal"]),
                                 (nmax[:, 0, 1, :], w["causal_t"]),
                                 (arena[:, 0, 0:512], w["sel"])]:
                    act.dma_start(dst, src).then_inc(rows_in, 16)
                    n_rows[0] += 16
                for n, name in enumerate(["ln1_g", "ln1_b", "ln2_g", "ln2_b", "ln3_g", "ln3_b", "fc2_b", "bo", "b2"]):
                    act.dma_start(rows[:, n, :], w[name].partition_broadcast(P)).then_inc(rows_in, 16)
                    n_rows[0] += 16
                for n, name in enumerate(["ca_qn", "ca_kn", "sa_qn", "sa_kn"]):
                    act.dma_start(qkw[:, n, :], w[name].partition_broadcast(P)).then_inc(rows_in, 16)
                    n_rows[0] += 16
                for n, name in enumerate(["gamma_pt", "gamma_ca", "gamma_ctx", "pre_ca_w", "pre_sa_w", "pre_ffn_w",
                                          "fc1_b"]):
                    act.dma_start(cols[:, n:n + 1], w[name].rearrange("(p o) -> p o", o=1)).then_inc(rows_in, 16)
                    n_rows[0] += 16
                act.dma_start(cols[:, 8:12], w["b1"]).then_inc(rows_in, 16)
                n_rows[0] += 16
                act.wait_ge(setup_sin, 1)
                act.activation(setup[:, 2:4, :], setup[:, 4:6, :], ACT.Sin).then_inc(setup_sin, 1)

            @block.vector
            def _(dve):
                n = [0]

                def link(ins):
                    ins.then_inc(setup_chain, 1)
                    n[0] += 1
                    dve.wait_ge(setup_chain, n[0])

                for zeroed in (own_keys, lo_keys):
                    link(dve.memset(zeroed[:, :, :, :].rearrange("p n i s -> p (n i s)").bitcast(F32), 0.0))
                link(dve.memset(shared_k[:, :, :, :].rearrange("p j n s -> p (j n s)").bitcast(F32), 0.0))
                link(dve.memset(nmaxT[:, :, :].rearrange("p n s -> p (n s)").bitcast(F32), 0.0))
                dve.wait_ge(pos_in, 16)
                dve.wait_ge(rows_in, n_rows[0])
                link(dve.tensor_copy(identb[:, :], ident[:, :]))
                link(dve.tensor_copy(causal_st[:, :], nmax[:, 0, 0, :]))
                link(dve.tensor_copy(causal_ts[:, :], nmax[:, 0, 1, :]))
                link(dve.tensor_copy(sel[:, :, :], arena[:, 0, 0:512].rearrange("p (i m) -> p i m", i=GH)))
                link(dve.memset(nmax[:, :, :, :], 0.0))
                link(dve.tensor_scalar(blockq[:, :, :], arena[:, 0, 0:512].rearrange("p (i m) -> p i m", i=GH), 0.0, None, ALU.mult))
                posf = setup[:, 0, 0:B * ST]
                link(dve.tensor_copy(posf, pos[:, :]))
                ang = setup[:, 1, :].rearrange("p (n f) -> p n f", f=4)
                link(dve.tensor_tensor(ang, posf.unsqueeze(2).broadcast_to([P, B * ST, 4]),
                                       consts[:, 48:52].unsqueeze(1).broadcast_to([P, B * ST, 4]), ALU.mult))
                ang, turns, r = setup[:, 1, :], setup[:, 2, :], setup[:, 4, :]
                link(dve.tensor_scalar(turns, ang, 1.0 / TWO_PI, ROUND, ALU.mult, ALU.add))
                link(dve.tensor_scalar(turns, turns, ROUND, None, ALU.subtract))
                c1 = 6.28125
                c2 = 0.001934051513671875
                c3 = float(TWO_PI - c1 - c2)
                link(dve.scalar_tensor_tensor(r, turns, -c1, ang, ALU.mult, ALU.add))
                link(dve.scalar_tensor_tensor(r, turns, -c2, r, ALU.mult, ALU.add))
                link(dve.scalar_tensor_tensor(r, turns, -c3, r, ALU.mult, ALU.add))
                rc = setup[:, 5, :]
                link(dve.tensor_scalar(rc, r, np.pi / 2, None, ALU.add))
                link(dve.tensor_scalar(turns, rc, np.pi, -TWO_PI, ALU.is_gt, ALU.mult))
                link(dve.tensor_tensor(rc, rc, turns, ALU.add))
                dve.tensor_scalar(setup[:, 4:6, :], setup[:, 4:6, :], 3.1415925, -3.1415925, ALU.min, ALU.max)\
                    .then_inc(setup_sin, 1)
                dve.wait_ge(setup_sin, 2)
                table = cs_all[:, :, :].rearrange("p i (t c r f) -> p (i t) c r f", c=2, r=2, f=4)
                sin4 = setup[:, 2, :].rearrange("p (n f) -> p n f", f=4)
                cos4 = setup[:, 3, :].rearrange("p (n f) -> p n f", f=4)
                link(dve.tensor_copy(table[:, :, 0, 0, :], cos4))
                link(dve.tensor_copy(table[:, :, 0, 1, :], cos4))
                link(dve.tensor_scalar(table[:, :, 1, 0, :], sin4, -1.0, None, ALU.mult))
                link(dve.tensor_copy(table[:, :, 1, 1, :], sin4))
                dve.wait_ge(weights_in, n_weights[0])
                for name, c, c0, m in [("fused", 0, 0, 2176), ("wq", 1, 0, 1024), ("w_ff1", 1, 0, 1024),
                                       ("wkv", 2, 0, 128), ("ca", 3, 0, 128), ("sa", 4, 0, 384),
                                       ("g_w1", 5, 0, 512), ("g_w3", 5, 0, 512)]:
                    link(dve.tensor_scalar(wt(name, c0, m), wt(name, c0, m), cols[:, c:c + 1], None, ALU.mult))
                for dst, src, heads in [("rot", wt("fused", 0, 1024), H), ("k2rot", wt("fused", 1024, 64), 1)]:
                    d4 = wt(dst, 0, heads * DH).rearrange("p (h r c) -> p h r c", r=2, c=DH // 2)
                    s4 = src.rearrange("p (h r c) -> p h r c", r=2, c=DH // 2)
                    link(dve.tensor_scalar(d4[:, :, 0, :], s4[:, :, 1, :], -1.0, None, ALU.mult))
                    link(dve.tensor_copy(d4[:, :, 1, :], s4[:, :, 0, :]))
                for half in range(2):
                    link(dve.tensor_copy(wt("k2", DH * half, DH), wt("fused", 1024, DH)))
                    link(dve.tensor_copy(wt("k2c", DH * half, DH), wt("wkv", 0, DH)))
                link(dve.tensor_copy(wt("k2rot", DH, DH), wt("k2rot", 0, DH)))

        with nc.Fori(0, ITERATIONS, hint_back_edge=True) as it:
            with nc.Block() as block:
                unit = {}
                scalar_count = {}
                score_unit = {}
                trans_unit = {}

                def order(kind):
                    return [s for s in STEPS if s[0] == kind]

                key_unit = {s[1:]: n for n, s in enumerate(s for s in order("heads") if NARROW[s[1]])}

                for _, a, j, g, hp in order("maxima"):
                    for i in (2 * hp, 2 * hp + 1):
                        score_unit[(a, j, g, i)] = len(score_unit)
                for _, a, j, g, hp in order("probs"):
                    for i in (2 * hp, 2 * hp + 1):
                        trans_unit[(a, j, g, i)] = len(trans_unit)

                def wait_evacuated(eng, *key):
                    n = unit[key]
                    eng.wait_ge(evacuated[n % NWORK], n // NWORK + 1)

                def wait_filled(eng, *key):
                    eng.wait_ge(work_full, unit[key] + 1)
                    return work_bank(unit[key])

                def empties(ins, *key):
                    ins.then_inc(evacuated[unit[key] % NWORK], 1)

                @block.tensor
                def _(pe):
                    def work(*key):
                        n = unit[key] = len(unit)
                        if n >= NWORK:
                            pe.wait_ge(evacuated[n % NWORK], n // NWORK)
                        return work_bank(n)

                    def mm(o, l, r, start=True, stop=True):
                        return pe.matmul(o, l, r, start=start, stop=stop)

                    def transpose(tag, j):
                        src, _ = TRANSPOSES[tag]
                        u = work("T", tag, j)
                        pe.wait_ge(natural[tag], j + 1)
                        for st in range(ST):
                            last = pe.transpose(u[:, st * P:(st + 1) * P], nat[src][:, j, st, :], ident[:, :])
                        last.then_inc(work_full, 1)

                    def project8(a, j):
                        qt, kt = SOURCES[a]
                        wait_evacuated(pe, "T", qt, j)
                        wait_evacuated(pe, "T", kt, j)
                        qs, ks = (trn[TRANSPOSES[t][1]] for t in (qt, kt))
                        m = {0: "L0_1", 1: "L0_2", 4: "ca", 5: "sa"}[a]
                        for st in range(ST):
                            u = work("qkv", a, j, st)
                            mm(u[:, 0:128], qs[:, j, st * P:(st + 1) * P], wt(m, 0, 128))
                            mm(u[:, 128:384], ks[:, j, st * P:(st + 1) * P], wt(m, 128, 256)).then_inc(work_full, 1)

                    def turn8(a, j):
                        if a in (4, 5):
                            pe.wait_ge(narrow_ready, PAIR * (a - 4) + j + 1)
                        for what, view in (("tq", qe(j)), ("tk", ke(j))):
                            for st in range(ST):
                                if a in (0, 1):
                                    wait_evacuated(pe, "qkv", a, j, st)
                                u = work(what, a, j, st)
                                for g in range(GROUPS):
                                    last = pe.transpose(u[:, g * P:(g + 1) * P],
                                                        view[:, st, g, :, :].rearrange("p i c -> p (i c)"), ident[:, :])
                                last.then_inc(work_full, 1)

                    def length(a, j):
                        pe.wait_ge(blockq_ready, PAIR * a + j + 1)
                        for st in range(ST):
                            wait_evacuated(pe, "tk", a, j, st)
                        for gp in range(2):
                            u = work("len", a, j, gp)
                            for e in range(2):
                                last = mm(u[:, e * S:(e + 1) * S], blockq[:, 2 * gp + e, :], k8T(j)[:, 2 * gp + e, :])
                            last.then_inc(work_full, 1)

                    def prep64(a, j):
                        kt = SOURCES[a][1]
                        wait_evacuated(pe, "T", kt, j)
                        ks = trn[TRANSPOSES[kt][1]][:, j, :]
                        kw = {2: ["k2", "k2rot"], 3: ["k2c"], 6: None}[a]
                        if a != 6:
                            project("k", kw, ks, a, j, 0, 1)
                        for tt in range(ST):
                            l = ks[:, tt * P:(tt + 1) * P]
                            if a == 6:
                                for half in range(2):
                                    u = work("v", a, j, tt, half)
                                    mm(u[:, :], l, wt("v3", 512 * half, 512)).then_inc(work_full, 1)
                            else:
                                u = work("v", a, j, tt, 0)
                                mm(u[:, 0:DH], l, wt("fused", 1088, DH) if a == 2 else wt("wkv", DH, DH))\
                                    .then_inc(work_full, 1)

                    def project(what, names, src, a, j, c, tiles):
                        for v, name in enumerate(names):
                            u = work(what, a, j, c, v)
                            for e in range(tiles):
                                last = mm(u[:, e * S:(e + 1) * S], wt(name, (c + e) * P, P), src)
                            last.then_inc(work_full, 1)

                    def heads(a, j, g):
                        if NARROW[a]:
                            return
                        qt, kt = SOURCES[a]
                        wait_evacuated(pe, "T", qt, j)
                        qs, ks = (trn[TRANSPOSES[t][1]][:, j, :] for t in (qt, kt))
                        project("q", {2: ["fused", "rot"], 3: ["wq"], 6: ["q3"]}[a], qs, a, j, 2 * g, 2)
                        if a == 6:
                            project("k", ["k3"], ks, a, j, 2 * g, 2)

                    def maxima(a, j, g, hp):
                        if g == 0 and hp == 0 and NARROW[a]:
                            for st in range(ST):
                                wait_evacuated(pe, "tq", a, j, st)
                                wait_evacuated(pe, "tk", a, j, st)
                        if NARROW[a]:
                            pe.wait_ge(keys_ready, key_unit[(a, j, g)] + 1)
                        else:
                            wait_evacuated(pe, "q", a, j, 2 * g, 1 if a == 2 else 0)
                            wait_evacuated(pe, "k", a, j, 2 * g if a == 6 else 0, 1 if a == 2 else 0)
                        for i in (2 * hp, 2 * hp + 1):
                            n = score_unit[(a, j, g, i)]
                            if n >= NSA:
                                pe.wait_ge(maxima_done, n - NSA + 1)
                            bank = score_bank(n)
                            for st in range(ST):
                                t1 = P if CAUSAL[a] and st == 0 else S
                                if NARROW[a]:
                                    l, m = q8T(j)[:, g, st * P:(st + 1) * P], own_keys[:, key_unit[(a, j, g)] % NR, i, 0:t1]
                                else:
                                    l, m = wide_q(a, j, g)[:, i, st * P:(st + 1) * P], key_parts(a, j, g, i)[0][:, 0:t1]
                                last = mm(bank[:, st, 0:t1], l, m, stop=not CAUSAL[a])
                                if CAUSAL[a]:
                                    last = mm(bank[:, st, t1 - P:t1], identb[:, :], causal_st[:, :], start=False)
                            last.then_inc(maxima_full, 1)

                    def turn_maxima(a, j, g):
                        u = work("max", a, j, g)
                        pe.wait_ge(maxima_done, score_unit[(a, j, g, GH - 1)] + 1)
                        for st in range(ST):
                            src = qe(j)[:, st, g, :, :].rearrange("p i c -> p (i c)") if NARROW[a] else nmax[:, g % 2, st, :]
                            last = pe.transpose(u[:, st * P:(st + 1) * P], src, ident[:, :])
                        last.then_inc(work_full, 1)

                    def probs_(a, j, g, hp):
                        wait_evacuated(pe, "max", a, j, g)
                        for i in (2 * hp, 2 * hp + 1):
                            n = trans_unit[(a, j, g, i)]
                            if n >= NST:
                                pe.wait_ge(probs_full, n - NST + 1)
                            for tt in range(ST):
                                at, s0 = span(a, tt)
                                o = transposed_slot(n)[:, at]
                                if NARROW[a]:
                                    last = mm(o, own_keys[:, key_unit[(a, j, g)] % NR, i, tt * P:(tt + 1) * P],
                                              q8T(j)[:, g, s0:S], stop=not CAUSAL[a])
                                else:
                                    hi, lo = (k[:, tt * P:(tt + 1) * P] for k in key_parts(a, j, g, i))
                                    mm(o, hi, wide_q(a, j, g)[:, i, s0:S], stop=False)
                                    mm(o, lo, wide_q(a, j, g)[:, i, s0:S], start=False, stop=False)
                                    last = mm(o, sel[:, i, :], nmaxT[:, g % 2, s0:S], start=False, stop=not CAUSAL[a])
                                if CAUSAL[a]:
                                    last = mm(o[:, 0:P], identb[:, :], causal_ts[:, :], start=False)
                            last.then_inc(scores_full, 1)

                    def values(a, j, g):
                        n0 = trans_unit[(a, j, g, 0)]
                        pe.wait_ge(probs_full, n0 + GH)
                        if NARROW[a]:
                            u = work("o", a, j, g)
                            for tt in range(ST):
                                at, s0 = span(a, tt)
                                for i in range(GH):
                                    last = mm(u[BLK * i:BLK * i + BLK, s0:S], v8(j)[:, tt, GH * g + i, :],
                                              probs[:, (n0 + i) % NP, at], start=tt == 0, stop=tt == 1)
                            last.then_inc(work_full, 1)
                            return
                        if g == 0:
                            pe.wait_ge(ones_ready, PAIR * {2: 0, 3: 1, 6: 2}[a] + j + 1)
                            for tt in range(ST):
                                for half in range(2 if a == 6 else 1):
                                    wait_evacuated(pe, "v", a, j, tt, half)
                        for st in range(ST):
                            u = work("o", a, j, g, st)
                            tiles = [0] if CAUSAL[a] and st == 0 else [0, 1]
                            for i in range(GH):
                                for tt in tiles:
                                    at, s0 = span(a, tt)
                                    c = at.start + st * P - s0
                                    last = mm(u[:, i * 65:i * 65 + 65], probs[:, (n0 + i) % NP, c:c + P],
                                              v64(a, j)[:, tt, GH * g + i if a == 6 else 0, :],
                                              start=tt == 0, stop=tt == tiles[-1])
                            last.then_inc(work_full, 1)

                    def collect(a, j, g):
                        for st in range(ST):
                            wait_evacuated(pe, "o", a, j, g, st)
                        u = work("oT", a, j, g)
                        for c in range(2):
                            for st in range(ST):
                                last = pe.transpose(u[:, (2 * c + st) * P:(2 * c + st + 1) * P],
                                                    onat[:, g % 2, st, c * P:(c + 1) * P], ident[:, :])
                        last.then_inc(work_full, 1)

                    def finish8(a, j):
                        for g in range(GROUPS):
                            wait_evacuated(pe, "o", a, j, g)
                        for st in range(ST):
                            u = work("z", a, j, st)
                            for g in range(GROUPS):
                                last = pe.transpose(u[:, g * P:(g + 1) * P], o8T(j)[:, g, st * P:(st + 1) * P], ident[:, :])
                            last.then_inc(work_full, 1)

                    def finish64(a, j):
                        for g in range(GROUPS):
                            wait_evacuated(pe, "oT", a, j, g)
                        u = work("y", a, j)
                        wo = {2: "attn_out", 3: "w_out", 6: "o3"}[a]
                        terms = [(o64T(j)[:, c, :], wt(wo, c * P, P)) for c in range(8)]
                        if a != 6:
                            pe.wait_ge(hidden_ready, PAIR * NF * (a - 2) + NF * (j + 1))
                            terms += [(hT(j)[:, f, :], wt("ff_out" if a == 2 else "w_ff2", f * P, P)) for f in range(NF)]
                        for st in range(ST):
                            for n, (l, r) in enumerate(terms):
                                last = mm(u[:, st * P:(st + 1) * P], l[:, st * P:(st + 1) * P], r,
                                          start=n == 0, stop=n == len(terms) - 1)
                        last.then_inc(work_full, 1)

                    def ffn(k, j):
                        tag = {0: "x3", 1: "x4", 2: "x7"}[k]
                        wait_evacuated(pe, "T", tag, j)
                        for f in range(NF):
                            u = work("ff", k, j, f)
                            if k == 2:
                                val, gate = wt("g_w3", f * P, P), wt("g_w1", f * P, P)
                            else:
                                name, c0 = ("fused", 1152) if k == 0 else ("w_ff1", 0)
                                val, gate = wt(name, c0 + f * P, P), wt(name, c0 + FF + f * P, P)
                            mm(u[:, 0:S], val, trn["xT"][:, j, :])
                            mm(u[:, S:2 * S], gate, trn["xT"][:, j, :]).then_inc(work_full, 1)

                    def ffn_out(k, j):
                        if k == 2:
                            pe.wait_ge(hidden_ready, PAIR * NF * 2 + NF * (j + 1))
                        else:
                            for f in range(NF):
                                wait_evacuated(pe, "h", j, f)
                        u = work("fo", k, j)
                        name = "g_w2" if k == 2 else "w2_3"
                        for st in range(ST):
                            for f in range(NF):
                                last = mm(u[:, st * P:(st + 1) * P], hT(j)[:, f, st * P:(st + 1) * P], wt(name, f * P, P),
                                          start=f == 0, stop=f == NF - 1)
                        last.then_inc(work_full, 1)

                    def gelu(j):
                        wait_evacuated(pe, "T", "x9", j)
                        for f in range(NF):
                            u = work("h", j, f)
                            mm(u[:, 0:S], wt("w1_3", f * P, P), trn["xT"][:, j, :]).then_inc(work_full, 1)

                    def fc(j):
                        wait_evacuated(pe, "T", "x2", j)
                        u = work("fc1", j)
                        mm(u[:, 0:S], wt("fc1"), trn["xT"][:, j, :]).then_inc(work_full, 1)
                        wait_evacuated(pe, "fc1", j)
                        u = work("fc2", j)
                        for st in range(ST):
                            last = mm(u[:, st * P:(st + 1) * P], hT(j)[:, 0, st * P:(st + 1) * P], wt("fc2"))
                        last.then_inc(work_full, 1)

                    def outproj(a, j):
                        wait_evacuated(pe, "T", f"z{a}", j)
                        u = work("y", a, j)
                        for st in range(ST):
                            last = mm(u[:, st * P:(st + 1) * P], trn["cT"][:, j, st * P:(st + 1) * P],
                                      wt("ca_o" if a == 4 else "sa_o"))
                        last.then_inc(work_full, 1)

                    stages = dict(transpose=transpose, project8=project8, turn8=turn8, length=length, prep64=prep64, heads=heads,
                                  turn_maxima=turn_maxima, maxima=maxima, probs=probs_, values=values, collect=collect,
                                  finish8=finish8, finish64=finish64,
                                  ffn=ffn, ffn_out=ffn_out, gelu=gelu, fc=fc, outproj=outproj)
                    for kind, *args in STEPS:
                        if kind in stages:
                            stages[kind](*args)

                @block.scalar
                def _(act):
                    done = [0]
                    group_done = {n: unit[("o", *k[:3])] if NARROW[k[0]] else unit[("o", *k[:3], ST - 1)]
                                  for k, n in trans_unit.items()}

                    def to_vector(ins, *key):
                        ins.then_inc(scalar_out, 1)
                        done[0] += 1
                        scalar_count[key] = done[0]

                    def transpose(tag, j):
                        u = wait_filled(act, "T", tag, j)
                        empties(act.activation(trn[TRANSPOSES[tag][1]][:, j, :], u[:, 0:S], ACT.Copy), "T", tag, j)

                    def project8(a, j):
                        for st in range(ST):
                            key = ("qkv", a, j, st)
                            u = wait_filled(act, *key)
                            heads = u[:, 0:384].rearrange("p (x h d) -> p x h d", x=3, d=DS)
                            act.activation(v8(j)[:, st, :, 0:DS], heads[:, 2], ACT.Copy)
                            if a < 2:
                                for view, x, slots in ((qe(j), 0, (0, 1)), (ke(j), 1, (0, 2))):
                                    hp = head_parts(view, st)
                                    o = hp[:, :, slots[0]:slots[1] + 1:slots[1] - slots[0], :]
                                    last = act.activation(o.bitcast(F32R), heads[:, x].unsqueeze(2).broadcast_to([P, H, 2, DS]), ACT.Copy)
                                to_vector(last, *key)
                            else:
                                empties(act.activation(qk_nat(j, 0)[:, st, :], u[:, 0:256], ACT.Copy), *key)

                    def norm8(a, j):
                        act.wait_ge(inverse_ready, PAIR * (a - 4) + j + 1)
                        act.activation(small[:, j, 64:128], small[:, j, 64:128], ACT.Sqrt).then_inc(head_roots, 1)

                    def turn8(a, j):
                        for what, dst in (("tq", q8T(j)), ("tk", k8T(j))):
                            for st in range(ST):
                                u = wait_filled(act, what, a, j, st)
                                empties(act.activation(dst[:, :, st * P:(st + 1) * P],
                                                       u.rearrange("p (g s) -> p g s", g=GROUPS), ACT.Copy), what, a, j, st)

                    def prep64(a, j):
                        if a == 3:
                            u = wait_filled(act, "k", a, j, 0, 0)
                            to_vector(act.activation(shared_k[:, j, 0, :], u[:, 0:S], ACT.Copy), "k", a, j, 0)
                        for tt in range(ST):
                            for half in range(2 if a == 6 else 1):
                                u = wait_filled(act, "v", a, j, tt, half)
                                k = 8 if a == 6 else 1
                                empties(act.activation(v64(a, j)[:, tt, 8 * half:8 * half + k, 0:DH],
                                                       u[:, 0:k * DH].rearrange("p (h d) -> p h d", d=DH), ACT.Copy),
                                        "v", a, j, tt, half)

                    def heads(a, j, g):
                        if NARROW[a]:
                            if a < 2:
                                act.wait_ge(length_done, PAIR * a + j + 1)
                            else:
                                for st in range(ST):
                                    wait_evacuated(act, "tk", a, j, st)
                            for i in range(GH):
                                r = slice(BLK * i, BLK * i + BLK)
                                last = act.activation(own_keys[r, key_unit[(a, j, g)] % NR, i, :],
                                                      k8T(j)[r, g, :].bitcast(F32), ACT.Copy)
                            last.then_inc(keys_ready, 1)
                            return
                        if a == 2:
                            return
                        for what in ("q", "k") if a == 6 else ("q",):
                            u = wait_filled(act, what, a, j, 2 * g, 0).rearrange("p (c s) -> p c s", c=2)
                            dst = wide_q(a, j, g) if what == "q" else wide_k(g)
                            for i in range(2):
                                last = act.activation(dst[half(i), i::2, :], u[half(i)], ACT.Copy)
                                if what == "k":
                                    last = act.activation(dst[other(i), i::2, :], u[half(i)], ACT.Copy)
                            to_vector(last, what, a, j, g)

                    def probs_(a, j, g, hp):
                        for i in (2 * hp, 2 * hp + 1):
                            n = trans_unit[(a, j, g, i)]
                            act.wait_ge(scores_full, n + 1)
                            if n >= NP:
                                act.wait_ge(work_full, group_done[n - NP] + 1)
                            c = span(a, 1)[0].stop
                            act.activation(probs[:, n % NP, 0:c], transposed_slot(n)[:, 0:c], ACT.Exp,
                                           scale=float(SCALE[a])).then_inc(probs_full, 1)

                    def values(a, j, g):
                        if NARROW[a]:
                            u = wait_filled(act, "o", a, j, g)
                            empties(act.activation(o8T(j)[:, g, :], u[:, 0:S], ACT.Copy), "o", a, j, g)

                    def collect(a, j, g):
                        u = wait_filled(act, "oT", a, j, g)
                        empties(act.activation(o64T(j)[:, 2 * g:2 * g + 2, :],
                                               u.rearrange("p (c s) -> p c s", c=2), ACT.Copy), "oT", a, j, g)

                    def ffn(k, j):
                        for f in range(NF):
                            u = wait_filled(act, "ff", k, j, f)
                            to_vector(act.activation(hT(j)[:, f, :], u[:, S:2 * S], ACT.Silu), "ff", k, j, f)

                    def gelu(j):
                        for f in range(NF):
                            u = wait_filled(act, "h", j, f)
                            empties(act.activation(hT(j)[:, f, :], u[:, 0:S], ACT.Gelu, bias=cols[:, 8 + f:9 + f]), "h", j, f)

                    def fc(j):
                        u = wait_filled(act, "fc1", j)
                        empties(act.activation(hT(j)[:, 0, :], u[:, 0:S], ACT.Relu, bias=cols[:, 6:7]), "fc1", j)

                    stages = dict(transpose=transpose, project8=project8, norm8=norm8, turn8=turn8, prep64=prep64, heads=heads, probs=probs_, values=values,
                                  collect=collect, ffn=ffn, gelu=gelu, fc=fc)
                    for kind, *args in STEPS:
                        if kind in stages:
                            stages[kind](*args)

                @block.vector
                def _(dve):
                    chain = [0]

                    def link(ins):
                        ins.then_inc(vector_step, 1)
                        chain[0] += 1
                        dve.wait_ge(vector_step, chain[0])

                    def signal(ins, s, value):
                        ins.then_inc(s, 1)
                        dve.wait_ge(s, value)

                    asked = [0]

                    def inverse_root(ins):
                        ins.then_inc(root_asked, 1)
                        asked[0] += 1
                        dve.wait_ge(root_done, asked[0])

                    def row(n):
                        return rows[:, n, :].unsqueeze(1).broadcast_to([P, ST, D])

                    def statistics(j, src, eps, mean):
                        sm = small[:, j, :]
                        if mean:
                            for st in range(ST):
                                last = dve.bn_stats(sm[:, 8 + 6 * st:14 + 6 * st], src[:, j, st, :])
                            link(last)
                            for st in range(ST):
                                last = dve.bn_aggr(sm[:, 4 + 2 * st:6 + 2 * st], sm[:, 8 + 6 * st:14 + 6 * st])
                            link(last)
                            mv = sm[:, 4:8].rearrange("p (s c) -> p s c", c=2)
                            dve.tensor_copy(sm[:, 0:2], mv[:, :, 0])
                            inverse_root(dve.tensor_scalar(sm[:, 2:4], mv[:, :, 1], eps, None, ALU.add))
                        else:
                            sq = tmp[:, 0:S].rearrange("p (s d) -> p s d", s=ST)
                            link(dve.tensor_tensor(sq, src[:, j], src[:, j], ALU.mult))
                            link(dve.tensor_reduce(sm[:, 4:6], sq, axis=AX, op=ALU.add))
                            inverse_root(dve.tensor_scalar(sm[:, 2:4], sm[:, 4:6], 1.0 / D, eps, ALU.mult, ALU.add))

                    def normed(j, src, dst, mean=True, eps=EPS_LN):
                        statistics(j, src, eps, mean)
                        sm = small[:, j, :]
                        for st in range(ST):
                            if mean:
                                last = dve.tensor_scalar(dst[:, j, st, :], src[:, j, st, :], sm[:, st:st + 1],
                                                         sm[:, 2 + st:3 + st], ALU.subtract, ALU.mult)
                            else:
                                last = dve.tensor_scalar(dst[:, j, st, :], src[:, j, st, :], sm[:, 2 + st:3 + st], None, ALU.mult)
                        return last

                    def start(j):
                        if j == 0:
                            dve.wait_ge(tokens_in, 32)
                            link(dve.tensor_copy(cs[:, :, :, :].rearrange("p t c d -> p (t c d)").unsqueeze(1),
                                                 cs_all[:, bass.ds(it, 1), :]))
                        token_mask(j, nat["x"], 24)
                        signal(dve.tensor_copy(small[:, j, 30:31], small[:, j, 24:25]), natural["x0"], j + 1)
                        dve.tensor_copy(small[:, j, 31:32], small[:, j, 24:25]).then_inc(natural["craw"], 1)

                    def token_mask(j, src, at):
                        sm = small[:, j, :]
                        link(dve.tensor_reduce(sm[:, at + 2:at + 4], src[:, j], axis=AX, op=ALU.max, apply_absolute_value=True))
                        link(dve.tensor_scalar(sm[:, at:at + 2], sm[:, at + 2:at + 4], 0.0, None, ALU.not_equal))

                    def pads(j):
                        q_, k_ = (view.rearrange("p s g i c -> p (s g i) c")[:, :, 24:32] for view in (qe(j), ke(j)))
                        dve.tensor_copy(q_, consts[:, 8:16].unsqueeze(1).broadcast_to([P, 32, 8]))
                        dve.tensor_copy(k_, consts[:, 16:24].unsqueeze(1).broadcast_to([P, 32, 8]))
                        link(dve.tensor_copy(v8(j).rearrange("p t h c -> p (t h) c")[:, :, 8:32],
                                        consts[:, 24:48].unsqueeze(1).broadcast_to([P, 32, 24])))

                    def project8(a, j):
                        pads(j)
                        if a < 2:
                            for st in range(ST):
                                key = ("qkv", a, j, st)
                                wait_filled(dve, *key)
                                u = work_bank(unit[key])
                                dve.wait_ge(scalar_out, scalar_count[key])
                                heads = u[:, 0:256].rearrange("p (x h d) -> p x h d", x=2, d=DS)
                                for view, x, lo in ((qe(j), 0, 2), (ke(j), 1, 1)):
                                    hp = head_parts(view, st)
                                    last = dve.tensor_tensor(hp[:, :, lo, :].bitcast(F32R), heads[:, x], hp[:, :, 0, :], ALU.subtract)
                                empties(last, *key)

                    def norm8(a, j):
                        for st in range(ST):
                            wait_evacuated(dve, "qkv", a, j, st)
                        X, Y = qk_nat(j, 0), qk_nat(j, 1)
                        X3, Y3 = (v.rearrange("p s (n d) -> p (s n) d", d=DS) for v in (X, Y))
                        ms = small[:, j, 64:128]
                        link(dve.tensor_tensor(Y, X, X, ALU.mult))
                        link(dve.tensor_reduce(ms, Y3, axis=AX, op=ALU.add))
                        link(dve.tensor_scalar(ms, ms, 1.0 / DS, EPS_RMS, ALU.mult, ALU.add))
                        dve.reciprocal(ms, ms).then_inc(inverse_ready, 1)
                        dve.wait_ge(head_roots, PAIR * (a - 4) + j + 1)
                        link(dve.tensor_tensor(X3, X3, ms.unsqueeze(2).broadcast_to([P, 64, DS]), ALU.mult))
                        for x in range(2):
                            v = X[:, :, 128 * x:128 * x + 128].rearrange("p s (n d) -> p s n d", d=DS)
                            g_ = qkw[:, 2 * (a - 4) + x, :].unsqueeze(1).unsqueeze(1).broadcast_to([P, ST, H, DS])
                            last = dve.tensor_tensor(v, v, g_, ALU.mult)
                        link(last)

                    def rope8(a, j):
                        X, Y = qk_nat(j, 0), qk_nat(j, 1)
                        Z = tmp[:, 0:512].rearrange("p (s e) -> p s e", s=ST)
                        for st in range(ST):
                            x3, y3, z3 = (v[:, st, :].rearrange("p (n d) -> p n d", d=DS) for v in (X, Y, Z))
                            c_, s_ = (cs[:, ST * j + st, m, :].unsqueeze(1).broadcast_to([P, 32, DS]) for m in (0, 1))
                            dve.tensor_tensor(y3, x3, c_, ALU.mult)
                            dve.tensor_tensor(z3[:, :, 0:4], x3[:, :, 4:8], s_[:, :, 0:4], ALU.mult)
                            last = dve.tensor_tensor(z3[:, :, 4:8], x3[:, :, 0:4], s_[:, :, 4:8], ALU.mult)
                        link(last)
                        link(dve.tensor_tensor(X, Y, Z, ALU.add))

                    def split8(a, j):
                        X = qk_nat(j, 0)
                        parts = [(head_parts(view, st), X[:, st, 128 * x:128 * x + 128].rearrange("p (h d) -> p h d", d=DS), slots, lo)
                                 for st in range(ST)
                                 for view, x, slots, lo in ((qe(j), 0, (0, 1), 2), (ke(j), 1, (0, 2), 1))]
                        for hp, src, slots, _ in parts:
                            o = hp[:, :, slots[0]:slots[1] + 1:slots[1] - slots[0], :]
                            last = dve.tensor_copy(o.bitcast(F32R), src.unsqueeze(2).broadcast_to([P, H, 2, DS]))
                        link(last)
                        for hp, src, _, lo in parts:
                            last = dve.tensor_tensor(hp[:, :, lo, :].bitcast(F32R), src, hp[:, :, 0, :], ALU.subtract)
                        signal(last, narrow_ready, PAIR * (a - 4) + j + 1)

                    def length(a, j):
                        wait_evacuated(dve, "tq", a, j, 0)
                        if (a, j) != (0, 0):
                            pa, pj = (a, j - 1) if j else (a - 1, 1)
                            wait_filled(dve, "len", pa, pj, 1)
                        cols25 = blockq[:, :, :].rearrange("p g (i c) -> p g i c", i=GH)[:, :, :, COL_LEN]
                        first = q8T(j)[:, :, 0:1].bitcast(F32).broadcast_to([P, GROUPS, GH])
                        signal(dve.tensor_tensor(cols25, first, consts[:, 0:4].unsqueeze(1).broadcast_to([P, GROUPS, GH]), ALU.mult),
                               blockq_ready, PAIR * a + j + 1)
                        ln = small[:, j, 32:36]
                        for gp in range(2):
                            u = wait_filled(dve, "len", a, j, gp)
                            t = tmp[:, 0:512]
                            signal(dve.tensor_scalar(t, u, 0.0, None, ALU.not_equal),
                                   evacuated[unit[("len", a, j, gp)] % NWORK], unit[("len", a, j, gp)] // NWORK + 1)
                            link(dve.tensor_reduce(ln[:, 2 * gp:2 * gp + 2], t.rearrange("p (e t) -> p e t", e=2), axis=AX, op=ALU.add))

                    def mask(a, j):
                        ln = small[:, j, 32:36]
                        lm = tmp[:, :].rearrange("p (g t) -> p g t", g=GROUPS)
                        for g in range(GROUPS):
                            last = dve.tensor_scalar(lm[:, g, :], iota[:, :], ln[:, g:g + 1], consts[:, 4:5], ALU.is_ge, ALU.mult)
                        link(last)
                        signal(dve.tensor_tensor(k8T(j), k8T(j).bitcast(F32), lm, ALU.add), length_done, PAIR * a + j + 1)

                    def prep64(a, j):
                        ones = v64(a, j)[:, :, :, DH:DH + 1].rearrange("p t h c -> p (t h) c")
                        n = ones.shape[1]
                        signal(dve.tensor_copy(ones, consts[:, 24:25].unsqueeze(1).broadcast_to([P, n, 1])),
                               ones_ready, PAIR * {2: 0, 3: 1, 6: 2}[a] + j + 1)
                        hi, *lo = (shared_k[:, j, m, :] for m in range(3))
                        if a == 2:
                            t = turned("k", a, j, 0, 1)[:, 0, :]
                            link(dve.tensor_copy(hi, t))
                        elif a == 3:
                            t = wait_filled(dve, "k", a, j, 0, 0)[:, 0:S]
                            dve.wait_ge(scalar_out, scalar_count[("k", a, j, 0)])
                        if a != 6:
                            n = unit[("k", a, j, 0, 1 if a == 2 else 0)]
                            for i in range(2):
                                last = dve.tensor_tensor(lo[i][half(i)], t[half(i)], hi[half(i)].bitcast(F32), ALU.subtract)
                            signal(last, evacuated[n % NWORK], n // NWORK + 1)

                    def heads(a, j, g):
                        if NARROW[a]:
                            return
                        q = wide_q(a, j, g)
                        if a == 2:
                            t = turned("q", a, j, 2 * g, 2)
                            for i in range(2):
                                last = dve.tensor_copy(q[half(i), i::2, :], t[half(i)])
                            link(last)
                            n = unit[("q", a, j, 2 * g, 1)]
                        else:
                            t = wait_filled(dve, "q", a, j, 2 * g, 0).rearrange("p (c s) -> p c s", c=2)
                            dve.wait_ge(scalar_out, scalar_count[("q", a, j, g)])
                            n = unit[("q", a, j, 2 * g, 0)]
                        for i in range(2):
                            last = dve.tensor_tensor(q[other(i), i::2, :], t[half(i)], q[half(i), i::2, :].bitcast(F32), ALU.subtract)
                        signal(last, evacuated[n % NWORK], n // NWORK + 1)
                        if a == 6:
                            key = ("k", a, j, 2 * g, 0)
                            t = wait_filled(dve, *key).rearrange("p (c s) -> p c s", c=2)
                            dve.wait_ge(scalar_out, scalar_count[("k", a, j, g)])
                            for i in range(2):
                                last = dve.tensor_tensor(lo_keys[half(i), g % NR, i::2, :], t[half(i)],
                                                         wide_k(g)[half(i), i::2, :].bitcast(F32), ALU.subtract)
                            empties(last, *key)

                    def turned(what, a, j, c, k):
                        t = [tmp[:, 512 * v:512 * v + k * S].rearrange("p (c s) -> p c s", c=k) for v in range(2)]
                        for v, table in enumerate((rope_cos, rope_sin)):
                            u = wait_filled(dve, what, a, j, c, v)[:, 0:k * S].rearrange("p (c s) -> p c s", c=k)
                            n = unit[(what, a, j, c, v)]
                            ins = dve.tensor_tensor(t[v], u, table[:, :].unsqueeze(1).broadcast_to([P, k, S]), ALU.mult)
                            if v == 0:
                                signal(ins, evacuated[n % NWORK], n // NWORK + 1)
                            else:
                                link(ins)
                        link(dve.tensor_tensor(t[0], t[0], t[1], ALU.add))
                        return t[0]

                    def maxima(a, j, g, hp):
                        for i in (2 * hp, 2 * hp + 1):
                            n = score_unit[(a, j, g, i)]
                            dve.wait_ge(maxima_full, n + 1)
                            o = qe(j)[:, :, g, i, COL_MAX] if NARROW[a] else nmax[:, g % 2, :, i]
                            bank = score_bank(n)
                            if CAUSAL[a]:
                                dve.tensor_reduce(o[:, 0:1], bank[:, 0, 0:P], axis=AX, op=ALU.max, negate=True)
                                dve.tensor_reduce(o[:, 1:2], bank[:, 1, :], axis=AX, op=ALU.max, negate=True)\
                                    .then_inc(maxima_done, 1)
                            else:
                                dve.tensor_reduce(o, bank, axis=AX, op=ALU.max, negate=True).then_inc(maxima_done, 1)

                    def turn_maxima(a, j, g):
                        u = wait_filled(dve, "max", a, j, g)
                        if NARROW[a]:
                            empties(dve.tensor_scalar(q8T(j)[:, g, :], u[:, 0:S], MAX_GUARD, None, ALU.min), "max", a, j, g)
                        else:
                            empties(dve.tensor_scalar(nmaxT[0:GH, g % 2, :], u[0:GH, 0:S], MAX_GUARD, None, ALU.min), "max", a, j, g)

                    def values(a, j, g):
                        if NARROW[a]:
                            return
                        for st in range(ST):
                            u = wait_filled(dve, "o", a, j, g, st)[:, 0:GH * 65].rearrange("p (h c) -> p h c", h=GH)
                            rec = small[:, j, 40 + 4 * st:44 + 4 * st]
                            link(dve.reciprocal(rec, u[:, :, DH]))
                            empties(dve.tensor_tensor(onat[:, g % 2, st, :].rearrange("p (h d) -> p h d", h=GH), u[:, :, 0:DH],
                                                      rec.unsqueeze(2).broadcast_to([P, GH, DH]), ALU.mult), "o", a, j, g, st)

                    def finish8(a, j):
                        for st in range(ST):
                            u = wait_filled(dve, "z", a, j, st).rearrange("p (h c) -> p h c", h=H)
                            rec = small[:, j, 128 + 16 * st:144 + 16 * st]
                            link(dve.reciprocal(rec, u[:, :, DS]))
                            if a < 2:
                                m = (24 if a == 0 else 56) + st
                                link(dve.tensor_scalar(rec, rec, small[:, j, m:m + 1], None, ALU.mult))
                            n = unit[("z", a, j, st)]
                            signal(dve.tensor_tensor(nat["z"][:, j, st, :].rearrange("p (h d) -> p h d", h=H), u[:, :, 0:DS],
                                                     rec.unsqueeze(2).broadcast_to([P, H, DS]), ALU.mult),
                                   evacuated[n % NWORK], n // NWORK + 1)
                        if a in (4, 5):
                            dve.tensor_copy(small[:, j, 30:31], small[:, j, 24:25]).then_inc(natural[f"z{a}"], 1)

                    def add_unit(j, *key):
                        u = wait_filled(dve, *key)[:, 0:S].rearrange("p (s d) -> p s d", s=ST)
                        n = unit[key]
                        signal(dve.tensor_tensor(nat["x"][:, j], nat["x"][:, j], u, ALU.add), evacuated[n % NWORK], n // NWORK + 1)

                    def norm_l0a(j):
                        link(dve.tensor_tensor(nat["z"][:, j], nat["z"][:, j], nat["x"][:, j], ALU.add))
                        link(normed(j, nat["z"], nat["y"]))
                        link(dve.tensor_tensor(nat["y"][:, j], nat["y"][:, j], row(0), ALU.mult))
                        signal(dve.tensor_tensor(nat["y"][:, j], nat["y"][:, j], row(1), ALU.add), natural["x1"], j + 1)
                        token_mask(j, nat["y"], 56)
                        for st in range(ST):
                            last = dve.tensor_scalar(nat["z"][:, j, st, :], nat["cx"][:, j, st, :], small[:, j, 56 + st:57 + st], None, ALU.mult)
                        last.then_inc(natural["cm"], 1)

                    def norm_l0b(j):
                        link(dve.tensor_tensor(nat["z"][:, j], nat["z"][:, j], nat["y"][:, j], ALU.add))
                        link(normed(j, nat["z"], nat["x"]))
                        link(dve.tensor_tensor(nat["x"][:, j], nat["x"][:, j], row(2), ALU.mult))
                        signal(dve.tensor_tensor(nat["x"][:, j], nat["x"][:, j], row(3), ALU.add), natural["x2"], j + 1)

                    def norm_l0c(j):
                        u = wait_filled(dve, "fc2", j)[:, 0:S].rearrange("p (s d) -> p s d", s=ST)
                        n = unit[("fc2", j)]
                        signal(dve.tensor_tensor(nat["z"][:, j], u, row(6), ALU.add), evacuated[n % NWORK], n // NWORK + 1)
                        for st in range(ST):
                            last = dve.scalar_tensor_tensor(nat["z"][:, j, st, :], nat["z"][:, j, st, :], small[:, j, 24 + st:25 + st],
                                                            nat["x"][:, j, st, :], ALU.mult, ALU.add)
                        link(last)
                        link(normed(j, nat["z"], nat["x"]))
                        link(dve.tensor_tensor(nat["x"][:, j], nat["x"][:, j], row(4), ALU.mult))
                        link(dve.tensor_tensor(nat["x"][:, j], nat["x"][:, j], row(5), ALU.add))

                    def norm_x3(j):
                        signal(normed(j, nat["x"], nat["y"]), natural["x3"], j + 1)

                    def norm_cn(j):
                        signal(normed(j, nat["cx"], nat["z"]), natural["cn"], j + 1)

                    def norm_l1(j):
                        signal(normed(j, nat["x"], nat["y"]), natural["x4"], j + 1)

                    def rms_(tag, j):
                        signal(normed(j, nat["x"], nat["y"], mean=False, eps=EPS_RMS), natural[tag], j + 1)

                    def ffn(k, j):
                        for f in range(NF):
                            u = wait_filled(dve, "ff", k, j, f)
                            dve.wait_ge(scalar_out, scalar_count[("ff", k, j, f)])
                            h = hT(j)[:, f, :]
                            n = unit[("ff", k, j, f)]
                            signal(dve.tensor_tensor(h, h, u[:, 0:S], ALU.mult), evacuated[n % NWORK], n // NWORK + 1)
                            dve.tensor_copy(small[:, j, 30:31], small[:, j, 24:25]).then_inc(hidden_ready, 1)

                    def copy_l3(j):
                        add_unit(j, "fo", 2, j)
                        dve.tensor_copy(small[:, j, 30:31], small[:, j, 24:25]).then_inc(natural["x8"], 1)

                    def bias_l3(j):
                        signal(dve.tensor_tensor(nat["x"][:, j], nat["x"][:, j], row(7), ALU.add), natural["x9"], j + 1)

                    def store(j):
                        add_unit(j, "fo", 3, j)
                        dve.tensor_tensor(nat["y"][:, j], nat["x"][:, j], row(8), ALU.add).then_inc(result_ready, 1)

                    stages = dict(start=start, project8=project8, norm8=norm8, rope8=rope8, split8=split8, length=length, mask=mask,
                                  prep64=prep64, heads=heads, turn_maxima=turn_maxima, maxima=maxima,
                                  values=values, finish8=finish8, ffn=ffn,
                                  finish64=lambda a, j: add_unit(j, "y", a, j),
                                  outproj=lambda a, j: add_unit(j, "y", a, j),
                                  norm_l0a=norm_l0a, norm_l0b=norm_l0b, norm_l0c=norm_l0c, norm_x3=norm_x3, norm_cn=norm_cn, norm_l1=norm_l1,
                                  rms_a=lambda j: rms_("x5", j), rms_b=lambda j: rms_("x6", j), rms_c=lambda j: rms_("x7", j),
                                  copy_l3=copy_l3, bias_l3=bias_l3, store=store)
                    for kind, *args in STEPS:
                        if kind in stages:
                            stages[kind](*args)

                @block.gpsimd
                def _(pool):
                    asked = [0]

                    def inverse_root(view):
                        asked[0] += 1
                        pool.wait_ge(root_asked, asked[0])
                        pool.tensor_tensor(view, view, consts[:, 52:53].broadcast_to(list(view.shape)), ALU.pow)\
                            .then_inc(root_done, 1)

                    norms = dict(norm_l0a=1, norm_l0b=1, norm_l0c=1, norm_x3=1, norm_cn=1, norm_l1=1, rms_a=1, rms_b=1, rms_c=1)
                    for kind, *args in STEPS:
                        if kind in norms:
                            for _ in range(norms[kind]):
                                inverse_root(small[:, args[-1], 2:4])

                @block.sync
                def _(sp):
                    def rows_of(t):
                        return t.rearrange("(i j) (s p) d -> i p (j s) d", j=PAIR, p=P)[bass.ds(it, 1)].rearrange("o p a d -> (o p) a d")
                    for k, src in (("x", w["x"]), ("cx", w["ctx"])):
                        sp.dma_start(nat[k][:, :, :, :].rearrange("p j s d -> p (j s) d"), rows_of(src)).then_inc(tokens_in, 16)
                    sp.wait_ge(result_ready, PAIR)
                    sp.dma_start(rows_of(out), nat["y"][:, :, :, :].rearrange("p j s d -> p (j s) d")).then_inc(stored, 16)
                    sp.wait_ge(stored, 16)

            names = [s for s in list(sems.values())[loop_first:]]
            nums = sorted(s.num for s in names)
            assert nums == list(range(nums[0], nums[-1] + 1))
            nc.gpsimd.sem_clear(range(nums[0], nums[-1] + 1))
            nc.all_engine_barrier()


def _tables():
    p, f = np.arange(P), np.float32
    ident = np.eye(P, dtype=f)
    causal = np.where(p[None, :] > p[:, None], f(NEG), f(0)).astype(f)
    inv = (1.0 / f(10000.0) ** (np.arange(0, DH, 2, dtype=f) / f(DH))).astype(f)
    ang = np.arange(S, dtype=f)[:, None] * inv[None, :]
    ang = np.concatenate([ang] * 4, axis=1).T
    consts = np.zeros((P, 128), f)
    for i in range(GH):
        consts[BLK * i:BLK * i + 3 * DS, i] = 1.0
        consts[BLK * i + COL_LEN, 4] = NEG
    consts[:, 8 + COL_LEN - 24] = 1.0
    consts[:, 16 + COL_MAX - 24] = 1.0
    consts[:, 24] = 1.0
    consts[:, 48:52] = 1.0 / f(10000.0) ** (np.arange(0, DS, 2, dtype=f) / f(DS))
    consts[:, 52] = -0.5
    sel = np.zeros((P, GH, P), f)
    for i in range(GH):
        sel[i, i, :] = 1.0
    return {"ident": ident, "causal": causal, "causal_t": np.ascontiguousarray(causal.T), "iota": np.arange(S, dtype=f),
            "rope_cos": np.cos(ang.astype(np.float64)).astype(f), "rope_sin": np.sin(ang.astype(np.float64)).astype(f),
            "consts": consts, "sel": sel.reshape(P, GH * P)}


def kernel(**inputs):
    import concourse.bacc as bacc
    from concourse.bass_utils import run_bass_kernel_spmd

    nc = bacc.Bacc("TRN2", target_bir_lowering=False, num_devices=1)
    arrays = {}

    def dram(name, a):
        a = np.ascontiguousarray(a)
        arrays[name] = a
        return nc.dram_tensor(name, a.shape, mybir.dt.from_np(a.dtype), kind="ExternalInput").ap()

    i = {k: np.asarray(v) for k, v in inputs.items()}
    w = {"x": dram("x_in", i["x"]), "ctx": dram("ctx_in", i["ctx_1024"]), "pos": dram("pos_in", i["pos_BxS2"].reshape(B * ST, P).T)}
    for k, v in _tables().items():
        w[k] = dram(f"table_{k}", v)

    def heads_in(name):
        return dram(name, i[name].transpose(1, 0, 2).reshape(D, D))

    def plain(name):
        return dram(name, i[name])

    def tiled(name):
        return plain(name).rearrange("(t p) n -> p t n", p=P)

    w["matrices"] = (
        [(f"L0_{c}:{128 * n}:128", heads_in(f"L0_xattn_W{x}{c}")) for c in (1, 2) for n, x in enumerate("qkv")]
        + [("fc1:0:128", dram("fc1_wT", i["L0_xattn_fc1_w"].T)), ("fc2:0:128", dram("fc2_wT", i["L0_xattn_fc2_w"].T)),
           ("fused:0:2176", plain("L1_xattn_w_fused")), ("attn_out:0:1024", tiled("L1_xattn_w_attn_out")),
           ("ff_out:0:512", tiled("L1_xattn_w_ff_out")), ("wq:0:1024", plain("L1_xattn_w_q")),
           ("wkv:0:128", plain("L1_xattn_w_kv")), ("w_out:0:1024", tiled("L1_xattn_w_out")),
           ("w_ff1:0:1024", plain("L1_xattn_w_ff1")), ("w_ff2:0:512", tiled("L1_xattn_w_ff2")),
           ("ca:0:128", plain("L2_xattn_ca_Wq")), ("ca:128:256", plain("L2_xattn_ca_Wkv")), ("ca_o:0:128", plain("L2_xattn_ca_Wo")),
           ("sa:0:128", plain("L2_xattn_sa_Wq")), ("sa:128:256", plain("L2_xattn_sa_Wkv")), ("sa_o:0:128", plain("L2_xattn_sa_Wo")),
           ("g_w1:0:512", plain("L2_xattn_W1")), ("g_w3:0:512", plain("L2_xattn_W3")), ("g_w2:0:512", tiled("L2_xattn_W2")),
           ("q3:0:1024", plain("L3_xattn_Wq")), ("k3:0:1024", plain("L3_xattn_Wk")), ("v3:0:1024", plain("L3_xattn_Wv")),
           ("o3:0:1024", tiled("L3_xattn_Wo")), ("w1_3:0:512", plain("L3_xattn_W1")), ("w2_3:0:512", tiled("L3_xattn_W2"))])
    for k in ("ln1_g", "ln1_b", "ln2_g", "ln2_b", "ln3_g", "ln3_b", "fc1_b", "fc2_b"):
        w[k] = plain(f"L0_xattn_{k}")
    for k in ("gamma_pt", "gamma_ca", "gamma_ctx"):
        w[k] = plain(f"L1_xattn_{k}")
    for k in ("ca_qn", "ca_kn", "sa_qn", "sa_kn", "pre_ca_w", "pre_sa_w", "pre_ffn_w"):
        w[k] = plain(f"L2_xattn_{k}")
    for k in ("bo", "b2"):
        w[k] = plain(f"L3_xattn_{k}")
    w["b1"] = dram("b1_columns", i["L3_xattn_b1"].reshape(NF, P).T)

    out = nc.dram_tensor("out", (B, S, D), F32, kind="ExternalOutput").ap()
    build_program(nc, w, out)
    r = run_bass_kernel_spmd(nc, [arrays], core_ids=[0])
    return r.results[0]["out"]
```
